# Optimizing a Trainium2 kernel written in Bass

```python
import numpy as np
import jax
import jax.numpy as jnp

def _softmax(x, axis=-1):
    return jax.nn.softmax(x, axis=axis)

def _gelu(x):
    return jax.nn.gelu(x, approximate=True)

def _silu(x):
    return jax.nn.silu(x)

def _sigmoid(x):
    return jax.nn.sigmoid(x)

def _layernorm(x, axis=-1, eps=1e-05):
    m = jnp.mean(x, axis=axis, keepdims=True)
    v = jnp.var(x, axis=axis, keepdims=True)
    return (x - m) / jnp.sqrt(v + eps)

def _scatter_add(tgt, idx, src, axis=0):
    return tgt.at[idx].add(src)

def _segment_sum(src, seg, n):
    return jax.ops.segment_sum(src, seg, n)
kernel_name = 'mk_pixart_seq_d4_seqx_r4_1579e8'

def setup_inputs(seed: int=0):
    np.random.seed(seed)
    _w = jnp.asarray

    def _rec_inputs():
        import jax
        import jax.numpy as jnp
        _rk = jax.random.key(seed)
        x = 7.22e-05 + 1 * jax.random.normal(jax.random.fold_in(_rk, 1), (2, 1024, 256), jnp.float32)
        _lenS = 1024 - jax.random.randint(jax.random.fold_in(_rk, 7), (2,), 0, max(1, 1024 // 4) + 1, jnp.int32)
        _lenS2 = 77 - jax.random.randint(jax.random.fold_in(_rk, 8), (2,), 0, max(1, 77 // 4) + 1, jnp.int32)
        cond_1024 = 0.000887014 + 1.03683 * jax.random.normal(jax.random.fold_in(_rk, 11), (2, 256), jnp.float32)
        _ctx_1024P = jax.random.normal(jax.random.fold_in(_rk, 12), (2, 16, 256), jnp.float32)
        _ctx_1024c = jax.random.dirichlet(jax.random.fold_in(_rk, 512), 0.3 * jnp.ones((16,), jnp.float32), (2, 77))
        _ctx_1024t = jnp.einsum('bsk,bkd->bsd', _ctx_1024c, _ctx_1024P)
        _ctx_1024t = _ctx_1024t * jax.lax.rsqrt(jnp.mean(jnp.square(_ctx_1024t)) + 1e-12) * 0.953939
        ctx_1024 = 0.00086875 + 0.999764 * (_ctx_1024t + 0.3 * jax.random.normal(jax.random.fold_in(_rk, 612), (2, 77, 256), jnp.float32))
        _validS = jnp.arange(1024)[None, :] < _lenS[:, None]
        _validS2 = jnp.arange(77)[None, :] < _lenS2[:, None]
        _causal = jnp.tril(jnp.ones((1024, 1024), dtype=bool))
        mask_BxS2_bf1 = jnp.ones((2, 77), dtype=bool)
        mask_SxS_bk0 = jnp.logical_not(jnp.broadcast_to(_validS[0:1, :], (1024, 1024)))
        return (x, cond_1024, ctx_1024, mask_BxS2_bf1, mask_SxS_bk0)
    x, cond_1024, ctx_1024, mask_BxS2_bf1, mask_SxS_bk0 = _rec_inputs()

    def _L0_xcond_setup():
        import jax, jax.numpy as jnp
        import numpy as np
        C = 256
        H = 16
        D = C // H
        WIN = 128
        SHIFT = 64
        TOPK = 16
        HID = 1024
        EPS = 1e-06

        def _ln(x):
            x32 = x.astype(jnp.float32)
            m = x32.mean(-1, keepdims=True)
            v = jnp.mean((x32 - m) ** 2, axis=-1, keepdims=True)
            return ((x32 - m) * jax.lax.rsqrt(v + EPS)).astype(x.dtype)

        def _self_attn(h, w_qkv, b_qkv, w_so, b_so):
            B, L, _ = h.shape
            qkv = h @ w_qkv + b_qkv
            qkv = jnp.roll(qkv, -SHIFT, axis=1)
            nw = L // WIN
            qkv = qkv.reshape(B, nw, WIN, 3, H, D)
            q, k, v = (qkv[:, :, :, 0], qkv[:, :, :, 1], qkv[:, :, :, 2])
            scores = jnp.einsum('bnqhd,bnkhd->bnhqk', q, k) / jnp.sqrt(jnp.float32(D)).astype(h.dtype)
            attn = jax.nn.softmax(scores, axis=-1)
            o = jnp.einsum('bnhqk,bnkhd->bnqhd', attn, v).reshape(B, L, C)
            o = jnp.roll(o, SHIFT, axis=1)
            return o @ w_so + b_so

        def _topk_cross_attn(h, ctx, w_q, b_q, w_kv, b_kv, w_co, b_co):
            B, L, _ = h.shape
            Lc = ctx.shape[1]
            q = (h @ w_q + b_q).reshape(B, L, H, D)
            kv = (ctx @ w_kv + b_kv).reshape(B, Lc, 2, H, D)
            k, v = (kv[:, :, 0], kv[:, :, 1])
            scores = jnp.einsum('bqhd,bkhd->bhqk', q, k) / jnp.sqrt(jnp.float32(D)).astype(h.dtype)
            top_s, top_i = jax.lax.top_k(scores, TOPK)
            attn = jax.nn.softmax(top_s, axis=-1)
            v_bh = jnp.transpose(v, (0, 2, 1, 3))
            vg = jnp.take_along_axis(v_bh[:, :, None, :, :], top_i[..., None], axis=3)
            o = jnp.einsum('bhqk,bhqkd->bqhd', attn, vg).reshape(B, L, C)
            return o @ w_co + b_co

        def _swiglu(h, w_m1, b_m1, w_m2, b_m2):
            u = h @ w_m1 + b_m1
            a, b = (u[..., :HID], u[..., HID:])
            return jax.nn.silu(a) * b @ w_m2 + b_m2
        key = jax.random.key(seed)
        ks = jax.random.split(key, 24)
        s = 0.02
        inp = {'x': jax.random.normal(ks[0], (2, 1024, C), jnp.float32), 'mod': jax.random.normal(ks[1], (2, C), jnp.float32), 'context': jax.random.normal(ks[2], (2, 256, C), jnp.float32), 'w_ada': jax.random.normal(ks[3], (C, 9 * C), jnp.float32) * s, 'b_ada': jnp.zeros((9 * C,), jnp.float32), 'w_qkv': jax.random.normal(ks[4], (C, 3 * C), jnp.float32) * s, 'b_qkv': jnp.zeros((3 * C,), jnp.float32), 'w_so': jax.random.normal(ks[5], (C, C), jnp.float32) * s, 'b_so': jnp.zeros((C,), jnp.float32), 'w_q': jax.random.normal(ks[6], (C, C), jnp.float32) * s, 'b_q': jnp.zeros((C,), jnp.float32), 'w_kv': jax.random.normal(ks[7], (C, 2 * C), jnp.float32) * s, 'b_kv': jnp.zeros((2 * C,), jnp.float32), 'w_co': jax.random.normal(ks[8], (C, C), jnp.float32) * s, 'b_co': jnp.zeros((C,), jnp.float32), 'w_m1': jax.random.normal(ks[9], (C, 2 * HID), jnp.float32) * s, 'b_m1': jnp.zeros((2 * HID,), jnp.float32), 'w_m2': jax.random.normal(ks[10], (HID, C), jnp.float32) * s, 'b_m2': jnp.zeros((C,), jnp.float32)}
        return inp
    _L0_xcond_all = _L0_xcond_setup()
    _L0_xcond_in = {k: v for k, v in _L0_xcond_all.items() if k in ('w_ada', 'b_ada', 'w_qkv', 'b_qkv', 'w_so', 'b_so', 'w_q', 'b_q', 'w_kv', 'b_kv', 'w_co', 'b_co', 'w_m1', 'b_m1', 'w_m2', 'b_m2')}
    del _L0_xcond_all

    def _L1_xcond_setup():
        import jax, jax.numpy as jnp
        import numpy as np
        H = 256
        RH = 2 * H
        E = 3
        B, T, P = (8, 512, 64)
        LN_EPS = 1e-05

        def _layer_norm(x, gamma, beta):
            mu = jnp.mean(x, axis=-1, keepdims=True)
            var = jnp.mean(jnp.square(x - mu), axis=-1, keepdims=True)
            return (x - mu) * jax.lax.rsqrt(var + LN_EPS) * gamma + beta
        key = jax.random.key(seed)
        ks = jax.random.split(key, 24)
        s = lambda fan_in: 1.0 / np.sqrt(fan_in)
        inp = {'mix_hidden_states': jax.random.normal(ks[0], (B, T, H), jnp.float32), 'global_anchor': jax.random.normal(ks[1], (B, H), jnp.float32), 'prototype_bank': jax.random.normal(ks[2], (B, P, H), jnp.float32), 'ln_gamma': jnp.ones((H,), jnp.float32), 'ln_beta': jnp.zeros((H,), jnp.float32), 'Wq': jax.random.normal(ks[3], (H, H), jnp.float32) * s(H), 'Wk': jax.random.normal(ks[4], (H, H), jnp.float32) * s(H), 'Wv': jax.random.normal(ks[5], (H, H), jnp.float32) * s(H), 'router_W': jax.random.normal(ks[6], (3 * H, E), jnp.float32) * s(3 * H), 'router_b': jnp.zeros((E,), jnp.float32), 'e_w1': jax.random.normal(ks[7], (E, 3 * H, RH), jnp.float32) * s(3 * H), 'e_b1': jnp.zeros((E, RH), jnp.float32), 'e_w2': jax.random.normal(ks[8], (E, RH, H), jnp.float32) * s(RH), 'e_b2': jnp.zeros((E, H), jnp.float32), 'gate_w1': jax.random.normal(ks[9], (3 * H, H), jnp.float32) * s(3 * H), 'gate_b1': jnp.zeros((H,), jnp.float32), 'gate_w2': jax.random.normal(ks[10], (H, H), jnp.float32) * s(H), 'gate_b2': jnp.zeros((H,), jnp.float32), 'out_w': jax.random.normal(ks[11], (H, H), jnp.float32) * s(H), 'out_b': jnp.zeros((H,), jnp.float32)}
        return inp
    _L1_xcond_all = _L1_xcond_setup()
    _L1_xcond_in = {k: v for k, v in _L1_xcond_all.items() if k in ('ln_gamma', 'ln_beta', 'Wq', 'Wk', 'Wv', 'router_W', 'router_b', 'e_w1', 'e_b1', 'e_w2', 'e_b2', 'gate_w1', 'gate_b1', 'gate_w2', 'gate_b2', 'out_w', 'out_b')}
    del _L1_xcond_all

    def _L2_xcond_setup():
        import jax, jax.numpy as jnp
        import numpy as np
        B, N, D, H, LC = (2, 256, 256, 16, 77)
        HD = D // H
        BLOCK = 16
        ROPE_BASE = 10000.0
        EPS = 1e-05

        def _block_diff_mask(n, block_size):
            idx = np.arange(2 * n)
            q = idx[:, None]
            kv = idx[None, :]
            fq = q >= n
            fkv = kv >= n
            bq = np.where(fq, (q - n) // block_size, q // block_size)
            bkv = np.where(fkv, (kv - n) // block_size, kv // block_size)
            block_diagonal = (bq == bkv) & (fq == fkv)
            offset_block_causal = (bq > bkv) & fkv & ~fq
            block_causal = (bq >= bkv) & fq & fkv
            return jnp.asarray(block_diagonal | offset_block_causal | block_causal)

        def _rope_tables(n):
            inv_freq = 1.0 / ROPE_BASE ** (np.arange(0, HD, 2, dtype=np.float32) / HD)
            freqs = np.outer(np.arange(n, dtype=np.float32), inv_freq)
            emb = np.concatenate([freqs, freqs], axis=-1)
            cos = jnp.asarray(np.cos(emb), jnp.float32)[None, :, None, :]
            sin = jnp.asarray(np.sin(emb), jnp.float32)[None, :, None, :]
            return (cos, sin)

        def _ln(x, w):
            xf = x.astype(jnp.float32)
            mu = jnp.mean(xf, axis=-1, keepdims=True)
            var = jnp.mean(jnp.square(xf - mu), axis=-1, keepdims=True)
            y = (xf - mu) * jax.lax.rsqrt(var + EPS)
            return y * w[None, None, :]

        def _apply_rope(t, cos, sin):
            t1, t2 = jnp.split(t, 2, axis=-1)
            rot = jnp.concatenate([-t2, t1], axis=-1)
            return t * cos + rot * sin

        def _attn(q, k, v, mask):
            scale = 1.0 / np.sqrt(HD)
            s = jnp.einsum('bqhd,bkhd->bhqk', q, k) * scale
            s = jnp.where(mask, s, jnp.finfo(s.dtype).min)
            a = jax.nn.softmax(s, axis=-1)
            return jnp.einsum('bhqk,bkhd->bqhd', a, v)
        key = jax.random.key(seed)
        ks = jax.random.split(key, 16)
        w = lambda k, shp: jax.random.normal(k, shp, jnp.float32) * 0.02
        inp = {'x': jax.random.normal(ks[0], (B, 2 * N, D), jnp.float32), 'cond_global': jax.random.normal(ks[1], (B, D), jnp.float32), 'cond_tokens': jax.random.normal(ks[2], (B, LC, D), jnp.float32), 'adaLN_W': w(ks[3], (D, 9 * D)), 'adaLN_b': w(ks[4], (9 * D,)), 'norm1_w': jnp.ones((D,), jnp.float32), 'qkv_W': w(ks[5], (D, 3 * D)), 'attn_out_W': w(ks[6], (D, D)), 'normc_w': jnp.ones((D,), jnp.float32), 'cq_W': w(ks[7], (D, D)), 'ck_W': w(ks[8], (D, D)), 'cv_W': w(ks[9], (D, D)), 'co_W': w(ks[10], (D, D)), 'norm2_w': jnp.ones((D,), jnp.float32), 'mlp_W1': w(ks[11], (D, 4 * D)), 'mlp_b1': w(ks[12], (4 * D,)), 'mlp_W2': w(ks[13], (4 * D, D)), 'mlp_b2': w(ks[14], (D,)), 'cond_kv_mask': jnp.ones((B, LC), bool), 'attn_mask': _block_diff_mask(N, BLOCK)}
        return inp
    _L2_xcond_all = _L2_xcond_setup()
    _L2_xcond_in = {k: v for k, v in _L2_xcond_all.items() if k in ('adaLN_W', 'adaLN_b', 'norm1_w', 'qkv_W', 'attn_out_W', 'normc_w', 'cq_W', 'ck_W', 'cv_W', 'co_W', 'norm2_w', 'mlp_W1', 'mlp_b1', 'mlp_W2', 'mlp_b2')}
    del _L2_xcond_all

    def _L3_xcond_setup():
        import jax, jax.numpy as jnp
        import numpy as np
        LN_EPS = 1e-06

        def _ln(x):
            mu = jnp.mean(x, axis=-1, keepdims=True)
            var = jnp.var(x, axis=-1, keepdims=True)
            return (x - mu) * jax.lax.rsqrt(var + LN_EPS)
        key = jax.random.key(seed)
        H, NH = (256, 16)
        B, N, S = (4, 256, 77)
        MLP = int(H * 4.0)
        ks = jax.random.split(key, 20)
        s = 1.0 / np.sqrt(H)
        return {'x': jax.random.normal(ks[0], (B, N, H), jnp.float32), 'c': jax.random.normal(ks[1], (B, H), jnp.float32), 'context': jax.random.normal(ks[2], (B, S, H), jnp.float32), 'W_mod': jax.random.normal(ks[3], (H, 6 * H), jnp.float32) * s, 'b_mod': jnp.zeros((6 * H,), jnp.float32), 'W_qkv': jax.random.normal(ks[4], (H, 3 * H), jnp.float32) * s, 'b_qkv': jnp.zeros((3 * H,), jnp.float32), 'W_proj': jax.random.normal(ks[5], (H, H), jnp.float32) * s, 'b_proj': jnp.zeros((H,), jnp.float32), 'W_qc': jax.random.normal(ks[6], (H, H), jnp.float32) * s, 'b_qc': jnp.zeros((H,), jnp.float32), 'W_kvc': jax.random.normal(ks[7], (H, 2 * H), jnp.float32) * s, 'b_kvc': jnp.zeros((2 * H,), jnp.float32), 'W_cproj': jax.random.normal(ks[8], (H, H), jnp.float32) * s, 'b_cproj': jnp.zeros((H,), jnp.float32), 'W_mlp1': jax.random.normal(ks[9], (H, MLP), jnp.float32) * s, 'b_mlp1': jnp.zeros((MLP,), jnp.float32), 'W_mlp2': jax.random.normal(ks[10], (MLP, H), jnp.float32) * (1.0 / np.sqrt(MLP)), 'b_mlp2': jnp.zeros((H,), jnp.float32)}
    _L3_xcond_all = _L3_xcond_setup()
    _L3_xcond_in = {k: v for k, v in _L3_xcond_all.items() if k in ('W_mod', 'b_mod', 'W_qkv', 'b_qkv', 'W_proj', 'b_proj', 'W_qc', 'b_qc', 'W_kvc', 'b_kvc', 'W_cproj', 'b_cproj', 'W_mlp1', 'b_mlp1', 'W_mlp2', 'b_mlp2')}
    del _L3_xcond_all
    return {'x': x, 'cond_1024': cond_1024, 'ctx_1024': ctx_1024, 'mask_BxS2_bf1': mask_BxS2_bf1, 'mask_SxS_bk0': mask_SxS_bk0, 'L0_xcond_w_ada': _L0_xcond_in['w_ada'], 'L0_xcond_b_ada': _L0_xcond_in['b_ada'], 'L0_xcond_w_qkv': _L0_xcond_in['w_qkv'], 'L0_xcond_b_qkv': _L0_xcond_in['b_qkv'], 'L0_xcond_w_so': _L0_xcond_in['w_so'], 'L0_xcond_b_so': _L0_xcond_in['b_so'], 'L0_xcond_w_q': _L0_xcond_in['w_q'], 'L0_xcond_b_q': _L0_xcond_in['b_q'], 'L0_xcond_w_kv': _L0_xcond_in['w_kv'], 'L0_xcond_b_kv': _L0_xcond_in['b_kv'], 'L0_xcond_w_co': _L0_xcond_in['w_co'], 'L0_xcond_b_co': _L0_xcond_in['b_co'], 'L0_xcond_w_m1': _L0_xcond_in['w_m1'], 'L0_xcond_b_m1': _L0_xcond_in['b_m1'], 'L0_xcond_w_m2': _L0_xcond_in['w_m2'], 'L0_xcond_b_m2': _L0_xcond_in['b_m2'], 'L1_xcond_ln_gamma': _L1_xcond_in['ln_gamma'], 'L1_xcond_ln_beta': _L1_xcond_in['ln_beta'], 'L1_xcond_Wq': _L1_xcond_in['Wq'], 'L1_xcond_Wk': _L1_xcond_in['Wk'], 'L1_xcond_Wv': _L1_xcond_in['Wv'], 'L1_xcond_router_W': _L1_xcond_in['router_W'], 'L1_xcond_router_b': _L1_xcond_in['router_b'], 'L1_xcond_e_w1': _L1_xcond_in['e_w1'], 'L1_xcond_e_b1': _L1_xcond_in['e_b1'], 'L1_xcond_e_w2': _L1_xcond_in['e_w2'], 'L1_xcond_e_b2': _L1_xcond_in['e_b2'], 'L1_xcond_gate_w1': _L1_xcond_in['gate_w1'], 'L1_xcond_gate_b1': _L1_xcond_in['gate_b1'], 'L1_xcond_gate_w2': _L1_xcond_in['gate_w2'], 'L1_xcond_gate_b2': _L1_xcond_in['gate_b2'], 'L1_xcond_out_w': _L1_xcond_in['out_w'], 'L1_xcond_out_b': _L1_xcond_in['out_b'], 'L2_xcond_adaLN_W': _L2_xcond_in['adaLN_W'], 'L2_xcond_adaLN_b': _L2_xcond_in['adaLN_b'], 'L2_xcond_norm1_w': _L2_xcond_in['norm1_w'], 'L2_xcond_qkv_W': _L2_xcond_in['qkv_W'], 'L2_xcond_attn_out_W': _L2_xcond_in['attn_out_W'], 'L2_xcond_normc_w': _L2_xcond_in['normc_w'], 'L2_xcond_cq_W': _L2_xcond_in['cq_W'], 'L2_xcond_ck_W': _L2_xcond_in['ck_W'], 'L2_xcond_cv_W': _L2_xcond_in['cv_W'], 'L2_xcond_co_W': _L2_xcond_in['co_W'], 'L2_xcond_norm2_w': _L2_xcond_in['norm2_w'], 'L2_xcond_mlp_W1': _L2_xcond_in['mlp_W1'], 'L2_xcond_mlp_b1': _L2_xcond_in['mlp_b1'], 'L2_xcond_mlp_W2': _L2_xcond_in['mlp_W2'], 'L2_xcond_mlp_b2': _L2_xcond_in['mlp_b2'], 'L3_xcond_W_mod': _L3_xcond_in['W_mod'], 'L3_xcond_b_mod': _L3_xcond_in['b_mod'], 'L3_xcond_W_qkv': _L3_xcond_in['W_qkv'], 'L3_xcond_b_qkv': _L3_xcond_in['b_qkv'], 'L3_xcond_W_proj': _L3_xcond_in['W_proj'], 'L3_xcond_b_proj': _L3_xcond_in['b_proj'], 'L3_xcond_W_qc': _L3_xcond_in['W_qc'], 'L3_xcond_b_qc': _L3_xcond_in['b_qc'], 'L3_xcond_W_kvc': _L3_xcond_in['W_kvc'], 'L3_xcond_b_kvc': _L3_xcond_in['b_kvc'], 'L3_xcond_W_cproj': _L3_xcond_in['W_cproj'], 'L3_xcond_b_cproj': _L3_xcond_in['b_cproj'], 'L3_xcond_W_mlp1': _L3_xcond_in['W_mlp1'], 'L3_xcond_b_mlp1': _L3_xcond_in['b_mlp1'], 'L3_xcond_W_mlp2': _L3_xcond_in['W_mlp2'], 'L3_xcond_b_mlp2': _L3_xcond_in['b_mlp2']}

def reference(x, cond_1024, ctx_1024, mask_BxS2_bf1, mask_SxS_bk0, L0_xcond_w_ada, L0_xcond_b_ada, L0_xcond_w_qkv, L0_xcond_b_qkv, L0_xcond_w_so, L0_xcond_b_so, L0_xcond_w_q, L0_xcond_b_q, L0_xcond_w_kv, L0_xcond_b_kv, L0_xcond_w_co, L0_xcond_b_co, L0_xcond_w_m1, L0_xcond_b_m1, L0_xcond_w_m2, L0_xcond_b_m2, L1_xcond_ln_gamma, L1_xcond_ln_beta, L1_xcond_Wq, L1_xcond_Wk, L1_xcond_Wv, L1_xcond_router_W, L1_xcond_router_b, L1_xcond_e_w1, L1_xcond_e_b1, L1_xcond_e_w2, L1_xcond_e_b2, L1_xcond_gate_w1, L1_xcond_gate_b1, L1_xcond_gate_w2, L1_xcond_gate_b2, L1_xcond_out_w, L1_xcond_out_b, L2_xcond_adaLN_W, L2_xcond_adaLN_b, L2_xcond_norm1_w, L2_xcond_qkv_W, L2_xcond_attn_out_W, L2_xcond_normc_w, L2_xcond_cq_W, L2_xcond_ck_W, L2_xcond_cv_W, L2_xcond_co_W, L2_xcond_norm2_w, L2_xcond_mlp_W1, L2_xcond_mlp_b1, L2_xcond_mlp_W2, L2_xcond_mlp_b2, L3_xcond_W_mod, L3_xcond_b_mod, L3_xcond_W_qkv, L3_xcond_b_qkv, L3_xcond_W_proj, L3_xcond_b_proj, L3_xcond_W_qc, L3_xcond_b_qc, L3_xcond_W_kvc, L3_xcond_b_kvc, L3_xcond_W_cproj, L3_xcond_b_cproj, L3_xcond_W_mlp1, L3_xcond_b_mlp1, L3_xcond_W_mlp2, L3_xcond_b_mlp2):
    import jax
    import jax.numpy as jnp

    def _L0_xcond_ref(x, mod, context, w_ada, b_ada, w_qkv, b_qkv, w_so, b_so, w_q, b_q, w_kv, b_kv, w_co, b_co, w_m1, b_m1, w_m2, b_m2):
        import jax, jax.numpy as jnp
        import numpy as np
        C = 256
        H = 16
        D = C // H
        WIN = 128
        SHIFT = 64
        TOPK = 16
        HID = 1024
        EPS = 1e-06

        def _ln(x):
            x32 = x.astype(jnp.float32)
            m = x32.mean(-1, keepdims=True)
            v = jnp.mean((x32 - m) ** 2, axis=-1, keepdims=True)
            return ((x32 - m) * jax.lax.rsqrt(v + EPS)).astype(x.dtype)

        def _self_attn(h, w_qkv, b_qkv, w_so, b_so):
            B, L, _ = h.shape
            qkv = h @ w_qkv + b_qkv
            qkv = jnp.roll(qkv, -SHIFT, axis=1)
            nw = L // WIN
            qkv = qkv.reshape(B, nw, WIN, 3, H, D)
            q, k, v = (qkv[:, :, :, 0], qkv[:, :, :, 1], qkv[:, :, :, 2])
            scores = jnp.einsum('bnqhd,bnkhd->bnhqk', q, k) / jnp.sqrt(jnp.float32(D)).astype(h.dtype)
            attn = jax.nn.softmax(scores, axis=-1)
            o = jnp.einsum('bnhqk,bnkhd->bnqhd', attn, v).reshape(B, L, C)
            o = jnp.roll(o, SHIFT, axis=1)
            return o @ w_so + b_so

        def _topk_cross_attn(h, ctx, w_q, b_q, w_kv, b_kv, w_co, b_co):
            B, L, _ = h.shape
            Lc = ctx.shape[1]
            q = (h @ w_q + b_q).reshape(B, L, H, D)
            kv = (ctx @ w_kv + b_kv).reshape(B, Lc, 2, H, D)
            k, v = (kv[:, :, 0], kv[:, :, 1])
            scores = jnp.einsum('bqhd,bkhd->bhqk', q, k) / jnp.sqrt(jnp.float32(D)).astype(h.dtype)
            top_s, top_i = jax.lax.top_k(scores, TOPK)
            attn = jax.nn.softmax(top_s, axis=-1)
            v_bh = jnp.transpose(v, (0, 2, 1, 3))
            vg = jnp.take_along_axis(v_bh[:, :, None, :, :], top_i[..., None], axis=3)
            o = jnp.einsum('bhqk,bhqkd->bqhd', attn, vg).reshape(B, L, C)
            return o @ w_co + b_co

        def _swiglu(h, w_m1, b_m1, w_m2, b_m2):
            u = h @ w_m1 + b_m1
            a, b = (u[..., :HID], u[..., HID:])
            return jax.nn.silu(a) * b @ w_m2 + b_m2
        m = jax.nn.silu(mod) @ w_ada + b_ada
        sh_msa, sc_msa, g_msa, sh_mca, sc_mca, g_mca, sh_mlp, sc_mlp, g_mlp = [m[:, i * C:(i + 1) * C][:, None, :] for i in range(9)]
        h = _ln(x) * (1 + sc_msa) + sh_msa
        h = _self_attn(h, w_qkv, b_qkv, w_so, b_so)
        x = x + h * g_msa
        h = _ln(x) * (1 + sc_mca) + sh_mca
        h = _topk_cross_attn(h, context, w_q, b_q, w_kv, b_kv, w_co, b_co)
        x = x + h * g_mca
        h = _ln(x) * (1 + sc_mlp) + sh_mlp
        h = _swiglu(h, w_m1, b_m1, w_m2, b_m2)
        x = x + h * g_mlp
        return x

    def _L1_xcond_ref(mix_hidden_states, global_anchor, prototype_bank, ln_gamma, ln_beta, Wq, Wk, Wv, router_W, router_b, e_w1, e_b1, e_w2, e_b2, gate_w1, gate_b1, gate_w2, gate_b2, out_w, out_b):
        import jax, jax.numpy as jnp
        import numpy as np
        H = 256
        RH = 2 * H
        E = 3
        B, T, P = (8, 512, 64)
        LN_EPS = 1e-05

        def _layer_norm(x, gamma, beta):
            mu = jnp.mean(x, axis=-1, keepdims=True)
            var = jnp.mean(jnp.square(x - mu), axis=-1, keepdims=True)
            return (x - mu) * jax.lax.rsqrt(var + LN_EPS) * gamma + beta
        x = mix_hidden_states
        nx = _layer_norm(x, ln_gamma, ln_beta)
        q = nx @ Wq
        k = prototype_bank @ Wk
        v = prototype_bank @ Wv
        scores = jnp.einsum('bth,bph->btp', q, k) * H ** (-0.5)
        weights = jax.nn.softmax(scores, axis=-1)
        evidence = jnp.einsum('btp,bph->bth', weights, v)
        anchor = jnp.broadcast_to(global_anchor[:, None, :], nx.shape)
        combined = jnp.concatenate([nx, evidence, anchor], axis=-1)
        router_logits = combined @ router_W + router_b
        router_probs = jax.nn.softmax(router_logits, axis=-1)
        h = jax.nn.silu(jnp.einsum('btc,ecr->bter', combined, e_w1) + e_b1)
        expert_out = jnp.einsum('bter,erh->bteh', h, e_w2) + e_b2
        routed = jnp.sum(expert_out * router_probs[..., None], axis=-2)
        g = jax.nn.sigmoid(jax.nn.silu(combined @ gate_w1 + gate_b1) @ gate_w2 + gate_b2)
        refined_delta = g * (routed @ out_w + out_b)
        return x + refined_delta

    def _L2_xcond_ref(x, cond_global, cond_tokens, adaLN_W, adaLN_b, norm1_w, qkv_W, attn_out_W, normc_w, cq_W, ck_W, cv_W, co_W, norm2_w, mlp_W1, mlp_b1, mlp_W2, mlp_b2, cond_kv_mask, attn_mask):
        import jax, jax.numpy as jnp
        import numpy as np
        B, N, D, H, LC = (2, 256, 256, 16, 77)
        HD = D // H
        BLOCK = 16
        ROPE_BASE = 10000.0
        EPS = 1e-05

        def _block_diff_mask(n, block_size):
            idx = np.arange(2 * n)
            q = idx[:, None]
            kv = idx[None, :]
            fq = q >= n
            fkv = kv >= n
            bq = np.where(fq, (q - n) // block_size, q // block_size)
            bkv = np.where(fkv, (kv - n) // block_size, kv // block_size)
            block_diagonal = (bq == bkv) & (fq == fkv)
            offset_block_causal = (bq > bkv) & fkv & ~fq
            block_causal = (bq >= bkv) & fq & fkv
            return jnp.asarray(block_diagonal | offset_block_causal | block_causal)

        def _rope_tables(n):
            inv_freq = 1.0 / ROPE_BASE ** (np.arange(0, HD, 2, dtype=np.float32) / HD)
            freqs = np.outer(np.arange(n, dtype=np.float32), inv_freq)
            emb = np.concatenate([freqs, freqs], axis=-1)
            cos = jnp.asarray(np.cos(emb), jnp.float32)[None, :, None, :]
            sin = jnp.asarray(np.sin(emb), jnp.float32)[None, :, None, :]
            return (cos, sin)

        def _ln(x, w):
            xf = x.astype(jnp.float32)
            mu = jnp.mean(xf, axis=-1, keepdims=True)
            var = jnp.mean(jnp.square(xf - mu), axis=-1, keepdims=True)
            y = (xf - mu) * jax.lax.rsqrt(var + EPS)
            return y * w[None, None, :]

        def _apply_rope(t, cos, sin):
            t1, t2 = jnp.split(t, 2, axis=-1)
            rot = jnp.concatenate([-t2, t1], axis=-1)
            return t * cos + rot * sin

        def _attn(q, k, v, mask):
            scale = 1.0 / np.sqrt(HD)
            s = jnp.einsum('bqhd,bkhd->bhqk', q, k) * scale
            s = jnp.where(mask, s, jnp.finfo(s.dtype).min)
            a = jax.nn.softmax(s, axis=-1)
            return jnp.einsum('bhqk,bkhd->bqhd', a, v)
        b, s, d = x.shape
        n = s // 2
        mod = (cond_global @ adaLN_W + adaLN_b)[:, None, :]
        sh_msa, sc_msa, g_msa, sh_x, sc_x, g_x, sh_mlp, sc_mlp, g_mlp = jnp.split(mod, 9, axis=-1)
        x_norm = _ln(x, norm1_w) * (1 + sc_msa) + sh_msa
        cos, sin = _rope_tables(n)

        def qkv(h):
            t = (h @ qkv_W).reshape(b, n, 3, H, HD)
            q, k, v = (t[:, :, 0], t[:, :, 1], t[:, :, 2])
            return (_apply_rope(q, cos, sin), _apply_rope(k, cos, sin), v)
        q1, k1, v1 = qkv(x_norm[:, :n])
        q2, k2, v2 = qkv(x_norm[:, n:])
        q = jnp.concatenate([q1, q2], axis=1)
        k = jnp.concatenate([k1, k2], axis=1)
        v = jnp.concatenate([v1, v2], axis=1)
        self_out = _attn(q, k, v, attn_mask[None, None]).reshape(b, s, d) @ attn_out_W
        x = x + g_msa * self_out
        xc = _ln(x, normc_w) * (1 + sc_x) + sh_x
        qc = (xc @ cq_W).reshape(b, s, H, HD)
        kc = (cond_tokens @ ck_W).reshape(b, LC, H, HD)
        vc = (cond_tokens @ cv_W).reshape(b, LC, H, HD)
        cross = _attn(qc, kc, vc, cond_kv_mask[:, None, None, :]).reshape(b, s, d) @ co_W
        x = x + g_x * cross
        xm = _ln(x, norm2_w) * (1 + sc_mlp) + sh_mlp
        h = jax.nn.gelu(xm @ mlp_W1 + mlp_b1, approximate=True)
        mlp_out = h @ mlp_W2 + mlp_b2
        return x + g_mlp * mlp_out

    def _L3_xcond_ref(x, c, context, W_mod, b_mod, W_qkv, b_qkv, W_proj, b_proj, W_qc, b_qc, W_kvc, b_kvc, W_cproj, b_cproj, W_mlp1, b_mlp1, W_mlp2, b_mlp2):
        import jax, jax.numpy as jnp
        import numpy as np
        LN_EPS = 1e-06

        def _ln(x):
            mu = jnp.mean(x, axis=-1, keepdims=True)
            var = jnp.var(x, axis=-1, keepdims=True)
            return (x - mu) * jax.lax.rsqrt(var + LN_EPS)
        B, N, H = x.shape
        NH = 16
        hd = H // NH
        scale = hd ** (-0.5)
        c_proj = jax.nn.silu(c) @ W_mod + b_mod
        shift_a, scale_a, gate_a, shift_m, scale_m, gate_m = jnp.split(c_proj, 6, axis=-1)

        def modulate(t, shift, sc):
            return t * (1 + sc[:, None]) + shift[:, None]
        x_norm = modulate(_ln(x), shift_a, scale_a)
        qkv = x_norm @ W_qkv + b_qkv
        q, k, v = jnp.split(qkv, 3, axis=-1)
        q = q.reshape(B, N, NH, hd).transpose(0, 2, 1, 3)
        k = k.reshape(B, N, NH, hd).transpose(0, 2, 1, 3)
        v = v.reshape(B, N, NH, hd).transpose(0, 2, 1, 3)
        attn_w = jax.nn.softmax(jnp.einsum('bhqd,bhkd->bhqk', q, k) * scale, axis=-1)
        attn_out = jnp.einsum('bhqk,bhkd->bhqd', attn_w, v)
        attn_out = attn_out.transpose(0, 2, 1, 3).reshape(B, N, H)
        attn_out = attn_out @ W_proj + b_proj
        x = x + gate_a[:, None] * attn_out
        S = context.shape[1]
        q_c = _ln(x) @ W_qc + b_qc
        kv_c = _ln(context) @ W_kvc + b_kvc
        k_c, v_c = jnp.split(kv_c, 2, axis=-1)
        q_c = q_c.reshape(B, N, NH, hd).transpose(0, 2, 1, 3)
        k_c = k_c.reshape(B, S, NH, hd).transpose(0, 2, 1, 3)
        v_c = v_c.reshape(B, S, NH, hd).transpose(0, 2, 1, 3)
        c_attn_w = jax.nn.softmax(jnp.einsum('bhqd,bhsd->bhqs', q_c, k_c) * scale, axis=-1)
        c_attn_out = jnp.einsum('bhqs,bhsd->bhqd', c_attn_w, v_c)
        c_attn_out = c_attn_out.transpose(0, 2, 1, 3).reshape(B, N, H)
        c_attn_out = c_attn_out @ W_cproj + b_cproj
        x = x + c_attn_out
        x_norm2 = modulate(_ln(x), shift_m, scale_m)
        h = jax.nn.gelu(x_norm2 @ W_mlp1 + b_mlp1)
        h = h @ W_mlp2 + b_mlp2
        x = x + gate_m[:, None] * h
        return x
    x = _L0_xcond_ref(x, cond_1024, ctx_1024, L0_xcond_w_ada, L0_xcond_b_ada, L0_xcond_w_qkv, L0_xcond_b_qkv, L0_xcond_w_so, L0_xcond_b_so, L0_xcond_w_q, L0_xcond_b_q, L0_xcond_w_kv, L0_xcond_b_kv, L0_xcond_w_co, L0_xcond_b_co, L0_xcond_w_m1, L0_xcond_b_m1, L0_xcond_w_m2, L0_xcond_b_m2)
    x = _L1_xcond_ref(x, cond_1024, ctx_1024, L1_xcond_ln_gamma, L1_xcond_ln_beta, L1_xcond_Wq, L1_xcond_Wk, L1_xcond_Wv, L1_xcond_router_W, L1_xcond_router_b, L1_xcond_e_w1, L1_xcond_e_b1, L1_xcond_e_w2, L1_xcond_e_b2, L1_xcond_gate_w1, L1_xcond_gate_b1, L1_xcond_gate_w2, L1_xcond_gate_b2, L1_xcond_out_w, L1_xcond_out_b)
    x = _L2_xcond_ref(x, cond_1024, ctx_1024, L2_xcond_adaLN_W, L2_xcond_adaLN_b, L2_xcond_norm1_w, L2_xcond_qkv_W, L2_xcond_attn_out_W, L2_xcond_normc_w, L2_xcond_cq_W, L2_xcond_ck_W, L2_xcond_cv_W, L2_xcond_co_W, L2_xcond_norm2_w, L2_xcond_mlp_W1, L2_xcond_mlp_b1, L2_xcond_mlp_W2, L2_xcond_mlp_b2, mask_BxS2_bf1, mask_SxS_bk0)
    x = _L3_xcond_ref(x, cond_1024, ctx_1024, L3_xcond_W_mod, L3_xcond_b_mod, L3_xcond_W_qkv, L3_xcond_b_qkv, L3_xcond_W_proj, L3_xcond_b_proj, L3_xcond_W_qc, L3_xcond_b_qc, L3_xcond_W_kvc, L3_xcond_b_kvc, L3_xcond_W_cproj, L3_xcond_b_cproj, L3_xcond_W_mlp1, L3_xcond_b_mlp1, L3_xcond_W_mlp2, L3_xcond_b_mlp2)
    return x

_drawn_inputs = setup_inputs


def setup_inputs(seed=0):
    import zlib

    import numpy as np

    out = dict(_drawn_inputs(seed))
    spreads = {'L0_xcond_b_ada': (0.0, 0.37),
     'L0_xcond_b_qkv': (0.0, 0.8),
     'L0_xcond_b_so': (0.0, 0.371),
     'L0_xcond_b_q': (0.0, 0.8),
     'L0_xcond_b_kv': (0.0, 0.8),
     'L0_xcond_b_co': (0.0, 0.376),
     'L0_xcond_b_m1': (0.0, 0.8),
     'L0_xcond_b_m2': (0.0, 2.0),
     'L1_xcond_ln_gamma': (1.0, 0.6),
     'L1_xcond_ln_beta': (0.0, 2.0),
     'L1_xcond_router_b': (0.0, 2.0),
     'L1_xcond_e_b1': (0.0, 2.0),
     'L1_xcond_e_b2': (0.0, 0.8),
     'L1_xcond_gate_b1': (0.0, 2.0),
     'L1_xcond_gate_b2': (0.0, 2.0),
     'L1_xcond_out_b': (0.0, 0.8),
     'L2_xcond_norm1_w': (1.0, 0.6),
     'L2_xcond_normc_w': (1.0, 0.6),
     'L2_xcond_norm2_w': (1.0, 0.6),
     'L3_xcond_b_mod': (0.0, 0.562),
     'L3_xcond_b_qkv': (0.0, 0.8),
     'L3_xcond_b_proj': (0.0, 0.8),
     'L3_xcond_b_qc': (0.0, 2.0),
     'L3_xcond_b_kvc': (0.0, 0.8),
     'L3_xcond_b_cproj': (0.0, 0.8),
     'L3_xcond_b_mlp1': (0.0, 2.0),
     'L3_xcond_b_mlp2': (0.0, 0.8)}
    factors = {'L0_xcond_w_qkv': 8.0,
     'L0_xcond_w_so': 5.308,
     'L0_xcond_w_q': 8.0,
     'L0_xcond_w_kv': 3.889,
     'L0_xcond_w_co': 3.306,
     'L0_xcond_w_m1': 7.163,
     'L0_xcond_w_m2': 7.102,
     'L2_xcond_adaLN_b': 8.0,
     'L2_xcond_qkv_W': 3.089,
     'L2_xcond_attn_out_W': 2.913,
     'L2_xcond_cq_W': 8.0,
     'L2_xcond_ck_W': 8.0,
     'L2_xcond_cv_W': 2.752,
     'L2_xcond_co_W': 2.774,
     'L2_xcond_mlp_b1': 64.0,
     'L2_xcond_mlp_b2': 64.0,
     'L1_xcond_Wq': 8.0,
     'L1_xcond_Wk': 8.0,
     'L1_xcond_Wv': 5.852,
     'L1_xcond_router_W': 5.614,
     'L1_xcond_gate_w1': 8.0,
     'L1_xcond_gate_w2': 6.18,
     'L2_xcond_mlp_W1': 6.771,
     'L2_xcond_mlp_W2': 6.568,
     'L3_xcond_W_qc': 3.56}
    for name, (base, spread) in spreads.items():
        noise = np.random.default_rng([zlib.crc32(name.encode()), seed]).standard_normal(out[name].shape)
        drawn = base * np.exp(spread * noise) if base else spread * noise
        out[name] = jnp.asarray(drawn.astype(out[name].dtype))
    for name, factor in factors.items():
        out[name] = (out[name] * factor).astype(out[name].dtype)
    return out
```

```python
from contextlib import ExitStack

import numpy as np

import concourse.bass as bass
from concourse import mybir

F32 = mybir.dt.float32
BF16 = mybir.dt.bfloat16
U8 = mybir.dt.uint8
ALU = mybir.AluOpType
ACT = mybir.ActivationFunctionType
AX_X = mybir.AxisListType.X

P = 128
B = 2
S = 1024
C = 256
CC = C // P
NT = S // P
H = 16
D = C // H
DV = D + 1
LC = 77
WIN = 128
SHIFT = 64
HID = 1024
E = 3
RH = 512
BLK = 512
NB = S // BLK
TPB = BLK // P
PAIR = 2
GROUPS = H // PAIR
PARTS = 3
Q_RUNS = ((0, 3, 0, 1), (3, 2, 0, 1), (5, 1, 0, 0))
K_RUNS = ((0, 3, 0, 0), (3, 2, 1, 0), (5, 1, 2, 0))
PRODUCTS = 6
ROWS = PRODUCTS * D
BIAS_ROW = ROWS
MAX_ROW = ROWS + 1
STACK = MAX_ROW + 2
MASKED = -(2.0 ** 100)
TAKEN = -3.0e38
ADA = 9 * C
L3MOD = 6 * C


def rope_tables():
    inv = 1.0 / 10000.0 ** (np.arange(0, D, 2, dtype=np.float32) / D)
    f = np.outer(np.arange(S // 2, dtype=np.float32), inv)
    emb = np.concatenate([f, f], axis=-1)
    sign = np.where(np.arange(D) < D // 2, -1.0, 1.0).astype(np.float32)
    cos = np.tile(np.cos(emb).astype(np.float32).T, (P // D, 1))
    sin = np.tile((np.sin(emb).astype(np.float32) * sign).T, (P // D, 1))
    return np.ascontiguousarray(cos), np.ascontiguousarray(sin)


COLS = {}
_at = 0
for _name, _n in (("L0_b_qkv", 3 * C), ("L0_b_q", C), ("L0_b_kv", 2 * C), ("L0_b_m1", 2 * HID),
                  ("L1_gamma", C), ("L1_beta", C), ("L2_n1", C), ("L2_nc", C), ("L2_n2", C),
                  ("L2_b1", HID), ("L3_b_qkv", 3 * C), ("L3_b_qc", C), ("L3_b_kvc", 2 * C), ("L3_b1", HID)):
    COLS[_name] = _at
    _at += _n // P
N_COLS = _at


class Queue:

    def __init__(self, eng, sem, one_by_one=False):
        self.one_by_one = one_by_one
        self.eng, self.sem, self.count, self.met = eng, sem, 0, {}
        self.planned = 0

    def _waits(self, after):
        need = {}
        if self.one_by_one and self.count:
            after = (after, (self.sem, self.count))
        for tok in flat(after):
            s, v = tok
            if self.met.get(s, 0) < v:
                need[s] = max(need.get(s, 0), v)
        self.met.update(need)
        for s, v in need.items():
            self.eng.wait_ge(s, v)

    def do(self, make, *after, ns=60):
        self._waits(after)
        make(self.eng).then_inc(self.sem, 1)
        self.count += 1
        self.planned += ns
        return (self.sem, self.count)

    def group(self, makes, *after, ns=60):
        self._waits(after)
        for make in makes:
            last = make(self.eng)
        last.then_inc(self.sem, 1)
        self.count += 1
        self.planned += ns * len(makes)
        return (self.sem, self.count)

    def dma(self, lane, out, in_, *after):
        self._waits(after)
        self.eng.dma_start(out, in_).then_inc(lane.sem, 16)
        lane.count += 16
        return (lane.sem, lane.count)


class Lane:

    def __init__(self, sem):
        self.sem, self.count = sem, 0

    def all(self):
        return (self.sem, self.count)


def flat(x):
    if x is None:
        return
    if isinstance(x, tuple) and len(x) == 2 and isinstance(x[1], int):
        yield x
        return
    for y in x:
        yield from flat(y)


class Slot:

    def __init__(self, ap):
        self.ap, self.readers, self.busy = ap, (), False

    @property
    def free(self):
        return self.readers

    @free.setter
    def free(self, toks):
        self.readers, self.busy = toks, False


class Ring:
    def __init__(self, aps):
        self.slots, self.n = [Slot(a) for a in aps], 0

    def take(self):
        s = self.slots[self.n % len(self.slots)]
        self.n += 1
        assert not s.busy, "a buffer is taken again before its readers are queued"
        s.busy = True
        return s


def build_program(nc, a, out):
    with ExitStack() as ctx:
        def sb(name, shape, dt=F32):
            return ctx.enter_context(nc.sbuf_tensor(name, shape, dt))

        def sem(name):
            return ctx.enter_context(nc.semaphore(name))

        def lane(name):
            return Lane(sem(name))

        banks = [ctx.enter_context(nc.psum_tensor(f"bank{i}", [P, BLK], F32)) for i in range(8)]
        score_banks = Ring(banks[0:2])
        pv_bank = Slot(banks[2])
        acc_banks = Ring(banks[3:5])
        work = Ring(banks[5:8])

        x = [sb(f"x{b}", [P, NT, C]) for b in range(B)]
        hT = [sb(f"hT{b}", [P, CC, S]) for b in range(B)]
        W = sb("weights", [P, 8192 + 15360])
        wX, wY, wC = W[:, 0:4096], W[:, 4096:8192], W[:, 8192:8192 + 15360]
        q_stack = [sb(f"q_stack{i}", [STACK, PAIR, S], BF16) for i in range(2)]
        k_stack = [sb(f"k_stack{i}", [P, PAIR, S], BF16) for i in range(2)]
        topk_room = [k[:, :, :].rearrange("p h s -> p (h s)").bitcast(F32) for k in k_stack]
        kx_stack = [sb(f"kx_stack{b}", [STACK, H, LC], BF16) for b in range(B)]
        V = sb("v", [P, NT, H, DV])
        Vx = [sb(f"v_context{b}", [LC, H, DV]) for b in range(B)]
        prob = Ring([sb(f"prob{i}", [P, BLK]) for i in range(6)])
        z_ring = Ring([sb(f"z{i}", [P, C]) for i in range(3)])
        t_ring = Ring([sb(f"t{i}", [P, BLK]) for i in range(2)])
        r_ring = Ring([sb(f"r{i}", [P, BLK]) for i in range(2)])
        part_ring = Ring([sb(f"parts{i}", [P, PARTS, BLK], BF16) for i in range(2)])
        hid_ring = Ring([sb(f"hidden{i}", [P, BLK]) for i in range(2)])
        act_ring = Ring([sb(f"gate_act{i}", [P, BLK]) for i in range(2)])
        lhs_ring = Ring([sb(f"lhs{i}", [P, CC, BLK]) for i in range(2)])
        y_ring = Ring([sb(f"y{i}", [P, 2, C]) for i in range(2)])
        tmc = [sb(f"row_consts{b}", [P, 2, C]) for b in range(B)]
        ident = sb("ident", [P, P])
        ident_b = sb("ident_b", [P, P], BF16)
        cols = sb("cols", [P, N_COLS])
        bq = sb("quarter_bias", [P, 16])
        ctxT = sb("ctxT", [P, CC, B, LC])
        condT, scondT = sb("condT", [P, CC, B]), sb("scondT", [P, CC, B])
        mod = {"L0": sb("mod0", [P, ADA // P, B]), "L2": sb("mod2", [P, ADA // P, B]),
               "L3": sb("mod3", [P, L3MOD // P, B])}
        anchor1 = sb("anchor1", [P, E * RH // P + 2, B])
        anchor_r = sb("anchor_r", [E, B])
        kT1 = wY[:, 3596:3596 + CC * B * LC].rearrange("p (c b l) -> p c b l", c=CC, b=B)
        v1 = [sb(f"v1_{b}", [LC, C]) for b in range(B)]
        eb2 = sb("e_b2", [E, C])
        stats = [sb(f"stats{b}", [P, NT, 6]) for b in range(B)]
        mv = [sb(f"mean_var{b}", [P, NT, 2]) for b in range(B)]
        rstd = [sb(f"rstd{b}", [P, NT]) for b in range(B)]
        max2 = Ring([sb(f"max2_{i}", [P, PAIR * NT, NB]) for i in range(2)])
        max1 = Ring([sb(f"max1_{i}", [P, PAIR * NT]) for i in range(2)])
        max_parts = Ring([sb(f"max_parts{i}", [PAIR * NT, 2, P], BF16) for i in range(2)])
        top8 = Ring([sb(f"top{i}", [P, 4, 2, 8]) for i in range(2)])
        s_left = Ring([r[:, 0:8 * LC].rearrange("p (a i n) -> p a i n", a=2, i=4) for r in topk_room])
        s_exp = Ring([r[:, 8 * LC:12 * LC].rearrange("p (i n) -> p i n", i=4) for r in topk_room])
        den = Ring([sb(f"den{i}", [P, TPB, 2, PAIR]) for i in range(2)])
        small = [sb("small", [P, TPB, 8])] * B
        routed = [sb("routed", [P, TPB, C])] * B

        rows_dram = {n: nc.dram_tensor(f"mod_rows_{n}", [B, w], F32, kind="Internal").ap()
                     for n, w in (("L0", ADA), ("L2", ADA), ("L3", L3MOD))}
        qk_dram = [[nc.dram_tensor(f"parts_{n}{b}", [C, PRODUCTS, S], BF16, kind="Internal").ap() for n in "qk"]
                   for b in range(B)]
        kx_dram = [nc.dram_tensor(f"parts_kx{b}", [C, PRODUCTS, LC], BF16, kind="Internal").ap() for b in range(B)]

        pe, ve, ac, po, sp = (Queue(eng, sem(f"{n}_done"), n == "pool") for eng, n in (
            (nc.tensor, "tensor"), (nc.vector, "vector"), (nc.scalar, "scalar"), (nc.gpsimd, "pool"), (nc.sync, "sync")))

        ld_const, ld_cond = lane("ld_const"), lane("ld_cond")
        ld_x = [lane(f"ld_x{b}") for b in range(B)]
        ld_mod = [lane(f"ld_mod{i}") for i in range(4)]
        st_mod = {n: lane(f"st_mod_{n}") for n in ("row0", "row1")}
        ld_tm = [lane(f"ld_tm{b}") for b in range(B)]
        st_parts = [lane(f"st_parts{i}") for i in range(2)]
        ld_kx = [lane(f"ld_kx{b}") for b in range(B)]
        ld_q = [lane(f"ld_q{i}") for i in range(3)]
        ld_k = [lane(f"ld_k{i}") for i in range(3)]
        ld_m = [lane(f"ld_m{i}") for i in range(3)]
        ld_w = {n: lane(f"ld_w{n}") for n in ("L0a", "L0m", "L1a", "L1m", "L2a", "L2m", "L3a", "L3m", "mask", "rope")}
        ld_row = [lane(f"ld_row{i}") for i in range(2)]
        ld_ctx = [lane(f"ld_ctx{b}") for b in range(B)]
        st_out = lane("st_out")

        wt = {}
        cosT, sinT = wC[:, 14336:14336 + 512], wC[:, 14336 + 512:15360]

        def place(region, lane_name, items, after):
            at = 0
            for name, src in items:
                k, n = src.shape[0] // P, src.shape[1]
                dst = region[:, at:at + k * n].rearrange("p (c n) -> p c n", c=k)
                at += k * n
                sp.dma(ld_w[lane_name], dst, src.rearrange("(c p) n -> p c n", p=P), after)
                wt[name] = dst
            return at

        def load_L0a(after=()):
            place(wX, "L0a", [("L0qkv", a["L0_w_qkv"]), ("L0so", a["L0_w_so"]), ("L0q", a["L0_w_q"]),
                              ("L0kv", a["L0_w_kv"]), ("L0co", a["L0_w_co"])], after)

        def load_L0m(after=()):
            place(wC[:, 0:6144], "L0m", [("L0m1", a["L0_w_m1"]), ("L0m2", a["L0_w_m2"])], after)

        def load_L1a(after=()):
            place(wY, "L1a", [("L1q", a["L1_Wq"]), ("L1k", a["L1_Wk"]), ("L1v", a["L1_Wv"]),
                              ("L1g1", a["L1_gate_w1"][0:2 * C, :]), ("L1g2", a["L1_gate_w2"]),
                              ("L1out", a["L1_out_w"]), ("L1r", a["L1_router_W"][0:2 * C, :])], after)

        def load_L1m(after=()):
            n = 0
            for e in range(E):
                n += place(wC[:, 6144 + n:15360], "L1m", [(f"L1w1_{e}", a["L1_e_w1"][e, 0:2 * C, :])], after)
            for e in range(E):
                n += place(wC[:, 6144 + n:15360], "L1m", [(f"L1w2_{e}", a["L1_e_w2"][e])], after)

        def load_L2a(after=()):
            place(wX, "L2a", [("L2qkv", a["L2_qkv_W"]), ("L2so", a["L2_attn_out_W"]), ("L2q", a["L2_cq_W"]),
                              ("L2k", a["L2_ck_W"]), ("L2v", a["L2_cv_W"]), ("L2co", a["L2_co_W"])], after)

        def load_L2m(after=()):
            sp.dma(ld_w["rope"], cosT, a["cos"], after)
            sp.dma(ld_w["rope"], sinT, a["sin"], after)
            place(wC[:, 6144:10240], "L2m", [("L2m1", a["L2_mlp_W1"]), ("L2m2", a["L2_mlp_W2"])], after)

        def load_L3a(after=()):
            place(wY, "L3a", [("L3qkv", a["L3_W_qkv"]), ("L3so", a["L3_W_proj"]), ("L3q", a["L3_W_qc"]),
                              ("L3kv", a["L3_W_kvc"]), ("L3co", a["L3_W_cproj"])], after)

        def load_L3m(after=()):
            place(wC[:, 10240:14336], "L3m", [("L3m1", a["L3_W_mlp1"]), ("L3m2", a["L3_W_mlp2"])], after)

        mask_bias = wC[:, 0:4096].bitcast(BF16).rearrange("p (t k) -> p t k", t=NT)
        mask_u8 = wC[:, 4096:6144].bitcast(U8).rearrange("p (t k) -> p t k", t=NT)
        mask_ready = []

        def load_mask(after=()):
            t = sp.dma(ld_w["mask"], mask_u8, a["mask_self"].rearrange("(t p) k -> p t k", p=P), after)
            for i in range(NT):
                t2 = ve.do(lambda e, i=i: e.tensor_scalar(mask_bias[:, i, :], mask_u8[:, i, :], 1.0, -MASKED,
                                                          ALU.subtract, ALU.mult), t, after)
            mask_ready.append(t2)
            rows_again[2] = (po.do(lambda e: e.memset(spare[0][BIAS_ROW:BIAS_ROW + 1, :, :], 1.0), t2),
                             po.do(lambda e: e.memset(spare[1][BIAS_ROW:STACK, :, :], -1.0), t2),
                             po.do(lambda e: e.memset(spare[1][BIAS_ROW:BIAS_ROW + 1, :, :], 0.0), t2))

        done_with, loaded = {}, {"L0a", "L0m", "L1a", "L1m"}
        NEXT = {"L0a": ("L2a", load_L2a), "L0m": ("mask", load_mask), "L1a": ("L3a", load_L3a),
                "L1m": ("L2m+L3m", lambda after: (load_L2m(after), load_L3m(after)))}

        def finished(region, *toks):
            done_with.setdefault(region, []).append(tuple(flat(toks)))
            if len(done_with[region]) == B:
                name, load = NEXT[region]
                load(tuple(flat(done_with[region])))
                loaded.update(name.split("+"))

        sp.dma(ld_cond, condT[:, :, :], a["condT"].rearrange("(c p) b -> p c b", p=P))
        sp.dma(ld_cond, ident[:, :], a["ident"])
        sp.dma(ld_cond, cols[:, :], a["cols"])
        for b in range(B):
            sp.dma(ld_x[b], x[b][:, :, :], a["x"][b].rearrange("(t p) c -> p t c", p=P))
        xtok = [[ld_x[b].all()] * NT for b in range(B)]
        ident_bt = ve.do(lambda e: e.tensor_copy(ident_b[:, :], ident[:, :]), ld_cond.all())
        silu_t = ac.do(lambda e: e.activation(scondT[:, :, :], condT[:, :, :], ACT.Silu), ld_cond.all())
        ones = []
        ones.append(po.do(lambda e: e.memset(V[:, :, :, D:DV], 1.0)))
        for b in range(B):
            ones.append(po.do(lambda e, b=b: e.memset(Vx[b][:, :, D:DV], 1.0)))
            ones.append(po.do(lambda e, b=b: e.memset(kx_stack[b][BIAS_ROW:STACK, :, :], -1.0)))
            t = po.do(lambda e, b=b: e.memset(kx_stack[b][BIAS_ROW:BIAS_ROW + 1, :, :], 0.0), ones[-1])
            ones.append(t)
        for i in range(2):
            t = po.do(lambda e, i=i: e.memset(k_stack[i][BIAS_ROW:STACK, :, :], -1.0))
            ones.append(po.do(lambda e, i=i: e.memset(k_stack[i][BIAS_ROW:BIAS_ROW + 1, :, :], 0.0), t))
            ones.append(po.do(lambda e, i=i: e.memset(q_stack[i][BIAS_ROW:BIAS_ROW + 1, :, :], 1.0)))
        stacks_init = tuple(ones)

        w_slots = [prob.slots[2 * i:2 * i + 2] for i in range(3)]
        pieces = []
        for n, w, bias, width in (("L0", "L0_w_ada", "L0_b_ada", ADA), ("L2", "L2_adaLN_W", "L2_adaLN_b", ADA),
                                  ("L3", "L3_W_mod", "L3_b_mod", L3MOD)):
            for c0 in range(0, width, BLK):
                k = min(BLK, width - c0)
                pieces.append((n, a[w][:, c0:c0 + k], a[bias][c0:c0 + k], k, mod[n], c0 // P, n != "L2",
                               rows_dram[n][:, c0:c0 + k]))
        for e in range(E):
            pieces.append(("L1", a["L1_e_w1"][e, 2 * C:3 * C, :], a["L1_e_b1"][e], RH, anchor1, e * RH // P, False, None))
        pieces.append(("L1", a["L1_gate_w1"][2 * C:3 * C, :], a["L1_gate_b1"], C, anchor1, E * RH // P, False, None))
        pieces.append(("L1", a["L1_router_W"][2 * C:3 * C, :], a["L1_router_b"], E, anchor_r, None, False, None))
        row_ring = Ring([t_ring.slots[0], t_ring.slots[1]])
        mod_done, gates_stored = {}, {}
        row_of = {id(s): i for i, s in enumerate(t_ring.slots)}

        def prologue(names):
            for n, w, bias, k, dst, c0, silu, rows in pieces:
                if n not in names:
                    continue
                i = prologue.n % 3
                prologue.n += 1
                two, rs, bs = w_slots[i], t_ring.take(), r_ring.take()
                lane_ = ld_mod[i]
                for c in range(CC):
                    sp.dma(lane_, two[c].ap[:, 0:k], w[c * P:(c + 1) * P, :], two[c].free)
                t = sp.dma(lane_, bs.ap[0:B, 0:k], bias.partition_broadcast(B), bs.free)
                bank, lhs = work.take(), scondT if silu else condT
                t = pe.group([lambda e, c=c, two=two, k=k, bank=bank, lhs=lhs: e.matmul(
                    bank.ap[0:B, 0:k], lhs[:, c, :], two[c].ap[:, 0:k], start=c == 0, stop=c == CC - 1)
                    for c in range(CC)], t, silu_t, ld_cond.all(), bank.free)
                for c in range(CC):
                    two[c].free = t
                t = ve.do(lambda e, rs=rs, bs=bs, k=k, bank=bank: e.tensor_tensor(
                    rs.ap[0:B, 0:k], bank.ap[0:B, 0:k], bs.ap[0:B, 0:k], ALU.add), t, lane_.all(), rs.free)
                bank.free = bs.free = t
                users = []
                if rows is not None:
                    users.append(sp.dma(st_mod[f"row{row_of[id(rs)]}"], rows, rs.ap[0:B, 0:k], t))
                bank = work.take()
                m = max(1, k // P)
                kk = min(k, P)
                t = pe.group([lambda e, j=j, rs=rs, bank=bank, kk=kk: e.transpose(
                    bank.ap[0:kk, 2 * j:2 * j + 2], rs.ap[0:B, j * P:j * P + kk], ident[0:B, 0:B])
                    for j in range(m)], t, bank.free)
                users.append(t)
                rs.free = tuple(users)
                src = bank.ap[0:kk, 0:2 * m]
                if c0 is None:
                    t = ve.do(lambda e, dst=dst, src=src: e.tensor_copy(dst[:, :], src), t)
                else:
                    t = ve.do(lambda e, dst=dst, src=src, c0=c0, m=m: e.tensor_copy(
                        dst[:, c0:c0 + m, :], src.rearrange("p (m b) -> p m b", b=B)), t)
                bank.free = t
                mod_done[n] = (t,)
            for n in names:
                if n == "L1":
                    continue
                nine = ADA // P
                sc = [2, 8, 14] if n != "L3" else [2, 8]
                t = mod_done[n]
                for i, s in enumerate(sc):
                    t = ve.do(lambda e, n=n, s=s: e.tensor_scalar(mod[n][:, s:s + 2, :], mod[n][:, s:s + 2, :],
                                                                  1.0, None, ALU.add), t)
                    if n == "L2":
                        for c in range(CC):
                            col = COLS[("L2_n1", "L2_nc", "L2_n2")[i]] + c
                            t = ve.do(lambda e, n=n, s=s, c=c, col=col: e.tensor_scalar(
                                mod[n][:, s + c, :], mod[n][:, s + c, :], cols[:, col:col + 1], None, ALU.mult), t)
                mod_done[n] = (t,)
                gates_stored[n] = [l.all() for l in st_mod.values()]
        prologue.n = 0

        def quarter(i, name, n):
            c = COLS[name]
            return ve.do(lambda e: e.tensor_scalar(bq[:, i:i + n], cols[:, c:c + n], 0.25, None, ALU.mult), ld_cond.all())

        prologue(["L0"])
        load_L0a()
        quarter_t = [quarter(0, "L0_b_qkv", 2), quarter(2, "L0_b_q", 2), quarter(4, "L3_b_qkv", 2), quarter(6, "L3_b_qc", 2)]
        sp.dma(ld_const, ctxT[:, :, :, :], a["ctxT"].rearrange("(c p) b l -> p c b l", p=P))
        sp.dma(ld_const, eb2[:, :], a["L1_e_b2"])
        load_L0m()
        load_L1a()
        prologue(["L1", "L2", "L3"])
        load_L1m()
        const_t = ld_const.all()

        def layer_norm(b, eps, scale, bias, after, dst, blk=None, roll=False, n_part=P):
            tiles = range(NT) if blk is None else range(blk * TPB, (blk + 1) * TPB)
            lo, hi = tiles[0], tiles[-1] + 1
            ts = []
            for t in tiles:
                s = ve.do(lambda e, t=t: e.bn_stats(stats[b][:, t, :], x[b][:, t, :]), xtok[b][t])
                ts.append(ve.do(lambda e, t=t: e.bn_aggr(mv[b][:, t, :], stats[b][:, t, :]), s))
            t = ve.do(lambda e: e.tensor_scalar(rstd[b][:, lo:hi], mv[b][:, lo:hi, 1], eps, None, ALU.add), ts)
            t = ac.do(lambda e: e.activation(rstd[b][:, lo:hi], rstd[b][:, lo:hi], ACT.Sqrt), t)
            rs = ve.do(lambda e: e.reciprocal(rstd[b][:, lo:hi], rstd[b][:, lo:hi]), t)
            yield
            out_t = []
            for bl in range(lo // TPB, hi // TPB):
                two = [work.take(), work.take()]
                for i in range(TPB):
                    z, t = z_ring.take(), bl * TPB + i
                    zt = ve.do(lambda e, z=z, t=t: e.tensor_scalar(
                        z.ap[:, :], x[b][:, t, :], mv[b][:, t, 0:1], rstd[b][:, t:t + 1],
                        ALU.subtract, ALU.mult), rs, z.free)
                    pt = pe.group([lambda e, c=c, z=z, i=i, two=two: e.transpose(
                        two[c].ap[:, i * P:(i + 1) * P], z.ap[:, c * P:(c + 1) * P], ident[:, :])
                        for c in range(CC)], zt, two[0].free, two[1].free)
                    z.free = pt
                for c in range(CC):
                    for src, to, n in dst_runs(bl, roll):
                        t = ac.do(lambda e, c=c, two=two, src=src, to=to, n=n: e.activation(
                            dst[:, c, to:to + n], two[c].ap[:, src:src + n], ACT.Identity,
                            scale=scale(c), bias=bias(c)), pt, after)
                        out_t.append(t)
                    two[c].free = t
                yield
            return tuple(out_t)

        def dst_runs(bl, roll):
            if not roll:
                return [(0, bl * BLK, BLK)]
            if bl == 0:
                return [(0, S - SHIFT, SHIFT), (SHIFT, 0, BLK - SHIFT)]
            return [(0, bl * BLK - SHIFT, BLK)]

        def mod_col(n, s, b):
            return lambda c: mod[n][:, s + c, b:b + 1]

        def store_runs(lane_, dram, c, col0, parts, runs, *after):
            for row, n, part, step in runs:
                src = parts[:, part:part + n, :] if step else parts[:, part:part + 1, :].to_broadcast([P, n, parts.shape[2]])
                t = sp.dma(lane_, dram[c * P:(c + 1) * P, row:row + n, col0:col0 + parts.shape[2]], src, after)
            return t

        def split_parts(bank, t0, n, scale, bias, dram, runs, c, col0, rope=None, free_dram=()):
            t_, r_, p_ = t_ring.take(), r_ring.take(), part_ring.take()
            lane_ = st_parts[part_ring.slots.index(p_)]
            tf, rf, pf = t_.ap[:, 0:n], r_.ap[:, 0:n], p_.ap
            bap = bank.ap[:, 0:n]
            t1 = ac.do(lambda e: e.activation(tf, bap, ACT.Identity, scale=scale, bias=bias), t0, t_.free, r_.free)
            bank.free = t1
            if rope is not None:
                mask = [(i & 16) | ((i + 8) & 15) for i in range(32)]
                s1 = ve.do(lambda e: e.stream_shuffle(rf, tf, mask), t1, r_.free)
                s2 = ve.do(lambda e: e.tensor_tensor(rf, rf, sinT, ALU.mult), s1, ld_w["rope"].all())
                s3 = po.do(lambda e: e.tensor_tensor(tf, tf, cosT, ALU.mult), t1, s1, ld_w["rope"].all())
                t1 = ve.do(lambda e: e.tensor_tensor(tf, tf, rf, ALU.add), s2, s3)
            t2 = ve.do(lambda e: e.tensor_copy(pf[:, 0, 0:n], tf), t1, p_.free)
            t3 = po.do(lambda e: e.tensor_tensor(rf, tf, pf[:, 0, 0:n], ALU.subtract), t1, t2, r_.free)
            t4 = ve.do(lambda e: e.tensor_copy(pf[:, 1, 0:n], rf), t3)
            t5 = ve.do(lambda e: e.tensor_tensor(pf[:, 2, 0:n], rf, pf[:, 1, 0:n], ALU.subtract), t4)
            t_.free, r_.free = (t3,), (t5,)
            if isinstance(dram, list):
                ts = [store_runs(lane_, dram[b], c, 0, pf[:, :, b * LC:(b + 1) * LC], runs, t2, t4, t5, free_dram)
                      for b in range(B)]
            else:
                ts = [store_runs(lane_, dram, c, col0, pf[:, :, 0:n], runs, t2, t4, t5, free_dram)]
            p_.free = ts[-1]
            return ts[-1]

        parts_read = [[(), ()] for _ in range(B)]

        def project_parts(b, which, w, col, scale, bias, h_tok, rope=False):
            last, parts_stored = (), []
            for c in range(CC):
                for bl in range(NB):
                    bank = work.take()
                    t = pe.group([lambda e, k=k, c=c, bl=bl, bank=bank: e.matmul(
                        bank.ap[:, :], w[:, k, col + c * P:col + (c + 1) * P], hT[b][:, k, bl * BLK:(bl + 1) * BLK],
                        start=k == 0, stop=k == CC - 1) for k in range(CC)], h_tok, bank.free, ns=840)
                    last = t
                    parts_stored.append(split_parts(bank, t, BLK, scale, bias(c), qk_dram[b][which], (Q_RUNS, K_RUNS)[which], c, bl * BLK,
                                                    rope=rope or None, free_dram=parts_read[b][which]))
                    yield
            return last, tuple(parts_stored)

        v_slot = Slot(V)

        def project_v(b, w, col, h_tok, bias_t):
            ts = []
            for tp in range(0, NT, 2):
                bank = work.take()
                t = pe.group([lambda e, i=i, k=k, tp=tp, bank=bank: e.matmul(
                    bank.ap[:, i * C:(i + 1) * C], hT[b][:, k, (tp + i) * P:(tp + i + 1) * P],
                    w[:, k, col:col + C], start=k == 0, stop=k == CC - 1)
                    for i in range(2) for k in range(CC)], h_tok, bank.free, ns=430)
                src = bank.ap[:, :].rearrange("p (t h d) -> p t h d", t=2, h=H)
                dst = V[:, tp:tp + 2, :, 0:D]
                if bias_t is None:
                    t2 = ve.do(lambda e, dst=dst, src=src: e.tensor_copy(dst, src), t, v_slot.free, stacks_init)
                else:
                    bv = tmc[b][:, 1, :].rearrange("p (h d) -> p h d", h=H)
                    for i in range(2):
                        t2 = ve.do(lambda e, dst=dst, src=src, i=i: e.tensor_tensor(
                            dst[:, i], src[:, i], bv, ALU.add), t, v_slot.free, stacks_init, bias_t)
                bank.free = t2
                ts.append(t2)
                yield
            return (tuple(ts), t)

        def load_stack(dst, dram, h0, lane_, *after):
            rows = dram[h0 * D:(h0 + PAIR) * D, :, :].rearrange("(h d) r t -> (d r) h t", d=D)
            return sp.dma(lane_, dst[0:ROWS, :, :], rows, after)

        spare = [wC[:, 4096 + 1024 * i:5120 + 1024 * i].bitcast(BF16).rearrange("p (h s) -> p h s", h=PAIR)
                 for i in range(2)]
        q_slots, k_slots = [Slot(t) for t in q_stack] + [Slot(spare[0])], [Slot(t) for t in k_stack] + [Slot(spare[1])]
        rows_again = [(), (), ()]
        attention_lock = [None]

        def attention(b, kind, mask, stored):
            out_view = hT[b][:, :, :].rearrange("p c (t f) -> p (c t) f", f=C)
            own_k = kind in ("window", "full")
            nk = P if own_k else LC
            depth = 3 if kind in ("full", "context") else 2
            heads = range(PAIR)
            v_all = V if own_k else Vx[b]
            all_reads, out_t = [], []

            def load(g):
                i = g % depth
                q, k = q_slots[i], k_slots[i]
                tq = load_stack(q.ap, qk_dram[b][0], g * PAIR, ld_q[i], stored["q"], q.free)
                parts_read[b][0] = (tq,)
                tk = ()
                if own_k:
                    tk = load_stack(k.ap, qk_dram[b][1], g * PAIR, ld_k[i], stored["k"], k.free)
                    parts_read[b][1] = (tk,)
                else:
                    tk = stored["k"]
                return dict(g=g, i=i, q=q, k=k, t=(tq, tk, stacks_init, rows_again[i]), reads=[], kreads=[])

            def key_rows(st, h, rows, lo, n):
                if own_k:
                    return st["k"].ap[0:rows, h, lo:lo + n]
                return kx_stack[b][0:rows, st["g"] * PAIR + h, 0:LC]

            def max_pieces(st):
                m2 = max2.take() if kind == "full" else None
                m1 = max1.take()
                red = []
                if kind == "full":
                    for h in heads:
                        for qt in range(NT):
                            for half in range(NB):
                                bank = work.take()
                                t = pe.do(lambda e, h=h, qt=qt, half=half, bank=bank: e.matmul(
                                    bank.ap[:, :], st["q"].ap[0:MAX_ROW, h, qt * P:(qt + 1) * P],
                                    st["k"].ap[0:MAX_ROW, h, half * BLK:(half + 1) * BLK], start=True, stop=True),
                                    st["t"], bank.free, ns=214)
                                to = m2.ap[:, h * NT + qt, half:half + 1]
                                if mask:
                                    t = ve.do(lambda e, bank=bank, qt=qt, half=half, to=to: e.tensor_tensor_reduce(
                                        bank.ap[:, :], bank.ap[:, :], mask_bias[:, qt, half * BLK:(half + 1) * BLK],
                                        1.0, -3.4e38, ALU.add, ALU.max, to), t, m2.free, mask_ready)
                                else:
                                    t = ve.do(lambda e, bank=bank, to=to: e.tensor_reduce(
                                        to, bank.ap[:, :], AX_X, ALU.max), t, m2.free)
                                bank.free = t
                                red.append(t)
                                yield
                    t = ve.do(lambda e: e.tensor_reduce(m1.ap[:, :], m2.ap[:, :, :], AX_X, ALU.max), red, m1.free)
                    m2.free = t
                else:
                    per = 4
                    n = nk
                    for h in heads:
                        for q0 in range(0, NT, per):
                            bank = work.take()
                            t = pe.group([lambda e, h=h, q0=q0, i=i, bank=bank: e.matmul(
                                bank.ap[:, i * n:(i + 1) * n], st["q"].ap[0:MAX_ROW, h, (q0 + i) * P:(q0 + i + 1) * P],
                                key_rows(st, h, MAX_ROW, (q0 + i) * P, P), start=True, stop=True)
                                for i in range(per)], st["t"], bank.free)
                            t = ve.do(lambda e, h=h, q0=q0, bank=bank: e.tensor_reduce(
                                m1.ap[:, h * NT + q0:h * NT + q0 + per],
                                bank.ap[:, 0:per * n].rearrange("p (i n) -> p i n", n=n), AX_X, ALU.max), t, m1.free)
                            bank.free = t
                            red.append(t)
                            yield
                    t = red
                bank, mp = work.take(), max_parts.take()
                n = PAIR * NT
                t = pe.do(lambda e: e.transpose(bank.ap[0:n, 0:P], m1.ap[:, :], ident[:, :]), t, bank.free)
                m1.free = t
                t1 = ve.do(lambda e: e.tensor_copy(mp.ap[:, 0, :], bank.ap[0:n, 0:P]), t, mp.free)
                t2 = ve.do(lambda e: e.tensor_tensor(mp.ap[:, 1, :], bank.ap[0:n, 0:P], mp.ap[:, 0, :],
                                                     ALU.subtract), t1)
                bank.free = t2
                rows = st["q"].ap
                for part in range(2):
                    sp.dma(ld_m[st["i"]], rows[MAX_ROW + part:MAX_ROW + part + 1, :, :].rearrange(
                        "r h (t q) -> r (h t) q", q=P), mp.ap[:, part, :], t2, st["q"].free)
                mp.free = ld_m[st["i"]].all()
                st["t"] = (st["t"], ld_m[st["i"]].all())
                yield

            def evac_exp(bank, t, half):
                p = prob.take()
                t = ac.do(lambda e: e.activation(p.ap[0:nk, :], bank.ap[0:nk, :], ACT.Exp), t, p.free)
                bank.free = t
                return p, t

            def pv(st, kt, tiles, first, last):
                t = None
                for half, h, p, tp in tiles:
                    strip = (half * PAIR + h) * 32
                    o = pv_bank.ap
                    head = st["g"] * PAIR + h
                    if kind == "window":
                        makes = [lambda e, i=i, half=half, head=head, strip=strip, p=p: e.matmul(
                            o[strip:strip + DV, i * P:(i + 1) * P], V[:, half * TPB + i, head, :],
                            p.ap[:, i * P:(i + 1) * P], start=True, stop=True, tile_position=(0, strip))
                            for i in range(TPB)]
                    else:
                        vv = V[:, kt, head, :] if own_k else Vx[b][:, head, :]
                        makes = [lambda e, vv=vv, strip=strip, p=p: e.matmul(
                            o[strip:strip + DV, :], vv, p.ap[0:nk, :], start=first, stop=last,
                            tile_position=(0, strip))]
                    t = pe.group(makes, tp, pv_bank.free if first else (), stored["v"], ns=230 if kind != "window" else 60)
                    p.free = t
                return t

            def finish(st, t):
                pv_out = t_ring.take()
                t1 = ve.do(lambda e: e.tensor_copy(pv_out.ap[:, :], pv_bank.ap[:, :]), t, pv_out.free, strips_zero)
                pv_bank.free = t1
                bank = work.take()
                t = pe.group([lambda e, i=i: e.transpose(bank.ap[:, i * P:(i + 1) * P],
                                                         pv_out.ap[:, i * P:(i + 1) * P], ident[:, :])
                              for i in range(TPB)], t1, bank.free)
                pv_out.free = t
                d = den.take()
                v5 = bank.ap[:, :].rearrange("p (t a h d) -> p t a h d", t=TPB, a=2, h=PAIR)
                for half in range(2):
                    r = ve.do(lambda e, half=half: e.reciprocal(d.ap[:, :, half, :], v5[:, :, half, :, D]), t, d.free)
                    to = out_view[:, half * TPB:(half + 1) * TPB, st["g"] * PAIR * D:(st["g"] + 1) * PAIR * D]
                    for h in heads:
                        dh = d.ap[:, :, half, h:h + 1].to_broadcast([P, TPB, D])
                        t2 = ve.do(lambda e, half=half, h=h, to=to, dh=dh: e.tensor_tensor(
                            to[:, :, h * D:(h + 1) * D], v5[:, :, half, h, 0:D], dh, ALU.mult), r, t, stored["h_free"])
                        out_t.append(t2)
                bank.free = d.free = t2

            def main_pieces(st):
                pend = None
                kts = range(NT) if kind == "full" else range(1)
                for kt in kts:
                    tiles = []
                    for half in range(2):
                        for h in heads:
                            bank = score_banks.take()
                            makes = []
                            if kind == "window":
                                makes = [lambda e, i=i, h=h, half=half, bank=bank: e.matmul(
                                    bank.ap[:, i * P:(i + 1) * P],
                                    st["k"].ap[0:STACK, h, (half * TPB + i) * P:(half * TPB + i + 1) * P],
                                    st["q"].ap[0:STACK, h, (half * TPB + i) * P:(half * TPB + i + 1) * P],
                                    start=True, stop=True) for i in range(TPB)]
                            else:
                                makes = [lambda e, h=h, half=half, bank=bank, kt=kt: e.matmul(
                                    bank.ap[0:nk, :], key_rows(st, h, STACK, kt * P, P),
                                    st["q"].ap[0:STACK, h, half * BLK:(half + 1) * BLK], start=True, stop=not mask)]
                                if mask:
                                    makes += [lambda e, i=i, half=half, bank=bank, kt=kt: e.matmul(
                                        bank.ap[:, i * P:(i + 1) * P],
                                        mask_bias[:, half * TPB + i, kt * P:(kt + 1) * P], ident_b[:, :],
                                        start=False, stop=i == TPB - 1) for i in range(TPB)]
                            t = pe.group(makes, st["t"], bank.free, ident_bt, mask_ready if mask else (), ns=90)
                            st["last"] = t
                            p, tp = evac_exp(bank, t, half)
                            tiles.append((half, h, p, tp))
                        yield
                        if half == 0 and pend is not None:
                            pv(st, *pend, kt - 1 == 0, False)
                            pend = None
                            yield
                    pend = (kt, tiles)
                t = pv(st, *pend, len(kts) == 1, True)
                st["q"].free = (st["last"],)
                st["k"].free = (st["last"],)
                finish(st, t)
                yield

            def topk_pieces(st):
                per = TPB
                for half in range(2):
                    tiles = []
                    for h in heads:
                        head = st["g"] * PAIR + h
                        bank = work.take()
                        t = pe.group([lambda e, h=h, half=half, i=i, bank=bank: e.matmul(
                            bank.ap[:, i * LC:(i + 1) * LC],
                            st["q"].ap[0:ROWS, h, (half * TPB + i) * P:(half * TPB + i + 1) * P],
                            kx_stack[b][0:ROWS, head, :], start=True, stop=True)
                            for i in range(per)], st["t"], bank.free)
                        st["last"] = t
                        sc = bank.ap[:, 0:per * LC].rearrange("p (i n) -> p i n", n=LC)
                        top, left, ex = top8.take(), s_left.take(), s_exp.take()
                        room_free = [s.free for s in k_slots]
                        a1 = [ve.do(lambda e, i=i, sc=sc, top=top: e.max(top.ap[:, i, 0, :], sc[:, i, :]), t, top.free)
                              for i in range(per)]
                        a2 = [ve.do(lambda e, i=i, sc=sc, top=top, left=left: e.match_replace(
                            out=left.ap[:, 0, i, :], in_to_replace=top.ap[:, i, 0, :], in_values=sc[:, i, :],
                            imm_value=TAKEN), a1[i], left.free, room_free) for i in range(per)]
                        sub = ve.do(lambda e, sc=sc, top=top, ex=ex: e.tensor_tensor(
                            ex.ap[:, :, :], sc, top.ap[:, :, 0, 0:1].to_broadcast([P, per, LC]), ALU.subtract),
                            a1, ex.free, room_free)
                        bank.free = (sub, a2[-1])
                        xp = ac.do(lambda e, ex=ex: e.activation(ex.ap[:, :, :], ex.ap[:, :, :], ACT.Exp), sub)
                        a3 = [ve.do(lambda e, i=i, top=top, left=left: e.max(
                            top.ap[:, i, 1, :], left.ap[:, 0, i, :]), a2[i]) for i in range(per)]
                        a4 = [ve.do(lambda e, i=i, top=top, left=left: e.match_replace(
                            out=left.ap[:, 1, i, :], in_to_replace=top.ap[:, i, 1, :], in_values=left.ap[:, 0, i, :],
                            imm_value=TAKEN), a3[i]) for i in range(per)]
                        top.free = a4[-1]
                        keep = ve.do(lambda e, ex=ex, left=left: e.scalar_tensor_tensor(
                            out=ex.ap[:, :, :], in0=left.ap[:, 1, :, :], scalar=TAKEN, in1=ex.ap[:, :, :],
                            op0=ALU.is_equal, op1=ALU.mult), a4, xp)
                        left.free = keep
                        bank, p = work.take(), prob.take()
                        t = pe.group([lambda e, i=i, ex=ex, bank=bank: e.transpose(
                            bank.ap[0:LC, i * P:(i + 1) * P], ex.ap[:, i, :], ident[:, :])
                            for i in range(per)], keep, bank.free)
                        ex.free = t
                        t = ac.do(lambda e, bank=bank, p=p: e.activation(p.ap[0:LC, :], bank.ap[0:LC, :], ACT.Copy),
                                  t, p.free)
                        bank.free = t
                        tiles.append((half, h, p, t))
                        yield
                    t = pv(st, 0, tiles, half == 0, True) if half == 0 else pv2(st, tiles)
                st["q"].free = (st["last"],)
                finish(st, t)
                yield

            def pv2(st, tiles):
                t = None
                for half, h, p, tp in tiles:
                    strip = (half * PAIR + h) * 32
                    t = pe.do(lambda e, h=h, strip=strip, p=p: e.matmul(
                        pv_bank.ap[strip:strip + DV, :], Vx[b][:, st["g"] * PAIR + h, :], p.ap[0:LC, :],
                        start=True, stop=True, tile_position=(0, strip)), tp)
                    p.free = t
                return t

            ready = [load(g) for g in range(depth - 1)]
            if kind != "topk":
                for _ in max_pieces(ready[0]):
                    yield
            for g in range(GROUPS):
                st = ready.pop(0)
                if g + depth - 1 < GROUPS:
                    ready.append(load(g + depth - 1))
                ahead = max_pieces(ready[0]) if ready and kind != "topk" else iter(())
                if kind == "full":
                    made, rate = 0.0, 33 / 20
                    for _ in main_pieces(st):
                        made += rate
                        while made >= 1:
                            made -= 1
                            if next(ahead, "end") == "end":
                                made = -1e9
                        yield
                else:
                    if kind == "context":
                        for _ in ahead:
                            yield
                    for _ in (topk_pieces if kind == "topk" else main_pieces)(st):
                        yield
                for _ in ahead:
                    yield
                if kind == "window":
                    yield 4000
            if kind == "topk":
                for i in range(2):
                    t = po.do(lambda e, i=i: e.memset(k_stack[i][BIAS_ROW:STACK, :, :], -1.0), s_left.slots[i].free,
                              s_exp.slots[i].free)
                    t = po.do(lambda e, i=i: e.memset(k_stack[i][BIAS_ROW:BIAS_ROW + 1, :, :], 0.0), t)
                    k_slots[i].free = t
                    rows_again[i] = t
            return tuple(out_t)

        z0 = ve.do(lambda e: e.memset(banks[2][:, :], 0.0))
        strips_zero = z0
        pv_bank.free = z0

        def token_consts(b, gate, bias, bias_v=None, last=()):
            if gate is not None:
                sp.dma(ld_tm[b], tmc[b][:, 0, :], rows_dram[gate[0]][b, gate[1]:gate[1] + C].partition_broadcast(P),
                       last, gates_stored[gate[0]])
            if bias is not None:
                sp.dma(ld_tm[b], tmc[b][:, 1, :], bias.partition_broadcast(P), last)
            return ld_tm[b].all()

        def pre_add(b, t_const, gated, tiles=range(0, NT, 2)):
            row = tmc[b][:, 1:2, :]
            if gated:
                t_const = (t_const, po.do(lambda e: e.tensor_tensor(tmc[b][:, 1, :], tmc[b][:, 1, :], tmc[b][:, 0, :],
                                                                    ALU.mult), t_const))
            for tp in tiles:
                for i in range(2):
                    t = po.do(lambda e, tp=tp, i=i: e.tensor_tensor(x[b][:, tp + i, :], x[b][:, tp + i, :],
                                                                    row[:, 0, :], ALU.add),
                              t_const, xtok[b][tp + i], xread[b])
                    xtok[b][tp + i] = (xtok[b][tp + i], t)
            return t

        xread = [() for _ in range(B)]

        def add_to_x(b, bank, t, tp, gated, t_const):
            src = bank.ap[:, :].rearrange("p (t f) -> p t f", t=2)
            if not gated:
                t = ve.do(lambda e: e.tensor_tensor(x[b][:, tp:tp + 2, :], x[b][:, tp:tp + 2, :], src, ALU.add),
                          t, xtok[b][tp], xtok[b][tp + 1], xread[b])
                bank.free = t
            else:
                y = y_ring.take()
                for i in range(2):
                    t1 = ve.do(lambda e, i=i: e.tensor_tensor(y.ap[:, i, :], src[:, i, :], tmc[b][:, 0, :], ALU.mult),
                               t, t_const, y.free)
                bank.free = t1
                t = po.do(lambda e: e.tensor_tensor(x[b][:, tp:tp + 2, :], x[b][:, tp:tp + 2, :], y.ap[:, :, :],
                                                    ALU.add), t1, xtok[b][tp], xtok[b][tp + 1], xread[b])
                y.free = t
            xtok[b][tp] = xtok[b][tp + 1] = (t,)
            return t

        def out_project(b, w, o_tok, gated, t_const, roll):
            o_view = hT[b][:, :, :].rearrange("p c (t f) -> p (c t) f", f=C)
            last = ()
            pend = []
            for bl in range(NB):
                banks_, lhs = [work.take(), work.take()], lhs_ring.take()
                for c in range(CC):
                    makes = []
                    if not roll:
                        for i in range(TPB):
                            makes.append(lambda e, i=i, c=c, bl=bl, bank=banks_[c]: e.transpose(
                                bank.ap[:, i * P:(i + 1) * P], o_view[:, bl * TPB + i, c * P:(c + 1) * P], ident[:, :]))
                    else:
                        for i in range(TPB):
                            r = bl * TPB + i
                            makes.append(lambda e, i=i, c=c, r=r, bank=banks_[c]: e.transpose(
                                bank.ap[:, i * P:(i + 1) * P], o_view[:, r, c * P:(c + 1) * P], ident[:, :]))
                    t = pe.group(makes, o_tok, banks_[c].free)
                    last = t
                    t = ac.do(lambda e, c=c, lhs=lhs, bank=banks_[c]: e.activation(lhs.ap[:, c, :], bank.ap[:, :], ACT.Copy),
                              t, lhs.free)
                    banks_[c].free = t
                    pend.append(t)
                if not roll:
                    for tp in range(0, TPB, 2):
                        t = project_pair(b, w, [[(lhs, (tp + i) * P, P, 0)] for i in range(2)], bl * TPB + tp, pend, gated, t_const)
                    lhs.free = t
                    yield
                else:
                    if bl == 0:
                        first = lhs
                        continue
                    def where(tok):
                        r = (tok - SHIFT) % S
                        return (first if r < BLK else lhs), r % BLK
                    for tp in range(0, NT, 2):
                        srcs = []
                        for i in range(2):
                            s0, s1 = where((tp + i) * P), where((tp + i) * P + SHIFT)
                            srcs.append([(s0[0], s0[1], SHIFT, 0), (s1[0], s1[1], SHIFT, SHIFT)])
                        t = project_pair(b, w, srcs, tp, pend, gated, t_const)
                    first.free = lhs.free = t
            return last

        def project_pair(b, w, srcs, tile, after, gated, t_const):
            bank = work.take()
            makes = []
            for i, runs in enumerate(srcs):
                for buf, col, n, row in runs:
                    for k in range(CC):
                        makes.append(lambda e, i=i, k=k, buf=buf, col=col, n=n, row=row, bank=bank: e.matmul(
                            bank.ap[row:row + n, i * C:(i + 1) * C], buf.ap[:, k, col:col + n], w[:, k, :],
                            start=k == 0, stop=k == CC - 1))
            t = pe.group(makes, after, bank.free, ns=430)
            add_to_x(b, bank, t, tile, gated, t_const)
            return t

        hidden_holder = [None]

        def hold_hidden(b):
            while hidden_holder[0] not in (None, b):
                yield "wait"
            hidden_holder[0] = b

        def mlp(b, name, h_tok, func, gated_unit, t_const):
            yield from hold_hidden(b)
            w1, w2 = wt[name + "m1"], wt[name + "m2"]
            c1 = COLS[{"L0": "L0_b_m1", "L2": "L2_b1", "L3": "L3_b1"}[name]]
            last = ()
            for bl in range(NB):
                accs = [acc_banks.take(), acc_banks.take()]
                pend = None

                def down(j, hid, t):
                    makes = [lambda e, i=i, j=j, hid=hid: e.matmul(
                        accs[i // 2].ap[:, (i % 2) * C:(i % 2 + 1) * C], hid.ap[:, i * P:(i + 1) * P], w2[:, j, :],
                        start=(j == 0 and i % 2 == 0), stop=j == HID // P - 1, skip_group_check=True)
                        for i in range(TPB)]
                    t = pe.group(makes, t, accs[0].free if j == 0 else (), accs[1].free if j == 0 else (), ns=430)
                    hid.free = t
                    return t

                for j in range(HID // P):
                    ups = []
                    for part in ((0, HID) if gated_unit else (0,)):
                        bank = work.take()
                        t = pe.group([lambda e, k=k, j=j, part=part, bank=bank: e.matmul(
                            bank.ap[:, :], w1[:, k, part + j * P:part + (j + 1) * P], hT[b][:, k, bl * BLK:(bl + 1) * BLK],
                            start=k == 0, stop=k == CC - 1) for k in range(CC)], h_tok, bank.free, ns=840)
                        ups.append((bank, t))
                    hid = hid_ring.take()
                    bank, t = ups[0]
                    if gated_unit:
                        act = act_ring.take()
                        t1 = ac.do(lambda e, j=j, bank=bank, act=act: e.activation(
                            act.ap[:, :], bank.ap[:, :], func, bias=cols[:, c1 + j:c1 + j + 1]), t, act.free)
                        bank.free = t1
                        bank2, t2 = ups[1]
                        t = ve.do(lambda e, j=j, bank2=bank2, act=act, hid=hid: e.scalar_tensor_tensor(
                            out=hid.ap[:, :], in0=bank2.ap[:, :], scalar=cols[:, c1 + 8 + j:c1 + 9 + j],
                            in1=act.ap[:, :], op0=ALU.add, op1=ALU.mult), t1, t2, hid.free)
                        act.free = bank2.free = t
                    else:
                        t = ac.do(lambda e, j=j, bank=bank, hid=hid: e.activation(
                            hid.ap[:, :], bank.ap[:, :], func, bias=cols[:, c1 + j:c1 + j + 1]), t, hid.free)
                        bank.free = t
                    if pend is not None:
                        down(*pend)
                    pend = (j, hid, t)
                    yield
                last = down(*pend)
                for i in range(2):
                    add_to_x(b, accs[i], last, bl * TPB + 2 * i, True, t_const)
                yield
            hidden_holder[0] = None
            return last

        def context_kv(name, wk, kcol, wv, vcol, k_bias, v_bias, key_mask, src, src_t, w_t):
            parts_stored = []
            for c in range(CC):
                bank = work.take()
                n = B * LC
                t = pe.group([lambda e, k=k, c=c, bank=bank: e.matmul(
                    bank.ap[:, 0:n], wk[:, k, kcol + c * P:kcol + (c + 1) * P],
                    src[:, k, :, :].rearrange("p b l -> p (b l)"), start=k == 0, stop=k == CC - 1)
                    for k in range(CC)], src_t, w_t, bank.free)
                parts_stored.append(split_parts(
                    bank, t, n, 1.0, cols[:, k_bias + c:k_bias + c + 1] if k_bias is not None else 0.0,
                    kx_dram, K_RUNS, c, 0, free_dram=tuple(flat(kx_read))))
            ks, vs = [], []
            for b in range(B):
                sp.dma(ld_kx[b], kx_stack[b][0:ROWS, :, :], kx_dram[b].rearrange("(h d) r t -> (d r) h t", d=D),
                       parts_stored, kx_free[b])
                ks.append(ld_kx[b].all())
                kx_read.append(ks[-1])
                if key_mask is not None:
                    ks[-1] = (ks[-1], key_mask(b))
                elif kx_masked[0]:
                    ks[-1] = (ks[-1], po.do(lambda e, b=b: e.memset(kx_stack[b][BIAS_ROW:BIAS_ROW + 1, :, :], 0.0), kx_free[b]))
                bank = work.take()
                t = pe.group([lambda e, k=k, b=b, bank=bank: e.matmul(
                    bank.ap[0:LC, 0:C], src[:, k, b, :], wv[:, k, vcol:vcol + C], start=k == 0, stop=k == CC - 1)
                    for k in range(CC)], src_t, w_t, bank.free)
                ctx_reads.append(t)
                dst = Vx[b][:, :, 0:D]
                vin = bank.ap[0:LC, 0:C].rearrange("p (h d) -> p h d", h=H)
                if v_bias is None:
                    t = ve.do(lambda e, dst=dst, vin=vin: e.tensor_copy(dst, vin), t, kx_free[b], stacks_init)
                else:
                    bs = r_ring.take()
                    tb = sp.dma(ld_row[r_ring.slots.index(bs)], bs.ap[0:LC, 0:C], v_bias.partition_broadcast(LC), bs.free)
                    t = ve.do(lambda e, dst=dst, vin=vin, bs=bs: e.tensor_tensor(
                        dst, vin, bs.ap[0:LC, 0:C].rearrange("p (h d) -> p h d", h=H), ALU.add),
                        t, tb, kx_free[b], stacks_init)
                    bs.free = t
                bank.free = t
                vs.append((t, stacks_init))
            return ks, vs

        kx_free = [(), ()]
        kx_read, ctx_reads, kx_masked = [], [], [False]
        ctx_ready = {}
        wl = {n: l for n, l in ld_w.items()}

        def ctx_stage(name):
            if name == "L0":
                ctx_ready[name] = context_kv("L0", wt["L0kv"], 0, wt["L0kv"], C, COLS["L0_b_kv"], a["L0_b_kv"][C:2 * C],
                                             None, ctxT, const_t, wl["L0a"].all())
            elif name == "L2":
                def key_mask(b):
                    u8 = key_u8[:, b, :]
                    row = kx_row
                    t = ve.do(lambda e: e.tensor_scalar(row[:, :], u8, 1.0, -MASKED, ALU.subtract, ALU.mult),
                              const_t, km_free)
                    for h in range(H):
                        t2 = sp.dma(ld_kx[b], kx_stack[b][BIAS_ROW:BIAS_ROW + 1, h, :], row[:, :], t, kx_free[b])
                    km_free[:] = [t2]
                    return t2
                ctx_ready[name] = context_kv("L2", wt["L2k"], 0, wt["L2v"], 0, None, None, key_mask, ctxT, const_t,
                                             wl["L2a"].all())
                kx_masked[0] = True
            else:
                ts = []
                for b in range(B):
                    z = z_ring.take()
                    t = sp.dma(ld_ctx[b], z.ap[0:LC, :], a["ctx"][b], z.free)
                    s6, m2_ = stats[b], mv[b]
                    t = ve.do(lambda e, z=z, b=b: e.bn_stats(cst[b][:, 0:6], z.ap[0:LC, :]), t)
                    t = ve.do(lambda e, b=b: e.bn_aggr(cst[b][:, 6:8], cst[b][:, 0:6]), t)
                    t = ve.do(lambda e, b=b: e.tensor_scalar(cst[b][:, 8:9], cst[b][:, 7:8], 1e-6, None, ALU.add), t)
                    t = ac.do(lambda e, b=b: e.activation(cst[b][:, 8:9], cst[b][:, 8:9], ACT.Sqrt), t)
                    t = ve.do(lambda e, b=b: e.reciprocal(cst[b][:, 9:10], cst[b][:, 8:9]), t)
                    t = ve.do(lambda e, z=z, b=b: e.tensor_scalar(z.ap[0:LC, :], z.ap[0:LC, :], cst[b][:, 6:7],
                                                                  cst[b][:, 9:10], ALU.subtract, ALU.mult), t)
                    bank = work.take()
                    t = pe.group([lambda e, c=c, z=z, bank=bank: e.transpose(
                        bank.ap[:, c * LC:(c + 1) * LC], z.ap[0:LC, c * P:(c + 1) * P], ident[0:LC, 0:LC])
                        for c in range(CC)], t, bank.free)
                    z.free = t
                    t = ac.do(lambda e, b=b, bank=bank: e.activation(
                        ctxT[:, :, b, :], bank.ap[:, 0:CC * LC].rearrange("p (c l) -> p c l", c=CC), ACT.Copy),
                        t, ctx_reads)
                    bank.free = t
                    ts.append(t)
                ctx_ready[name] = context_kv("L3", wt["L3kv"], 0, wt["L3kv"], C, COLS["L3_b_kvc"], a["L3_b_kvc"][C:2 * C],
                                             None, ctxT, ts, wl["L3a"].all())

        key_u8 = sb("key_u8", [1, B, LC], U8)
        key_u8_t = sp.dma(ld_const, key_u8[:, :, :], a["mask_ctx"].rearrange("(o b) l -> o b l", o=1))
        const_t = ld_const.all()
        kx_row = sb("key_mask_row", [1, LC], BF16)
        km_free = []
        cst = [sb(f"ctx_stats{b}", [LC, 10]) for b in range(B)]
        ctx_left = {}

        def left_context(name, b, toks):
            kx_free[b] = tuple(flat(toks))
            ctx_left.setdefault(name, set()).add(b)

        holder = [None]

        def attention_stage(b, kind, mask, stored):
            while holder[0] not in (None, b):
                yield "wait"
            holder[0] = b
            out = yield from attention(b, kind, mask, stored)
            return out

        def self_attention(b, name, wa, bias_q, bias_k, v_bias, roll, rope, mask, h_tok, kind):
            while holder[0] not in (None, b):
                yield "wait"
            holder[0] = b
            w = wt[name + "qkv"]
            tb = None
            if v_bias is not None:
                tb = sp.dma(ld_tm[b], tmc[b][:, 1, :], v_bias.partition_broadcast(P), tm_free[b])
            v_t, last_v = yield from project_v(b, w, 2 * C, (h_tok, wl[name + "a"].all()), tb)
            if tb is not None:
                tm_free[b] = (tm_free[b], v_t)
            hw = (h_tok, wl[name + "a"].all(), quarter_t)
            last_k, k_stored = yield from project_parts(b, 1, w, C, 1.0, bias_k, hw, rope)
            last_q, q_stored = yield from project_parts(b, 0, w, 0, 0.25, bias_q, hw, rope)
            stored = {"q": q_stored, "k": k_stored, "v": (v_t, stacks_init), "h_free": (last_q,)}
            o = yield from attention(b, kind, mask, stored)
            v_slot.free = (pe.sem, pe.count)
            holder[0] = None
            return o

        tm_free = [(), ()]

        def cross_attention(b, name, bias_q, h_tok, kind):
            w = wt[name + "q"]
            hw = (h_tok, wl[name + "a"].all(), quarter_t)
            last_q, q_stored = yield from project_parts(b, 0, w, 0, 0.25, bias_q, hw)
            if name not in ctx_ready:
                prev = {"L2": "L0", "L3": "L2"}.get(name)
                while prev and len(ctx_left.get(prev, ())) < B:
                    yield "wait"
                if name not in ctx_ready:
                    ctx_stage(name)
            ks, vs = ctx_ready[name]
            while holder[0] not in (None, b):
                yield "wait"
            holder[0] = b
            stored = {"q": q_stored, "k": (ks[b], stacks_init), "v": vs[b], "h_free": (last_q,)}
            o = yield from attention(b, kind, False, stored)
            holder[0] = None
            left_context(name, b, (pe.sem, pe.count))
            return o

        def wait_loaded(n):
            while n not in loaded:
                yield "wait"

        def block(b, name, gates, shs, eps, self_bias, cross_bias, v_bias, out_biases, kind, roll, rope, mask, cross_kind,
                  func, gated_unit, plain_cross):
            def norm(i):
                sh, sc = shs[i]
                if sh is None:
                    return (lambda c: 1.0), (lambda c: 0.0)
                return mod_col(name, sc, b), mod_col(name, sh, b)
            hfree = (pe.sem, pe.count)

            def row_consts(i):
                g, bias = gates[i], out_biases[i]
                t = token_consts(b, (name, g) if g is not None else None, bias, None, tm_free[b])
                if bias is not None:
                    t = (t, pre_add(b, t, g is not None))
                return t
            yield from wait_loaded(name + "a") if name in ("L2", "L3") else ()
            sc, sh = norm(0)
            h_tok = yield from layer_norm(b, eps, sc, sh, (mod_done[name], h_last[b]), hT[b], roll=roll)
            if mask:
                yield from wait_loaded("mask")
                yield from wait_loaded("L2m")
            o = yield from self_attention(b, name, None, self_bias[0], self_bias[1], v_bias, roll, rope, mask, h_tok, kind)
            xread[b] = h_tok
            tc = row_consts(0)
            last = yield from out_project(b, wt[name + "so"], o, gates[0] is not None, tc, roll)
            tm_free[b] = tuple(flat((xtok[b], (ve.sem, ve.count), (po.sem, po.count))))
            sc, sh = norm(1)
            h_tok = yield from layer_norm(b, eps, sc, sh, (mod_done[name], last), hT[b])
            o = yield from cross_attention(b, name, cross_bias, h_tok, cross_kind)
            xread[b] = h_tok
            tc = row_consts(1)
            last = yield from out_project(b, wt[name + "co"], o, gates[1] is not None, tc, False)
            tm_free[b] = tuple(flat((xtok[b], (ve.sem, ve.count), (po.sem, po.count))))
            finished(name + "a", (pe.sem, pe.count)) if name == "L0" else None
            sc, sh = norm(2)
            h_tok = yield from layer_norm(b, eps, sc, sh, (mod_done[name], last), hT[b])
            yield from wait_loaded(name + "m")
            xread[b] = h_tok
            tc = row_consts(2)
            last = yield from mlp(b, name, (h_tok, wl[name + "m"].all()), func, gated_unit, tc)
            tm_free[b] = tuple(flat((xtok[b], (ve.sem, ve.count), (po.sem, po.count))))
            if name == "L0":
                finished("L0m", (pe.sem, pe.count))
            h_last[b] = (last,)

        h_last = [(), ()]
        small_free = [()]

        l1_ready = []

        def l1_context():
            wk, wv = wt["L1k"], wt["L1v"]
            for c in range(CC):
                bank = work.take()
                t = pe.group([lambda e, k=k, c=c, bank=bank: e.matmul(
                    bank.ap[:, 0:B * LC], wk[:, k, c * P:(c + 1) * P], ctxT[:, k, :, :].rearrange("p b l -> p (b l)"),
                    start=k == 0, stop=k == CC - 1) for k in range(CC)], const_t, wl["L1a"].all(), bank.free)
                t = ac.do(lambda e, c=c, bank=bank: e.activation(
                    kT1[:, c, :, :].rearrange("p b l -> p (b l)"), bank.ap[:, 0:B * LC], ACT.Copy), t)
                bank.free = t
                l1_ready.append(t)
            for b in range(B):
                bank = work.take()
                t = pe.group([lambda e, k=k, b=b, bank=bank: e.matmul(
                    bank.ap[0:LC, 0:C], ctxT[:, k, b, :], wv[:, k, :], start=k == 0, stop=k == CC - 1)
                    for k in range(CC)], bank.free)
                ctx_reads.append(t)
                t = ac.do(lambda e, b=b, bank=bank: e.activation(v1[b][:, :], bank.ap[0:LC, 0:C], ACT.Copy), t)
                bank.free = t
                l1_ready.append(t)

        def softmax_rows(b, src, n, w, t, scale, dst, scr):
            mx, sm = scr
            t1 = ve.do(lambda e: e.tensor_reduce(mx, src, AX_X, ALU.max), t, small_free[0])
            t2 = ve.do(lambda e: e.tensor_tensor(dst, src, mx.unsqueeze(2).to_broadcast([P, n, w]), ALU.subtract), t1,
                       small_free[0])
            t3 = ac.do(lambda e: e.activation(dst, dst, ACT.Exp, scale=scale), t2)
            t4 = ve.do(lambda e: e.tensor_reduce(sm, dst, AX_X, ALU.add), t3)
            t5 = ve.do(lambda e: e.reciprocal(sm, sm), t4)
            t6 = ve.do(lambda e: e.tensor_tensor(dst, dst, sm.unsqueeze(2).to_broadcast([P, n, w]), ALU.mult), t5)
            return t2, t6

        wrow = [sb("w_rows", [P, TPB, LC])] * B
        prow = [sb("p_rows", [P, TPB, E])] * B
        comb = [hT[b][:, :, :].rearrange("p c (h s) -> p (c h) s", h=2) for b in range(B)]

        def layer1(b):
            if not l1_ready:
                l1_context()
            sp.dma(ld_tm[b], tmc[b][:, 0, :], a["L1_gate_b2"].partition_broadcast(P), tm_free[b])
            tc = sp.dma(ld_tm[b], tmc[b][:, 1, :], a["L1_out_b"].partition_broadcast(P), tm_free[b])
            cg, cb = COLS["L1_gamma"], COLS["L1_beta"]
            wa, wm = wl["L1a"].all(), wl["L1m"].all()
            cm = comb[b]
            for bl in range(NB):
                nx = cm[:, 0:2, :]
                view = nx

                h_tok = yield from layer_norm1(b, bl, cm, cg, cb)
                xread[b] = h_tok
                yield from hold_hidden(b)
                qs = lhs_ring.take()
                qts = []
                for c in range(CC):
                    bank = work.take()
                    t = pe.group([lambda e, k=k, c=c, bank=bank: e.matmul(
                        bank.ap[:, :], wt["L1q"][:, k, c * P:(c + 1) * P], cm[:, k, :], start=k == 0, stop=k == CC - 1)
                        for k in range(CC)], h_tok, wa, bank.free, ns=840)
                    t = ac.do(lambda e, c=c, bank=bank: e.activation(qs.ap[:, c, :], bank.ap[:, :], ACT.Copy), t, qs.free)
                    bank.free = t
                    qts.append(t)
                bank = work.take()
                t = pe.group([lambda e, i=i, k=k, bank=bank: e.matmul(
                    bank.ap[:, i * LC:(i + 1) * LC], qs.ap[:, k, i * P:(i + 1) * P], kT1[:, k, b, :],
                    start=k == 0, stop=k == CC - 1) for i in range(TPB) for k in range(CC)], qts, l1_ready, bank.free)
                qs.free = t
                src = bank.ap[:, 0:TPB * LC].rearrange("p (i n) -> p i n", n=LC)
                rd, t = softmax_rows(b, src, TPB, LC, t, float(C) ** -0.5, wrow[b][:, :, :],
                                     (small[b][:, :, 0], small[b][:, :, 1]))
                bank.free = rd
                yield
                bank = work.take()
                t = pe.group([lambda e, i=i, bank=bank: e.transpose(
                    bank.ap[0:LC, i * P:(i + 1) * P], wrow[b][:, i, :], ident[:, :]) for i in range(TPB)], t, bank.free)
                wT = act_ring.take()
                t = ac.do(lambda e, bank=bank, wT=wT: e.activation(wT.ap[0:LC, :], bank.ap[0:LC, :], ACT.Copy), t, wT.free)
                bank.free = t
                ev = []
                for c in range(CC):
                    bank = work.take()
                    t2 = pe.do(lambda e, c=c, bank=bank, wT=wT: e.matmul(
                        bank.ap[:, :], v1[b][:, c * P:(c + 1) * P], wT.ap[0:LC, :], start=True, stop=True), t, bank.free)
                    wT.free = t2
                    t2 = ac.do(lambda e, c=c, bank=bank: e.activation(cm[:, CC + c, :], bank.ap[:, :], ACT.Copy), t2, h_last[b])
                    bank.free = t2
                    ev.append(t2)
                cmt = (h_tok, ev)
                yield
                bank = work.take()
                t = pe.group([lambda e, k=k, bank=bank: e.matmul(
                    bank.ap[0:E, :], wt["L1r"][:, k, :], cm[:, k, :], start=k == 0, stop=k == 3) for k in range(4)],
                    cmt, bank.free)
                lg = act_ring.take()
                t = ac.do(lambda e, bank=bank, lg=lg: e.activation(lg.ap[0:E, :], bank.ap[0:E, :], ACT.Identity,
                                                                   bias=anchor_r[:, b:b + 1]), t, mod_done["L1"], lg.free)
                bank.free = t
                bank = work.take()
                t = pe.group([lambda e, i=i, bank=bank: e.transpose(
                    bank.ap[:, i * E:(i + 1) * E], lg.ap[0:E, i * P:(i + 1) * P], ident[0:E, 0:E]) for i in range(TPB)],
                    t, bank.free)
                lg.free = t
                src = bank.ap[:, 0:TPB * E].rearrange("p (i n) -> p i n", n=E)
                rd, p_t = softmax_rows(b, src, TPB, E, t, 1.0, prow[b][:, :, :], (small[b][:, :, 2], small[b][:, :, 3]))
                bank.free = rd
                bank = work.take()
                t = pe.group([lambda e, i=i, bank=bank: e.transpose(
                    bank.ap[0:E, i * P:(i + 1) * P], prow[b][:, i, :], ident[:, :]) for i in range(TPB)], p_t, bank.free)
                pT = act_ring.take()
                t = ac.do(lambda e, bank=bank, pT=pT: e.activation(pT.ap[0:E, :], bank.ap[0:E, :], ACT.Copy), t, pT.free)
                bank.free = t
                rt = []
                for tp in range(0, TPB, 2):
                    bank = work.take()
                    t2 = pe.group([lambda e, i=i, tp=tp, bank=bank: e.matmul(
                        bank.ap[:, i * C:(i + 1) * C], pT.ap[0:E, (tp + i) * P:(tp + i + 1) * P], eb2[:, :],
                        start=True, stop=True) for i in range(2)], t, const_t, bank.free)
                    t2 = ac.do(lambda e, tp=tp, bank=bank: e.activation(
                        routed[b][:, tp:tp + 2, :], bank.ap[:, :].rearrange("p (t f) -> p t f", t=2), ACT.Copy),
                        t2, small_free[0])
                    pT.free = bank.free = t2
                    rt += [t2, t2]
                yield
                for ex in range(E):
                    accs = [acc_banks.take(), acc_banks.take()]
                    pend = None

                    def down(j, hid, t, ex=ex, accs=accs):
                        t = pe.group([lambda e, i=i, j=j, hid=hid: e.matmul(
                            accs[i // 2].ap[:, (i % 2) * C:(i % 2 + 1) * C], hid.ap[:, i * P:(i + 1) * P],
                            wt[f"L1w2_{ex}"][:, j, :], start=(j == 0 and i % 2 == 0), stop=j == RH // P - 1,
                            skip_group_check=True) for i in range(TPB)], t, wm,
                            accs[0].free if j == 0 else (), accs[1].free if j == 0 else (), ns=430)
                        hid.free = t
                        return t
                    for j in range(RH // P):
                        bank, hid = work.take(), hid_ring.take()
                        t = pe.group([lambda e, k=k, j=j, ex=ex, bank=bank: e.matmul(
                            bank.ap[:, :], wt[f"L1w1_{ex}"][:, k, j * P:(j + 1) * P], cm[:, k, :],
                            start=k == 0, stop=k == 3) for k in range(4)], cmt, wm, bank.free, ns=840)
                        t = ac.do(lambda e, j=j, ex=ex, bank=bank, hid=hid: e.activation(
                            hid.ap[:, :], bank.ap[:, :], ACT.Silu,
                            bias=anchor1[:, ex * (RH // P) + j, b:b + 1]), t, hid.free)
                        bank.free = t
                        if pend is not None:
                            down(*pend)
                        pend = (j, hid, t)
                        yield
                    t = down(*pend)
                    for i in range(TPB):
                        rt[i] = ve.do(lambda e, i=i, ex=ex, accs=accs: e.scalar_tensor_tensor(
                            out=routed[b][:, i, :], in0=accs[i // 2].ap[:, (i % 2) * C:(i % 2 + 1) * C],
                            scalar=prow[b][:, i, ex:ex + 1], in1=routed[b][:, i, :], op0=ALU.mult, op1=ALU.add),
                            t, rt[i], p_t)
                        accs[i // 2].free = rt[i]
                    yield
                gh = lhs_ring.take()
                gts = []
                for c in range(CC):
                    bank = work.take()
                    t = pe.group([lambda e, k=k, c=c, bank=bank: e.matmul(
                        bank.ap[:, :], wt["L1g1"][:, k, c * P:(c + 1) * P], cm[:, k, :], start=k == 0, stop=k == 3)
                        for k in range(4)], cmt, bank.free)
                    h_last[b] = (t,)
                    t = ac.do(lambda e, c=c, bank=bank: e.activation(
                        gh.ap[:, c, :], bank.ap[:, :], ACT.Silu, bias=anchor1[:, E * RH // P + c, b:b + 1]), t, gh.free)
                    bank.free = t
                    gts.append(t)
                rT = lhs_ring.take()
                rts = []
                for c in range(CC):
                    bank = work.take()
                    t = pe.group([lambda e, i=i, c=c, bank=bank: e.transpose(
                        bank.ap[:, i * P:(i + 1) * P], routed[b][:, i, c * P:(c + 1) * P], ident[:, :])
                        for i in range(TPB)], rt, bank.free)
                    small_free[0] = (t,)
                    t = ac.do(lambda e, c=c, bank=bank: e.activation(rT.ap[:, c, :], bank.ap[:, :], ACT.Copy), t, rT.free)
                    bank.free = t
                    rts.append(t)
                for tp in range(0, TPB, 2):
                    g_bank = work.take()
                    tg = pe.group([lambda e, i=i, k=k, tp=tp, bank=g_bank: e.matmul(
                        bank.ap[:, i * C:(i + 1) * C], gh.ap[:, k, (tp + i) * P:(tp + i + 1) * P], wt["L1g2"][:, k, :],
                        start=k == 0, stop=k == CC - 1) for i in range(2) for k in range(CC)], gts, g_bank.free)
                    y = y_ring.take()
                    for i in range(2):
                        t1 = ve.do(lambda e, i=i, y=y, bank=g_bank: e.tensor_tensor(
                            y.ap[:, i, :], bank.ap[:, i * C:(i + 1) * C], tmc[b][:, 0, :], ALU.add), tg, tc, y.free)
                    g_bank.free = t1
                    t1 = ac.do(lambda e, y=y: e.activation(y.ap[:, :, :], y.ap[:, :, :], ACT.Sigmoid), t1)
                    o_bank = work.take()
                    to = pe.group([lambda e, i=i, k=k, tp=tp, bank=o_bank: e.matmul(
                        bank.ap[:, i * C:(i + 1) * C], rT.ap[:, k, (tp + i) * P:(tp + i + 1) * P], wt["L1out"][:, k, :],
                        start=k == 0, stop=k == CC - 1) for i in range(2) for k in range(CC)], rts, o_bank.free)
                    r_ = r_ring.take()
                    for i in range(2):
                        t2 = ve.do(lambda e, i=i, r_=r_, bank=o_bank: e.tensor_tensor(
                            r_.ap[:, i * C:(i + 1) * C], bank.ap[:, i * C:(i + 1) * C], tmc[b][:, 1, :], ALU.add),
                            to, tc, r_.free)
                    o_bank.free = t2
                    y2 = y.ap[:, :, :].rearrange("p t f -> p (t f)")
                    t3 = ve.do(lambda e, r_=r_, y2=y2: e.tensor_tensor(y2, r_.ap[:, :], y2, ALU.mult), t1, t2)
                    r_.free = t3
                    tile = bl * TPB + tp
                    t4 = po.do(lambda e, tile=tile, y=y: e.tensor_tensor(
                        x[b][:, tile:tile + 2, :], x[b][:, tile:tile + 2, :], y.ap[:, :, :], ALU.add), t3, h_tok)
                    y.free = t4
                    xtok[b][tile] = xtok[b][tile + 1] = (t4,)
                gh.free = tg
                rT.free = to
                small_free[0] = (small_free[0], t, rt, p_t)
                hidden_holder[0] = None
                yield
            tm_free[b] = tuple(flat((t2, t1, (ve.sem, ve.count))))
            finished("L1a", (pe.sem, pe.count))
            finished("L1m", (pe.sem, pe.count))

        def layer_norm1(b, bl, cm, cg, cb):
            return (yield from layer_norm(b, 1e-5, lambda c: cols[:, cg + c:cg + c + 1],
                                          lambda c: cols[:, cb + c:cb + c + 1], (h_last[b],),
                                          Shifted(cm, bl * BLK), blk=bl))

        class Shifted:
            def __init__(self, ap, base):
                self.ap, self.base = ap, base

            def __getitem__(self, key):
                p, c, s = key
                return self.ap[p, c, s.start - self.base:s.stop - self.base]

        def stream(b):
            def q4(i):
                return lambda c: bq[:, i + c:i + c + 1]

            def col(name):
                return lambda c: cols[:, COLS[name] + c:COLS[name] + c + 1]

            def kcol(name):
                return lambda c: cols[:, COLS[name] + CC + c:COLS[name] + CC + c + 1]

            def zero(c):
                return 0.0
            yield from block(b, "L0", (2 * C, 5 * C, 8 * C), ((0, 2), (6, 8), (12, 14)), 1e-6,
                             (q4(0), kcol("L0_b_qkv")), q4(2), a["L0_b_qkv"][2 * C:3 * C],
                             (a["L0_b_so"], a["L0_b_co"], a["L0_b_m2"]), "window", True, False, False, "topk",
                             ACT.Silu, True, False)
            yield from layer1(b)
            yield from block(b, "L2", (2 * C, 5 * C, 8 * C), ((0, 2), (6, 8), (12, 14)), 1e-5,
                             (zero, zero), zero, None, (None, None, a["L2_mlp_b2"]), "full", False, True, True, "context",
                             ACT.Gelu_apprx_tanh, False, False)
            yield from block(b, "L3", (2 * C, None, 5 * C), ((0, 2), (None, None), (6, 8)), 1e-6,
                             (q4(4), kcol("L3_b_qkv")), q4(6), a["L3_b_qkv"][2 * C:3 * C],
                             (a["L3_b_proj"], a["L3_b_cproj"], a["L3_b_mlp2"]), "full", False, False, False, "context",
                             ACT.Gelu_apprx_tanh, False, True)
            sp.dma(st_out, out[b].rearrange("(t p) c -> p t c", p=P), x[b][:, :, :], xtok[b])

        streams = {b: stream(b) for b in range(B)}
        spent = {b: 0 for b in range(B)}
        stuck = 0
        while streams:
            b = min(streams, key=lambda s: (spent[s], s))
            before = pe.planned
            try:
                said = next(streams[b])
            except StopIteration:
                del streams[b]
                continue
            if said == "wait":
                stuck += 1
                assert stuck < 100, "both streams wait"
                others = [spent[s] for s in streams if s != b]
                spent[b] = max([spent[b]] + others) + 1
            else:
                stuck = 0
                spent[b] += max(1, pe.planned - before) + (said or 0)

        for l in [st_out, *st_mod.values()] + st_parts:
            sp._waits(l.all())


def kernel(**inputs):
    import concourse.bacc as bacc
    from concourse.bass_utils import run_bass_kernel_spmd

    raw = {k: np.asarray(v) for k, v in inputs.items()}

    def column(v):
        return v.reshape(-1, P).T

    names = {"L0": "L0_xcond_", "L1": "L1_xcond_", "L2": "L2_xcond_", "L3": "L3_xcond_"}
    arrays = {}
    for k, v in raw.items():
        for short, long in names.items():
            if k.startswith(long):
                arrays[short + "_" + k[len(long):]] = v
    cols = np.concatenate([column(arrays[n]) for n in (
        "L0_b_qkv", "L0_b_q", "L0_b_kv", "L0_b_m1", "L1_ln_gamma", "L1_ln_beta", "L2_norm1_w", "L2_normc_w",
        "L2_norm2_w", "L2_mlp_b1", "L3_b_qkv", "L3_b_qc", "L3_b_kvc", "L3_b_mlp1")], axis=1)
    cos, sin = rope_tables()
    arrays.update(
        x=raw["x"], ctx=raw["ctx_1024"], ctxT=raw["ctx_1024"].transpose(2, 0, 1), condT=raw["cond_1024"].T,
        mask_self=raw["mask_SxS_bk0"], mask_ctx=raw["mask_BxS2_bf1"],
        cols=cols, cos=cos, sin=sin, ident=np.eye(P, dtype=np.float32))
    for n in ("L0_b_q", "L0_b_m1", "L1_ln_gamma", "L1_ln_beta", "L2_norm1_w", "L2_normc_w", "L2_norm2_w", "L2_mlp_b1",
              "L3_b_qc", "L3_b_mlp1"):
        arrays.pop(n)
    arrays = {k: np.ascontiguousarray(v) for k, v in arrays.items()}

    nc = bacc.Bacc("TRN2", target_bir_lowering=False, num_devices=1, dynamic_dma_scratch_size=1024)
    aps = {k: nc.dram_tensor(f"in_{k}", v.shape, mybir.dt.from_np(v.dtype), kind="ExternalInput").ap()
           for k, v in arrays.items()}
    out = nc.dram_tensor("out_x", (B, S, C), F32, kind="ExternalOutput").ap()
    build_program(nc, aps, out)
    r = run_bass_kernel_spmd(nc, [{f"in_{k}": v for k, v in arrays.items()}], core_ids=[0])
    return r.results[0]["out_x"]
```

```python
from contextlib import ExitStack

import numpy as np

import concourse.bass as bass
from concourse import mybir

F32 = mybir.dt.float32
BF16 = mybir.dt.bfloat16
U8 = mybir.dt.uint8
I32 = mybir.dt.int32
ALU = mybir.AluOpType
ACT = mybir.ActivationFunctionType
AX_X = mybir.AxisListType.X

P = 128
B = 2
S = 1024
C = 256
CC = C // P
NT = S // P
H = 16
D = C // H
DV = D + 1
LC = 77
SHIFT = 64
HID = 1024
E = 3
RH = 512
BLK = 512
NB = S // BLK
TPB = BLK // P
PAIR = 2
GROUPS = H // PAIR
PARTS = 3
Q_RUNS = ((0, 3, 0, 1), (3, 2, 0, 1), (5, 1, 0, 0))
K_RUNS = ((0, 3, 0, 0), (3, 2, 1, 0), (5, 1, 2, 0))
PRODUCTS = 6
ROWS = PRODUCTS * D
BIAS_ROW = ROWS
MAX_ROW = ROWS + 1
STACK = MAX_ROW + 2
MASKED = -(2.0 ** 100)
TAKEN = -3.0e38
MAXIMA_LEAD = 2
HOLDER_LEAD = 2000.0
ROOT_GUESS = 0x5F3759DF
ADA = 9 * C
L3MOD = 6 * C


def rope_tables():
    inv = 1.0 / 10000.0 ** (np.arange(0, D, 2, dtype=np.float32) / D)
    f = np.outer(np.arange(S // 2, dtype=np.float32), inv)
    emb = np.concatenate([f, f], axis=-1)
    sign = np.where(np.arange(D) < D // 2, -1.0, 1.0).astype(np.float32)
    cos = np.tile(np.cos(emb).astype(np.float32).T, (P // D, 1))
    sin = np.tile((np.sin(emb).astype(np.float32) * sign).T, (P // D, 1))
    return np.ascontiguousarray(cos), np.ascontiguousarray(sin)


COLS = {}
_at = 0
for _name, _n in (("L0_b_qkv", 3 * C), ("L0_b_q", C), ("L0_b_kv", 2 * C), ("L0_b_m1", 2 * HID),
                  ("L1_gamma", C), ("L1_beta", C), ("L2_n1", C), ("L2_nc", C), ("L2_n2", C),
                  ("L2_b1", HID), ("L3_b_qkv", 3 * C), ("L3_b_qc", C), ("L3_b_kvc", 2 * C), ("L3_b1", HID)):
    COLS[_name] = _at
    _at += _n // P
N_COLS = _at


class Op:

    def __init__(self, queue, makes, after, lane=None):
        self.queue, self.makes, self.after, self.lane = queue, makes, tuple(flat(after)), lane
        self.start = self.end = 0.0
        self.sem = self.value = None


class Plan:

    def __init__(self):
        self.ops, self.stream, self.clock = [], None, 0.0

    def aside(self, name, queue, *args):
        stream = self.stream
        self.stream = (stream[0] if isinstance(stream, tuple) else stream, name)
        result = queue(*args)
        self.stream = stream
        return result

    def emit(self):
        for n, op in enumerate(self.ops):
            op.n = n
        for op in sorted(self.ops, key=lambda o: (o.start, o.n)):
            q = op.queue
            q.wait(op.after)
            if q.one_by_one and q.met.get(q.sem, 0) < q.count:
                q.met[q.sem] = q.count
                q.eng.wait_ge(q.sem, q.count)
            for make in op.makes:
                last = make(q.eng)
            if op.lane is None:
                q.count += 1
                last.then_inc(q.sem, 1)
                op.sem, op.value = q.sem, q.count
            else:
                op.lane.count += 16
                last.then_inc(op.lane.sem, 16)
                op.sem, op.value = op.lane.sem, op.lane.count


class Queue:
    HOP, SAME = 190.0, 75.0
    DMA_LATENCY, DMA_RATE = 2000.0, 150.0

    def __init__(self, eng, sem, plan, cost, one_by_one=False):
        self.one_by_one = one_by_one
        self.eng, self.sem, self.plan, self.cost = eng, sem, plan, cost
        self.count, self.met = 0, {}
        self.starts, self.ends = [], []
        self.latest = {}

    def place(self, op, ns, latency=0.0, floor=0.0):
        plan = self.plan
        ready = max([floor] + [o.end + (self.SAME if o.queue is self else self.HOP) for o in op.after])
        mine = self.latest.get(plan.stream)
        t = max(ready, mine.start + mine.ns if mine else 0.0)
        i, hi = 0, len(self.starts)
        while i < hi:
            mid = (i + hi) // 2
            i, hi = (mid + 1, hi) if self.starts[mid] <= t else (i, mid)
        if i and self.ends[i - 1] > t:
            t = self.ends[i - 1]
        while i < len(self.starts) and self.starts[i] < t + ns:
            t = self.ends[i]
            i += 1
        self.starts.insert(i, t)
        self.ends.insert(i, t + ns)
        op.start, op.ns, op.end = t, ns, t + ns + latency
        self.latest[plan.stream] = op
        plan.ops.append(op)
        if op.lane is None:
            plan.clock = max(plan.clock, t)
        return op

    def do(self, make, *after, ns=None):
        return self.place(Op(self, [make], after), ns or self.cost)

    def group(self, makes, *after, ns=None):
        return self.place(Op(self, list(makes), after), (ns or self.cost) * len(makes))

    def dma(self, lane, out, in_, *after):
        op = Op(self, [lambda e: e.dma_start(out, in_)], after, lane)
        size = 4.0
        for n in out.shape:
            size *= n
        floor = lane.last.start + lane.last.ns if lane.last is not None else 0.0
        lane.last = self.place(op, self.cost, self.DMA_LATENCY + size / self.DMA_RATE, floor)
        return op

    def so_far(self, b):
        return tuple(op for key, op in self.latest.items() if key == b or isinstance(key, tuple) and key[0] == b)

    def wait(self, after):
        need = {}
        for op in after:
            if self.met.get(op.sem, 0) < op.value:
                need[op.sem] = max(need.get(op.sem, 0), op.value)
        self.met.update(need)
        for s, v in need.items():
            self.eng.wait_ge(s, v)


class Lane:

    def __init__(self, sem):
        self.sem, self.count, self.last = sem, 0, None

    def all(self):
        return self.last


def flat(x):
    if x is None:
        return
    if isinstance(x, Op):
        yield x
        return
    for y in x:
        yield from flat(y)


class Slot:

    def __init__(self, ap):
        self.ap, self.readers, self.busy = ap, (), False

    @property
    def free(self):
        return self.readers

    @free.setter
    def free(self, toks):
        self.readers, self.busy = toks, False


class Ring:

    def __init__(self, aps):
        self.slots = [Slot(a) for a in aps]

    def take(self):
        s = min((s for s in self.slots if not s.busy), key=lambda s: max([o.end for o in flat(s.readers)], default=0.0))
        s.busy = True
        return s


def build_program(nc, a, out):
    with ExitStack() as ctx:
        def sb(name, shape, dt=F32):
            return ctx.enter_context(nc.sbuf_tensor(name, shape, dt))

        def sem(name):
            return ctx.enter_context(nc.semaphore(name))

        def lane(name):
            return Lane(sem(name))

        banks = [ctx.enter_context(nc.psum_tensor(f"bank{i}", [P, BLK], F32)) for i in range(8)]
        psum = Ring(banks)

        x = [sb(f"x{b}", [P, NT, C]) for b in range(B)]
        hT = [sb(f"hT{b}", [P, CC, S]) for b in range(B)]
        W = sb("weights", [P, 8192 + 15360])
        wX, wY, wC = W[:, 0:4096], W[:, 4096:8192], W[:, 8192:8192 + 15360]
        q_stack = [sb(f"q_stack{i}", [STACK, PAIR, S], BF16) for i in range(2)]
        k_stack = [sb(f"k_stack{i}", [P, PAIR, S], BF16) for i in range(2)]
        window_stacks = [wC[:, 6144 + 1024 * i:7168 + 1024 * i].bitcast(BF16).rearrange("p (h s) -> p h s", h=PAIR)
                         for i in range(6)]
        V_window1 = wC[:, 12288:12288 + NT * H * DV].rearrange("p (t h d) -> p t h d", t=NT, h=H)
        xq_stack0 = [wY[:, 1024 * i:1024 * (i + 1)].bitcast(BF16).rearrange("p (h s) -> p h s", h=PAIR) for i in range(2)]
        topk_room = [wY[:, 2048 + 1024 * i:3072 + 1024 * i] for i in range(2)]
        kx_stack = [sb(f"kx_stack{b}", [STACK, H, LC], BF16) for b in range(B)]
        V = sb("v", [P, NT, H, DV])
        Vx = [sb(f"v_context{b}", [LC, H, DV]) for b in range(B)]
        prob = Ring([sb(f"prob{i}", [P, BLK]) for i in range(6)])
        z_ring = Ring([sb(f"z{i}", [P, C]) for i in range(3)])
        t_ring = r_ring = Ring([sb(f"t{i}", [P, BLK]) for i in range(4)])
        part_ring = Ring([sb(f"parts{i}", [P, PARTS, BLK], BF16) for i in range(2)])
        hid_ring = Ring([sb(f"hidden{i}", [P, BLK]) for i in range(2)])
        act_ring = Ring([sb(f"gate_act{i}", [P, BLK]) for i in range(2)])
        lhs_ring = Ring([sb(f"lhs{i}", [P, CC, BLK]) for i in range(2)])
        y_ring = Ring([sb(f"y{i}", [P, 2, C]) for i in range(2)])
        tmc = [sb(f"row_consts{b}", [P, 2, C]) for b in range(B)]
        ident = sb("ident", [P, P])
        ident_b = sb("ident_b", [P, P], BF16)
        cols = sb("cols", [P, N_COLS])
        half_cols = sb("half_cols", [P, N_COLS])
        bq = sb("quarter_bias", [P, 8])
        ctxT = sb("ctxT", [P, CC, B, LC])
        condT, scondT = sb("condT", [P, CC, B]), sb("scondT", [P, CC, B])
        mod = {"L0": sb("mod0", [P, ADA // P, B]), "L2": sb("mod2", [P, ADA // P, B]),
               "L3": sb("mod3", [P, L3MOD // P, B])}
        anchor1 = sb("anchor1", [P, E * RH // P + 2, B])
        half_anchor = sb("half_anchor", [P, E * RH // P + 2, B])
        anchor_r = sb("anchor_r", [E, B])
        kT1 = wY[:, 3596:3596 + CC * B * LC].rearrange("p (c b l) -> p c b l", c=CC, b=B)
        v1 = [sb(f"v1_{b}", [LC, C]) for b in range(B)]
        eb2 = sb("e_b2", [E, C])
        stats = [sb(f"stats{b}", [P, NT, 6]) for b in range(B)]
        mv = [sb(f"mean_var{b}", [P, NT, 2]) for b in range(B)]
        rstd = [sb(f"rstd{b}", [P, NT]) for b in range(B)]
        newton = [sb(f"newton{b}", [P, 2, NT]) for b in range(B)]
        max2 = Ring([sb(f"max2_{i}", [P, PAIR * NT, NB]) for i in range(2)])
        max1 = Ring([sb(f"max1_{i}", [P, PAIR * NT]) for i in range(2)])
        max_parts = Ring([sb(f"max_parts{i}", [PAIR * NT, 2, P], BF16) for i in range(2)])
        top8 = Ring([sb(f"top{i}", [P, 4, 3, 8]) for i in range(2)])
        s_left = Ring([r[:, 0:8 * LC].rearrange("p (a i n) -> p a i n", a=2, i=4) for r in topk_room])
        s_exp = Ring([r[:, 8 * LC:12 * LC].rearrange("p (i n) -> p i n", i=4) for r in topk_room])
        den = Ring([sb(f"den{i}", [P, TPB, 2, PAIR]) for i in range(2)])
        small = [sb("small", [P, TPB, 8])] * B
        routed = [sb("routed", [P, TPB, C])] * B

        rows_dram = {n: nc.dram_tensor(f"mod_rows_{n}", [B, w], F32, kind="Internal").ap()
                     for n, w in (("L0", ADA), ("L2", ADA), ("L3", L3MOD))}
        qk_dram = [[nc.dram_tensor(f"parts_{n}{b}", [C, PRODUCTS, S], BF16, kind="Internal").ap() for n in "qk"]
                   for b in range(B)]
        kx_dram = [nc.dram_tensor(f"parts_kx{b}", [C, PRODUCTS, LC], BF16, kind="Internal").ap() for b in range(B)]

        plan = Plan()
        pe, ve, ac, po, sp = (Queue(eng, sem(f"{n}_done"), plan, cost, n == "pool") for eng, n, cost in (
            (nc.tensor, "tensor", 100.0), (nc.vector, "vector", 350.0), (nc.scalar, "scalar", 500.0),
            (nc.gpsimd, "pool", 1200.0), (nc.sync, "sync", 480.0)))

        ld_const, ld_cond = lane("ld_const"), lane("ld_cond")
        ld_x = [lane(f"ld_x{b}") for b in range(B)]
        ld_mod = [lane(f"ld_mod{i}") for i in range(3)]
        ld_mod_bias, st_mod = lane("ld_mod_bias"), lane("st_mod")
        ld_tm = [lane(f"ld_tm{b}") for b in range(B)]
        st_parts = [lane(f"st_parts{i}") for i in range(2)]
        ld_kx = [lane(f"ld_kx{b}") for b in range(B)]
        ld_q = [lane(f"ld_q{i}") for i in range(8)]
        ld_k = [lane(f"ld_k{i}") for i in range(6)]
        ld_m = [lane(f"ld_m{i}") for i in range(8)]
        ld_w = {n: lane(f"ld_w{n}") for n in ("L0a", "L0m", "L1a", "L1m", "L2a", "L2m", "L3a", "L3m", "mask", "rope")}
        ld_row = [lane(f"ld_row{i}") for i in range(4)]
        ld_ctx = [lane(f"ld_ctx{b}") for b in range(B)]
        st_out = lane("st_out")

        wt = {}
        cosT, sinT = wC[:, 4096:4608], wC[:, 4608:5120]

        def place(region, lane_name, items, after):
            at = 0
            for name, src in items:
                k, n = src.shape[0] // P, src.shape[1]
                dst = region[:, at:at + k * n].rearrange("p (c n) -> p c n", c=k)
                at += k * n
                sp.dma(ld_w[lane_name], dst, src.rearrange("(c p) n -> p c n", p=P), after)
                wt[name] = dst
            return at

        def load_L0a(after=()):
            place(wX, "L0a", [("L0qkv", a["L0_w_qkv"]), ("L0so", a["L0_w_so"]), ("L0q", a["L0_w_q"]),
                              ("L0kv", a["L0_w_kv"]), ("L0co", a["L0_w_co"])], after)

        def load_L0m(after=()):
            place(wC[:, 0:6144], "L0m", [("L0m1", a["L0_w_m1"]), ("L0m2", a["L0_w_m2"])], after)

        def load_L1a(after=()):
            place(wY, "L1a", [("L1q", a["L1_Wq"]), ("L1k", a["L1_Wk"]), ("L1v", a["L1_Wv"]),
                              ("L1g1", a["L1_gate_w1"][0:2 * C, :]), ("L1g2", a["L1_gate_w2"]),
                              ("L1out", a["L1_out_w"]), ("L1r", a["L1_router_W"][0:2 * C, :])], after)

        def load_L1m(after=()):
            n = 0
            for e in range(E):
                n += place(wC[:, 6144 + n:15360], "L1m", [(f"L1w1_{e}", a["L1_e_w1"][e, 0:2 * C, :])], after)
            for e in range(E):
                n += place(wC[:, 6144 + n:15360], "L1m", [(f"L1w2_{e}", a["L1_e_w2"][e])], after)

        def load_L2a(after=()):
            place(wX, "L2a", [("L2qkv", a["L2_qkv_W"]), ("L2so", a["L2_attn_out_W"]), ("L2q", a["L2_cq_W"]),
                              ("L2k", a["L2_ck_W"]), ("L2v", a["L2_cv_W"]), ("L2co", a["L2_co_W"])], after)

        def load_L2m(after=()):
            place(wC[:, 6144:10240], "L2m", [("L2m1", a["L2_mlp_W1"]), ("L2m2", a["L2_mlp_W2"])], after)

        def load_L3a(after=()):
            place(wY, "L3a", [("L3qkv", a["L3_W_qkv"]), ("L3so", a["L3_W_proj"]), ("L3q", a["L3_W_qc"]),
                              ("L3kv", a["L3_W_kvc"]), ("L3co", a["L3_W_cproj"])], after)

        def load_L3m(after=()):
            place(wC[:, 10240:14336], "L3m", [("L3m1", a["L3_W_mlp1"]), ("L3m2", a["L3_W_mlp2"])], after)

        mask_bias = wC[:, 0:4096].bitcast(BF16).rearrange("p (t k) -> p t k", t=NT)
        mask_u8 = wC[:, 4096:6144].bitcast(U8).rearrange("p (t k) -> p t k", t=NT)
        mask_ready = []

        def load_mask(after=()):
            t = sp.dma(ld_w["mask"], mask_u8, a["mask_self"].rearrange("(t p) k -> p t k", p=P), after)
            for i in range(NT):
                t2 = ve.do(lambda e, i=i: e.tensor_scalar(mask_bias[:, i, :], mask_u8[:, i, :], 1.0, -MASKED,
                                                          ALU.subtract, ALU.mult), t, after, ns=600)
            mask_ready.append(t2)
            sp.dma(ld_w["rope"], cosT, a["cos"], t2)
            sp.dma(ld_w["rope"], sinT, a["sin"], t2)

        def cross_stacks(after):
            x_rows["L2"] = x_rows["L3"] = [po.do(lambda e, i=i: e.memset(xq_stack[i][BIAS_ROW:BIAS_ROW + 1, :, :], 1.0), after)
                                           for i in range(2)]

        done_with, loaded = {}, {"L0a", "L0m"}
        NEXT = {"L0a": ("L2a", load_L2a), "L0m": ("mask", load_mask), "L0x": ("L1a", load_L1a), "L2parts": ("L2x", cross_stacks), "L1a": ("L2third", lambda after: third_pair("L2", after)),
                "L2self": ("L3a+L3third", lambda after: (load_L3a(after), third_pair("L3", after))),
                "L1m": ("L2m+L3m", lambda after: (load_L2m(after), load_L3m(after)))}

        def finished(region, *toks):
            done_with.setdefault(region, []).append(tuple(flat(toks)))
            if len(done_with[region]) == B:
                name, load = NEXT[region]
                load(tuple(flat(done_with[region])))
                loaded.update(name.split("+"))

        sp.dma(ld_cond, condT[:, :, :], a["condT"].rearrange("(c p) b -> p c b", p=P))
        sp.dma(ld_cond, ident[:, :], a["ident"])
        sp.dma(ld_cond, cols[:, :], a["cols"])
        for b in range(B):
            sp.dma(ld_x[b], x[b][:, :, :], a["x"][b].rearrange("(t p) c -> p t c", p=P))
        xtok = [[ld_x[b].all()] * NT for b in range(B)]
        ident_bt = ve.do(lambda e: e.tensor_copy(ident_b[:, :], ident[:, :]), ld_cond.all(), ns=3820)
        t = ac.do(lambda e: e.activation(scondT[:, :, :], condT[:, :, :], ACT.Tanh, scale=0.5), ld_cond.all(), ns=3800)
        t = ve.do(lambda e: e.tensor_scalar(scondT[:, :, :], scondT[:, :, :], 0.5, 0.5, ALU.mult, ALU.add), t, ns=70)
        silu_t = ve.do(lambda e: e.tensor_tensor(scondT[:, :, :], scondT[:, :, :], condT[:, :, :], ALU.mult), t, ns=75)
        half_t = ve.do(lambda e: e.tensor_scalar(half_cols[:, :], cols[:, :], 0.5, None, ALU.mult), ld_cond.all(), ns=100)
        ones = []
        ones.append(po.do(lambda e: e.memset(V[:, :, :, D:DV], 1.0), ns=660))
        for b in range(B):
            ones.append(po.do(lambda e, b=b: e.memset(Vx[b][:, :, D:DV], 1.0), ns=50))
            ones.append(po.do(lambda e, b=b: e.memset(kx_stack[b][BIAS_ROW:STACK, :, :], -1.0)))
            t = po.do(lambda e, b=b: e.memset(kx_stack[b][BIAS_ROW:BIAS_ROW + 1, :, :], 0.0), ones[-1])
            ones.append(t)
        for i in range(2):
            t = po.do(lambda e, i=i: e.memset(k_stack[i][BIAS_ROW:STACK, :, :], -1.0), ns=1740)
            ones.append(po.do(lambda e, i=i: e.memset(k_stack[i][BIAS_ROW:BIAS_ROW + 1, :, :], 0.0), t, ns=1740))
            ones.append(po.do(lambda e, i=i: e.memset(q_stack[i][BIAS_ROW:BIAS_ROW + 1, :, :], 1.0), ns=1740))
        window1_init = []
        for i in range(3):
            q, k = window_stacks[2 * i:2 * i + 2]
            window1_init.append(po.do(lambda e, q=q: e.memset(q[BIAS_ROW:BIAS_ROW + 1, :, :], 1.0)))
            t = po.do(lambda e, k=k: e.memset(k[BIAS_ROW:STACK, :, :], -1.0))
            window1_init.append(po.do(lambda e, k=k: e.memset(k[BIAS_ROW:BIAS_ROW + 1, :, :], 0.0), t))
        window1_init.append(po.do(lambda e: e.memset(V_window1[:, :, :, D:DV], 1.0)))
        stacks_init = tuple(ones)

        strips_zero = [ve.do(lambda e, i=i: e.memset(banks[i][:, :], 0.0), ns=540) for i in range(8)]
        for s_ in psum.slots:
            s_.free = strips_zero[psum.slots.index(s_)]

        x_rows = {}
        mod_w = Ring([wY[:, i * CC * BLK:(i + 1) * CC * BLK].rearrange("p (c n) -> p c n", c=CC) for i in range(3)])
        mod_bias, mod_row = Ring([wY[0:B, 3072:3584]]), Ring([wY[0:B, 3584:4096]])
        NORMS = {"L0": ((0, 2), (6, 8), (12, 14)), "L2": ((0, 2), (6, 8), (12, 14)), "L3": ((0, 2), (None, None), (6, 8))}
        mod_done, gates_stored = {}, {}

        def mod_piece(w, bias, k, dst, c0, lhs, rows):
            two, rs, bs = mod_w.take(), mod_row.take(), mod_bias.take()
            t = sp.dma(ld_mod[mod_w.slots.index(two)], two.ap[:, :, 0:k], w.rearrange("(c p) n -> p c n", p=P), two.free)
            tb = sp.dma(ld_mod_bias, bs.ap[:, 0:k], bias.partition_broadcast(B), bs.free)
            bank = psum.take()
            t = pe.group([lambda e, c=c, two=two, k=k, bank=bank, lhs=lhs: e.matmul(
                bank.ap[0:B, 0:k], lhs[:, c, :], two.ap[:, c, 0:k], start=c == 0, stop=c == CC - 1)
                for c in range(CC)], t, silu_t, ld_cond.all(), bank.free, ns=1390)
            two.free = t
            t = ve.do(lambda e, rs=rs, bs=bs, k=k, bank=bank: e.tensor_tensor(
                rs.ap[:, 0:k], bank.ap[0:B, 0:k], bs.ap[:, 0:k], ALU.add), t, tb, rs.free, ns=600)
            bank.free = bs.free = t
            return plan.aside("turn", mod_turn, k, dst, c0, rows, rs, t)

        def mod_turn(k, dst, c0, rows, rs, t):
            stored = sp.dma(st_mod, rows, rs.ap[:, 0:k], t) if rows is not None else ()
            bank = psum.take()
            m = max(1, k // P)
            kk = min(k, P)
            t = pe.group([lambda e, j=j, rs=rs, bank=bank, kk=kk: e.transpose(
                bank.ap[0:kk, 2 * j:2 * j + 2], rs.ap[:, j * P:j * P + kk], ident[0:B, 0:B])
                for j in range(m)], t, bank.free, ns=50)
            rs.free = (t, stored)
            src = bank.ap[0:kk, 0:2 * m]
            if c0 is None:
                t = ve.do(lambda e, dst=dst, src=src: e.tensor_copy(dst[:, :], src), t, ns=65)
            else:
                t = ve.do(lambda e, dst=dst, src=src, c0=c0, m=m: e.tensor_copy(
                    dst[:, c0:c0 + m, :], src.rearrange("p (m b) -> p m b", b=B)), t, ns=100)
            bank.free = t
            return t

        def modulation(n, w, bias, width, silu):
            todo = [i for i in range(3) if NORMS[n][i][0] is not None]
            for i in range(3):
                mod_done[n, i] = ()
            for c in range(0, width, BLK):
                k = min(BLK, width - c)
                t = mod_piece(a[w][:, c:c + k], a[bias][c:c + k], k, mod[n], c // P, scondT if silu else condT,
                              rows_dram[n][:, c:c + k])
                yield
                while todo and (NORMS[n][todo[0]][1] + CC) * P <= c + k:
                    i = todo.pop(0)
                    sc = NORMS[n][i][1]
                    t = ve.do(lambda e, sc=sc: e.tensor_scalar(mod[n][:, sc:sc + CC, :], mod[n][:, sc:sc + CC, :],
                                                               1.0, None, ALU.add), t, ns=100)
                    if n == "L2":
                        for c2 in range(CC):
                            col = COLS[("L2_n1", "L2_nc", "L2_n2")[i]] + c2
                            t = ve.do(lambda e, sc=sc, c2=c2, col=col: e.tensor_scalar(
                                mod[n][:, sc + c2, :], mod[n][:, sc + c2, :], cols[:, col:col + 1], None, ALU.mult), t,
                                ns=130)
                    mod_done[n, i] = t
            gates_stored[n] = st_mod.all()

        def anchor_stream():
            for ex in range(E):
                anchor_done.append(mod_piece(a["L1_e_w1"][ex, 2 * C:3 * C, :], a["L1_e_b1"][ex], RH, anchor1,
                                             ex * RH // P, condT, None))
                yield
            anchor_done.append(mod_piece(a["L1_gate_w1"][2 * C:3 * C, :], a["L1_gate_b1"], C, anchor1, E * RH // P, condT, None))
            anchor_done.append(mod_piece(a["L1_router_W"][2 * C:3 * C, :], a["L1_router_b"], E, anchor_r, None, condT, None))
            anchor_done.append(ve.do(lambda e: e.tensor_scalar(half_anchor[:, :, :], anchor1[:, :, :], 0.5, None, ALU.mult),
                                     anchor_done, ns=85))
            yield
            yield from modulation("L2", "L2_adaLN_W", "L2_adaLN_b", ADA, False)
            yield from modulation("L3", "L3_W_mod", "L3_b_mod", L3MOD, True)
            x_rows["L0"] = [po.do(lambda e, i=i: e.memset(xq_stack0[i][BIAS_ROW:BIAS_ROW + 1, :, :], 1.0),
                                  pe.so_far(plan.stream), ve.so_far(plan.stream), st_mod.all(), ns=1740) for i in range(2)]
        anchor_done = []

        def quarter(i, name, n):
            c = COLS[name]
            return ve.do(lambda e: e.tensor_scalar(bq[:, i:i + n], cols[:, c:c + n], 0.25, None, ALU.mult), ld_cond.all(), ns=70)

        for _ in modulation("L0", "L0_w_ada", "L0_b_ada", ADA, True):
            pass
        load_L0a()
        quarter_t = [quarter(0, "L0_b_qkv", 2), quarter(2, "L0_b_q", 2), quarter(4, "L3_b_qkv", 2), quarter(6, "L3_b_qc", 2)]
        sp.dma(ld_const, ctxT[:, :, :, :], a["ctxT"].rearrange("(c p) b l -> p c b l", p=P))
        sp.dma(ld_const, eb2[:, :], a["L1_e_b2"])
        load_L0m()
        const_t = ld_const.all()

        def inverse_root(y, room, var, eps, after):
            n = y.shape[1]
            p = y.shape[0]
            v, w = room[0:p, 0, 0:n], room[0:p, 1, 0:n]
            t = ve.do(lambda e: e.tensor_scalar(v, var, eps, None, ALU.add), after, ns=75)
            t = ve.do(lambda e: e.tensor_scalar(w.bitcast(I32), v.bitcast(I32), 1, None, ALU.logical_shift_right), t, ns=75)
            t = ve.do(lambda e: e.tensor_scalar(y.bitcast(I32), w.bitcast(I32), -1, ROOT_GUESS, ALU.mult, ALU.add), t, ns=75)
            for _ in range(4):
                t = ve.do(lambda e: e.tensor_tensor(w, y, y, ALU.mult), t, ns=75)
                t = ve.do(lambda e: e.tensor_tensor(w, w, v, ALU.mult), t, ns=75)
                t = ve.do(lambda e: e.tensor_scalar(w, w, -0.5, 1.5, ALU.mult, ALU.add), t, ns=75)
                t = ve.do(lambda e: e.tensor_tensor(y, y, w, ALU.mult), t, ns=75)
            return t

        def layer_norm(b, eps, scale, bias, after, dst, blk=None, roll=False):
            tiles = range(NT) if blk is None else range(blk * TPB, (blk + 1) * TPB)
            lo, hi = tiles[0], tiles[-1] + 1
            ts = []
            for t in tiles:
                s = ve.do(lambda e, t=t: e.bn_stats(stats[b][:, t, :], x[b][:, t, :]), xtok[b][t])
                ts.append(ve.do(lambda e, t=t: e.bn_aggr(mv[b][:, t, :], stats[b][:, t, :]), s, ns=75))
            rs = inverse_root(rstd[b][:, lo:hi], newton[b], mv[b][:, lo:hi, 1], eps, ts)
            yield
            out_t = []
            for bl in range(lo // TPB, hi // TPB):
                two = [psum.take(), psum.take()]
                for i in range(TPB):
                    z, t = z_ring.take(), bl * TPB + i
                    zt = ve.do(lambda e, z=z, t=t: e.tensor_scalar(
                        z.ap[:, :], x[b][:, t, :], mv[b][:, t, 0:1], rstd[b][:, t:t + 1],
                        ALU.subtract, ALU.mult), rs, z.free, ns=320)
                    pt = pe.group([lambda e, c=c, z=z, i=i, two=two: e.transpose(
                        two[c].ap[:, i * P:(i + 1) * P], z.ap[:, c * P:(c + 1) * P], ident[:, :])
                        for c in range(CC)], zt, two[0].free, two[1].free, ns=170)
                    z.free = pt
                for c in range(CC):
                    for src, to, n in dst_runs(bl, roll):
                        t = ac.do(lambda e, c=c, two=two, src=src, to=to, n=n: e.activation(
                            dst[:, c, to:to + n], two[c].ap[:, src:src + n], ACT.Identity,
                            scale=scale(c), bias=bias(c)), pt, after, ns=630)
                        out_t.append(t)
                    two[c].free = t
                yield
            return tuple(out_t)

        def dst_runs(bl, roll):
            if not roll:
                return [(0, bl * BLK, BLK)]
            if bl == 0:
                return [(0, S - SHIFT, SHIFT), (SHIFT, 0, BLK - SHIFT)]
            return [(0, bl * BLK - SHIFT, BLK)]

        def mod_col(n, s, b):
            return lambda c: mod[n][:, s + c, b:b + 1]

        def store_runs(lane_, dram, c, col0, parts, runs, *after):
            for row, n, part, step in runs:
                src = parts[:, part:part + n, :] if step else parts[:, part:part + 1, :].to_broadcast([P, n, parts.shape[2]])
                t = sp.dma(lane_, dram[c * P:(c + 1) * P, row:row + n, col0:col0 + parts.shape[2]], src, after)
            return t

        def split_parts(bank, t0, n, scale, bias, dram, runs, c, col0, rope=None, free_dram=()):
            t_, p_ = t_ring.take(), part_ring.take()
            lane_ = st_parts[part_ring.slots.index(p_)]
            tf, pf = t_.ap[:, 0:n], p_.ap
            bap = bank.ap[:, 0:n]
            t1 = ac.do(lambda e: e.activation(tf, bap, ACT.Identity, scale=scale, bias=bias), t0, t_.free)
            bank.free = t1
            if rope is not None:
                mask = [(i & 16) | ((i + 8) & 15) for i in range(32)]
                r_ = t_ring.take()
                rf = r_.ap[:, 0:n]
                s1 = ve.do(lambda e: e.stream_shuffle(rf, tf, mask), t1, r_.free, ns=600)
                s2 = ve.do(lambda e: e.tensor_tensor(rf, rf, sinT, ALU.mult), s1, ld_w["rope"].all(), ns=600)
                s3 = po.do(lambda e: e.tensor_tensor(tf, tf, cosT, ALU.mult), t1, s1, ld_w["rope"].all())
                t1 = ve.do(lambda e: e.tensor_tensor(tf, tf, rf, ALU.add), s2, s3, ns=600)
                r_.free = t1
                t2 = ve.do(lambda e: e.tensor_copy(pf[:, 0, 0:n], tf), t1, p_.free, ns=320)
            else:
                t2 = ac.do(lambda e: e.activation(pf[:, 0, 0:n], bap, ACT.Identity, scale=scale, bias=bias), p_.free)
                bank.free = t2
            t3 = ve.do(lambda e: e.tensor_tensor(tf, tf, pf[:, 0, 0:n], ALU.subtract), t1, t2, ns=570)
            t4 = ve.do(lambda e: e.tensor_copy(pf[:, 1, 0:n], tf), t3, ns=320)
            t5 = ve.do(lambda e: e.tensor_tensor(pf[:, 2, 0:n], tf, pf[:, 1, 0:n], ALU.subtract), t4, ns=570)
            t_.free = (t5,)
            if isinstance(dram, list):
                ts = [store_runs(lane_, dram[b], c, 0, pf[:, :, b * LC:(b + 1) * LC], runs, t2, t4, t5, free_dram)
                      for b in range(B)]
            else:
                ts = [store_runs(lane_, dram, c, col0, pf[:, :, 0:n], runs, t2, t4, t5, free_dram)]
            p_.free = ts[-1]
            return ts[-1]

        parts_read = [[(), ()] for _ in range(B)]

        def project_parts(b, which, w, col, scale, bias, h_tok, rope=False):
            last, parts_stored = (), []
            for c in range(CC):
                for bl in range(NB):
                    bank = psum.take()
                    t = pe.group([lambda e, k=k, c=c, bl=bl, bank=bank: e.matmul(
                        bank.ap[:, :], w[:, k, col + c * P:col + (c + 1) * P], hT[b][:, k, bl * BLK:(bl + 1) * BLK],
                        start=k == 0, stop=k == CC - 1) for k in range(CC)], h_tok, bank.free, ns=1000)
                    last = t
                    parts_stored.append(plan.aside("parts", split_parts, bank, t, BLK, scale, bias(c), qk_dram[b][which], (Q_RUNS, K_RUNS)[which], c, bl * BLK,
                                                    rope or None, parts_read[b][which]))
                    yield
            return last, tuple(parts_stored)

        v_slot, v_window1 = Slot(V), Slot(V_window1)

        def project_v(b, v_to, w, col, h_tok, bias_t):
            ts = []
            for tp in range(0, NT, 2):
                bank = psum.take()
                t = pe.group([lambda e, i=i, k=k, tp=tp, bank=bank: e.matmul(
                    bank.ap[:, i * C:(i + 1) * C], hT[b][:, k, (tp + i) * P:(tp + i + 1) * P],
                    w[:, k, col:col + C], start=k == 0, stop=k == CC - 1)
                    for i in range(2) for k in range(CC)], h_tok, bank.free, ns=530)
                src = bank.ap[:, :].rearrange("p (t h d) -> p t h d", t=2, h=H)
                dst = v_to.ap[:, tp:tp + 2, :, 0:D]
                if bias_t is None:
                    t2 = ve.do(lambda e, dst=dst, src=src: e.tensor_copy(dst, src), t, v_to.free, stacks_init, window1_init if v_to is v_window1 else (), ns=600)
                else:
                    bv = tmc[b][:, 1, :].rearrange("p (h d) -> p h d", h=H)
                    for i in range(2):
                        t2 = ve.do(lambda e, dst=dst, src=src, i=i, bv=bv: e.tensor_tensor(
                            dst[:, i], src[:, i], bv, ALU.add), t, v_to.free, stacks_init, window1_init if v_to is v_window1 else (), bias_t)
                bank.free = t2
                ts.append(t2)
                yield
            return (tuple(ts), t)

        def load_stack(dst, dram, h0, lane_, *after):
            rows = dram[h0 * D:(h0 + PAIR) * D, :, :].rearrange("(h d) r t -> (d r) h t", d=D)
            return sp.dma(lane_, dst[0:ROWS, :, :], rows, after)

        xq_stack = [wC[:, 4096 + 1024 * i:5120 + 1024 * i].bitcast(BF16).rearrange("p (h s) -> p h s", h=PAIR)
                    for i in range(2)]
        self_q, self_k = [Slot(t) for t in q_stack], [Slot(t) for t in k_stack]
        window_q, window_k = [Slot(t) for t in window_stacks[0::2]], [Slot(t) for t in window_stacks[1::2]]
        third = {n: [r[:, 1024 * i:1024 * (i + 1)].bitcast(BF16).rearrange("p (h s) -> p h s", h=PAIR) for i in range(2)]
                 for n, r in (("L2", wY), ("L3", wC))}
        third_slots = {n: [Slot(t) for t in pair] for n, pair in third.items()}

        def third_pair(n, after):
            q, k = third[n]
            third_slots[n][0].free = (po.do(lambda e: e.memset(q[BIAS_ROW:BIAS_ROW + 1, :, :], 1.0), after),)
            t = po.do(lambda e: e.memset(k[BIAS_ROW:STACK, :, :], -1.0), after)
            third_slots[n][1].free = (po.do(lambda e: e.memset(k[BIAS_ROW:BIAS_ROW + 1, :, :], 0.0), t),)

        cross_q = {"L0": [Slot(t) for t in xq_stack0], "L2": [Slot(t) for t in xq_stack]}
        cross_q["L3"] = cross_q["L2"]

        def attention(b, name, kind, mask, stored):
            out_view = hT[b][:, :, :].rearrange("p c (t f) -> p (c t) f", f=C)
            own_k = kind in ("window", "full")
            nk = P if own_k else LC
            own = kind == "window" and b == 1
            depth = 3 if own or kind == "full" and name + "third" in loaded else 2
            q_slots = (window_q if own else self_q[:]) if own_k else cross_q[name]
            k_slots = window_k if own else self_k[:]
            if kind == "full" and depth == 3:
                q_slots.append(third_slots[name][0])
                k_slots.append(third_slots[name][1])
            const_rows = (stacks_init, window1_init if own else ()) if own_k else x_rows[name][:]
            heads = range(PAIR)
            v_all = V_window1 if own else V if own_k else Vx[b]
            out_t = []

            def load(g):
                i = g % depth
                q, k = q_slots[i], k_slots[i] if own_k else None
                lane_q = (i + 5 if own else i) if own_k else i + 3
                lane_k = i + 3 if own else i
                tq = load_stack(q.ap, qk_dram[b][0], g * PAIR, ld_q[lane_q], stored["q"], q.free)
                parts_read[b][0] = (tq,)
                tk = ()
                if own_k:
                    tk = load_stack(k.ap, qk_dram[b][1], g * PAIR, ld_k[lane_k], stored["k"], k.free)
                    parts_read[b][1] = (tk,)
                else:
                    tk = stored["k"]
                return dict(g=g, m=ld_m[lane_q], q=q, k=k, t=(tq, tk, const_rows))

            def key_rows(st, h, rows, lo, n):
                if own_k:
                    return st["k"].ap[0:rows, h, lo:lo + n]
                return kx_stack[b][0:rows, st["g"] * PAIR + h, 0:LC]

            def max_pieces(st):
                m2 = max2.take() if kind == "full" else None
                m1 = max1.take()
                red = []
                if kind == "full":
                    for h in heads:
                        for qt in range(NT):
                            for half in range(NB):
                                bank = psum.take()
                                t = pe.do(lambda e, h=h, qt=qt, half=half, bank=bank: e.matmul(
                                    bank.ap[:, :], st["q"].ap[0:MAX_ROW, h, qt * P:(qt + 1) * P],
                                    st["k"].ap[0:MAX_ROW, h, half * BLK:(half + 1) * BLK], start=True, stop=True),
                                    st["t"], bank.free, ns=260)
                                to = m2.ap[:, h * NT + qt, half:half + 1]
                                if mask:
                                    t = ve.do(lambda e, bank=bank, qt=qt, half=half, to=to: e.tensor_tensor_reduce(
                                        bank.ap[:, :], bank.ap[:, :], mask_bias[:, qt, half * BLK:(half + 1) * BLK],
                                        1.0, -3.4e38, ALU.add, ALU.max, to), t, m2.free, mask_ready, ns=610)
                                else:
                                    t = ve.do(lambda e, bank=bank, to=to: e.tensor_reduce(
                                        to, bank.ap[:, :], AX_X, ALU.max), t, m2.free, ns=600)
                                bank.free = t
                                red.append(t)
                                yield
                    t = ve.do(lambda e: e.tensor_reduce(m1.ap[:, :], m2.ap[:, :, :], AX_X, ALU.max), red, m1.free, ns=100)
                    m2.free = t
                else:
                    per = 4
                    n = nk
                    for h in heads:
                        for q0 in range(0, NT, per):
                            bank = psum.take()
                            t = pe.group([lambda e, h=h, q0=q0, i=i, bank=bank, n=n: e.matmul(
                                bank.ap[:, i * n:(i + 1) * n], st["q"].ap[0:MAX_ROW, h, (q0 + i) * P:(q0 + i + 1) * P],
                                key_rows(st, h, MAX_ROW, (q0 + i) * P, P), start=True, stop=True)
                                for i in range(per)], st["t"], bank.free, ns=65)
                            t = ve.do(lambda e, h=h, q0=q0, bank=bank, n=n: e.tensor_reduce(
                                m1.ap[:, h * NT + q0:h * NT + q0 + per],
                                bank.ap[:, 0:per * n].rearrange("p (i n) -> p i n", n=n), AX_X, ALU.max), t, m1.free, ns=460)
                            bank.free = t
                            red.append(t)
                            yield
                    t = red
                plan.aside("rows", max_rows, st, m1, t)
                yield

            def max_rows(st, m1, t):
                bank, mp = psum.take(), max_parts.take()
                n = PAIR * NT
                t = pe.do(lambda e, bank=bank, n=n: e.transpose(bank.ap[0:n, 0:P], m1.ap[:, :], ident[:, :]), t, bank.free, ns=160)
                m1.free = t
                t1 = ve.do(lambda e, bank=bank, n=n: e.tensor_copy(mp.ap[:, 0, :], bank.ap[0:n, 0:P]), t, mp.free, ns=200)
                t2 = ve.do(lambda e, bank=bank, n=n: e.tensor_tensor(mp.ap[:, 1, :], bank.ap[0:n, 0:P], mp.ap[:, 0, :],
                                                     ALU.subtract), t1, ns=200)
                bank.free = t2
                rows = st["q"].ap
                for part in range(2):
                    sp.dma(st["m"], rows[MAX_ROW + part:MAX_ROW + part + 1, :, :].rearrange(
                        "r h (t q) -> r (h t) q", q=P), mp.ap[:, part, :], t2, st["q"].free)
                mp.free = st["m"].all()
                st["t"] = (st["t"], st["m"].all())

            def evac_exp(bank, t):
                p = prob.take()
                t = ac.do(lambda e: e.activation(p.ap[0:nk, :], bank.ap[0:nk, :], ACT.Exp), t, p.free)
                bank.free = t
                return p, t

            def pv(st, bank, kt, tiles, first, last):
                o, t = bank.ap, None
                for half, h, p, tp in tiles:
                    strip = (half * PAIR + h) * 32
                    head = st["g"] * PAIR + h
                    if kind == "window":
                        makes = [lambda e, i=i, half=half, head=head, strip=strip, p=p, o=o: e.matmul(
                            o[strip:strip + DV, i * P:(i + 1) * P], v_all[:, half * TPB + i, head, :],
                            p.ap[:, i * P:(i + 1) * P], start=True, stop=True, tile_position=(0, strip))
                            for i in range(TPB)]
                    else:
                        vv = v_all[:, kt, head, :] if own_k else v_all[:, head, :]
                        makes = [lambda e, vv=vv, strip=strip, p=p, o=o: e.matmul(
                            o[strip:strip + DV, :], vv, p.ap[0:nk, :], start=first, stop=last,
                            tile_position=(0, strip))]
                    t = pe.group(makes, tp, bank.free if first else (), stored["v"], ns=250 if kind != "window" else 110)
                    p.free = t
                return t

            def finish(st, pv_out_bank, t):
                pv_out = t_ring.take()
                t1 = ve.do(lambda e: e.tensor_copy(pv_out.ap[:, :], pv_out_bank.ap[:, :]), t, pv_out.free, strips_zero,
                           ns=600)
                pv_out_bank.free = t1
                bank = psum.take()
                t = pe.group([lambda e, i=i: e.transpose(bank.ap[:, i * P:(i + 1) * P],
                                                         pv_out.ap[:, i * P:(i + 1) * P], ident[:, :])
                              for i in range(TPB)], t1, bank.free, ns=160)
                pv_out.free = t
                d = den.take()
                v5 = bank.ap[:, :].rearrange("p (t a h d) -> p t a h d", t=TPB, a=2, h=PAIR)
                for half in range(2):
                    r = ve.do(lambda e, half=half: e.reciprocal(d.ap[:, :, half, :], v5[:, :, half, :, D]), t, d.free, ns=120)
                    to = out_view[:, half * TPB:(half + 1) * TPB, st["g"] * PAIR * D:(st["g"] + 1) * PAIR * D]
                    for h in heads:
                        dh = d.ap[:, :, half, h:h + 1].to_broadcast([P, TPB, D])
                        t2 = ve.do(lambda e, half=half, h=h, to=to, dh=dh: e.tensor_tensor(
                            to[:, :, h * D:(h + 1) * D], v5[:, :, half, h, 0:D], dh, ALU.mult), r, t, stored["h_free"], ns=140)
                        out_t.append(t2)
                bank.free = d.free = t2

            def main_pieces(st):
                kts = range(NT) if kind == "full" else range(1)

                def scores(kt, half):
                    tiles = []
                    for h in heads:
                        bank = psum.take()
                        if kind == "window":
                            makes = [lambda e, i=i, h=h, half=half, bank=bank: e.matmul(
                                bank.ap[:, i * P:(i + 1) * P],
                                st["k"].ap[0:STACK, h, (half * TPB + i) * P:(half * TPB + i + 1) * P],
                                st["q"].ap[0:STACK, h, (half * TPB + i) * P:(half * TPB + i + 1) * P],
                                start=True, stop=True) for i in range(TPB)]
                        else:
                            makes = [lambda e, h=h, half=half, bank=bank, kt=kt: e.matmul(
                                bank.ap[0:nk, :], key_rows(st, h, STACK, kt * P, P),
                                st["q"].ap[0:STACK, h, half * BLK:(half + 1) * BLK], start=True, stop=not mask)]
                            if mask:
                                makes += [lambda e, i=i, half=half, bank=bank, kt=kt: e.matmul(
                                    bank.ap[:, i * P:(i + 1) * P],
                                    mask_bias[:, half * TPB + i, kt * P:(kt + 1) * P], ident_b[:, :],
                                    start=False, stop=i == TPB - 1) for i in range(TPB)]
                        t = pe.group(makes, st["t"], bank.free, ident_bt, mask_ready if mask else (),
                                     ns=240 if len(makes) == 1 else 100 if mask else 95)
                        st["last"] = t
                        p, tp = evac_exp(bank, t)
                        tiles.append((half, h, p, tp))
                    return tiles

                pv_out = psum.take() if kind == "full" else None
                tiles = scores(0, 0)
                for kt in kts:
                    tiles += scores(kt, 1)
                    ahead = scores(kt + 1, 0) if kt + 1 < len(kts) else []
                    if pv_out is None:
                        pv_out = psum.take()
                    t = plan.aside("pv", pv, st, pv_out, kt, tiles, kt == 0, kt + 1 == len(kts))
                    tiles = ahead
                    if kt + 1 < len(kts):
                        yield
                st["q"].free = (st["last"],)
                if own_k:
                    st["k"].free = (st["last"],)
                plan.aside("pv", finish, st, pv_out, t)
                yield

            def topk_pieces(st):
                per = TPB

                def scores(half, h):
                    bank = psum.take()
                    t = pe.group([lambda e, h=h, half=half, i=i, bank=bank: e.matmul(
                        bank.ap[:, i * LC:(i + 1) * LC],
                        st["q"].ap[0:ROWS, h, (half * TPB + i) * P:(half * TPB + i + 1) * P],
                        kx_stack[b][0:ROWS, st["g"] * PAIR + h, :], start=True, stop=True)
                        for i in range(per)], st["t"], bank.free, ns=50)
                    st["last"] = t
                    return half, h, bank, t

                def keep_16(bank, t):
                    sc = bank.ap[:, 0:per * LC].rearrange("p (i n) -> p i n", n=LC)
                    top, left, ex = top8.take(), s_left.take(), s_exp.take()
                    a1 = [ve.do(lambda e, i=i, sc=sc, top=top: e.max(top.ap[:, i, 0, :], sc[:, i, :]), t, top.free,
                                x_rows["L0"], ns=148) for i in range(per)]
                    a2 = [ve.do(lambda e, i=i, sc=sc, top=top, left=left: e.match_replace(
                        out=left.ap[:, 0, i, :], in_to_replace=top.ap[:, i, 0, :], in_values=sc[:, i, :],
                        imm_value=TAKEN), a1[i], left.free, ns=160) for i in range(per)]
                    low = ve.do(lambda e, top=top: e.tensor_scalar(top.ap[:, :, 2, 0:1], top.ap[:, :, 0, 0:1], -1.0, None,
                                                                   ALU.mult), a1, ns=65)
                    xp = [ac.do(lambda e, i=i, sc=sc, top=top, ex=ex: e.activation(
                        ex.ap[:, i, :], sc[:, i, :], ACT.Exp, bias=top.ap[:, i, 2, 0:1]), low, ex.free, ns=210)
                        for i in range(per)]
                    bank.free = (xp[-1], a2[-1])
                    a3 = [ve.do(lambda e, i=i, top=top, left=left: e.max(
                        top.ap[:, i, 1, :], left.ap[:, 0, i, :]), a2[i], ns=148) for i in range(per)]
                    a4 = [ve.do(lambda e, i=i, top=top, left=left: e.match_replace(
                        out=left.ap[:, 1, i, :], in_to_replace=top.ap[:, i, 1, :], in_values=left.ap[:, 0, i, :],
                        imm_value=TAKEN), a3[i], ns=160) for i in range(per)]
                    top.free = (a4[-1], xp[-1])
                    keep = ve.do(lambda e, ex=ex, left=left: e.scalar_tensor_tensor(
                        out=ex.ap[:, :, :], in0=left.ap[:, 1, :, :], scalar=TAKEN, in1=ex.ap[:, :, :],
                        op0=ALU.is_equal, op1=ALU.mult), a4, xp, ns=400)
                    left.free = keep
                    return ex, keep

                def turn(ex, keep):
                    bank, p = psum.take(), prob.take()
                    t = pe.group([lambda e, i=i, ex=ex, bank=bank: e.transpose(
                        bank.ap[0:LC, i * P:(i + 1) * P], ex.ap[:, i, :], ident[:, :])
                        for i in range(per)], keep, bank.free, ns=180)
                    ex.free = t
                    t = ac.do(lambda e, bank=bank, p=p: e.activation(p.ap[0:LC, :], bank.ap[0:LC, :], ACT.Copy),
                              t, p.free)
                    bank.free = t
                    return p, t

                order = [(half, h) for half in range(2) for h in heads]
                tiles, cur = [], scores(*order[0])
                for n, (half, h) in enumerate(order):
                    nxt = scores(*order[n + 1]) if n + 1 < len(order) else None
                    ex, keep = keep_16(*cur[2:])
                    if nxt is None:
                        st["q"].free = (st["last"],)
                    tiles.append((half, h) + plan.aside("pv", turn, ex, keep))
                    cur = nxt
                    if n < 2:
                        yield
                pv_out = psum.take()
                t = plan.aside("pv", pv, st, pv_out, 0, tiles, True, True)
                plan.aside("pv", finish, st, pv_out, t)
                yield

            stacks = []

            def all_maxima():
                for g in range(GROUPS):
                    yield from max_pieces(stacks[g])

            maxima, made = all_maxima(), 0
            per_group = PAIR * NT * NB + 1 if kind == "full" else PAIR * NB + 1

            def maxima_to(n):
                nonlocal made
                while kind != "topk" and made < min(n, per_group * len(stacks)):
                    plan.stream = (b, "maxima")
                    next(maxima)
                    plan.stream = b
                    made += 1
                    yield

            for g in range(depth - 1):
                stacks.append(load(g))
            yield from maxima_to(per_group)
            for g in range(GROUPS):
                if g + depth - 1 < GROUPS:
                    stacks.append(load(g + depth - 1))
                if kind == "full":
                    yield from maxima_to(per_group * (g + 1))
                    for k, _ in enumerate(main_pieces(stacks[g])):
                        for _ in maxima_to(per_group * (g + 1 + (k + 1 + MAXIMA_LEAD) / NT)):
                            pass
                        yield
                else:
                    yield from maxima_to(per_group * (g + 2))
                    yield from (topk_pieces if kind == "topk" else main_pieces)(stacks[g])
            return tuple(out_t)

        def token_consts(b, gate, bias, last=()):
            if gate is not None:
                sp.dma(ld_tm[b], tmc[b][:, 0, :], rows_dram[gate[0]][b, gate[1]:gate[1] + C].partition_broadcast(P),
                       last, gates_stored[gate[0]])
            if bias is not None:
                sp.dma(ld_tm[b], tmc[b][:, 1, :], bias.partition_broadcast(P), last)
            return ld_tm[b].all()

        def pre_add(b, t_const, gated, tiles=range(0, NT, 2)):
            row = tmc[b][:, 1:2, :]
            if gated:
                t_const = (t_const, po.do(lambda e: e.tensor_tensor(tmc[b][:, 1, :], tmc[b][:, 1, :], tmc[b][:, 0, :],
                                                                    ALU.mult), t_const, ns=690))
            for tp in tiles:
                for i in range(2):
                    t = po.do(lambda e, tp=tp, i=i: e.tensor_tensor(x[b][:, tp + i, :], x[b][:, tp + i, :],
                                                                    row[:, 0, :], ALU.add),
                              t_const, xtok[b][tp + i], xread[b], ns=690)
                    xtok[b][tp + i] = (xtok[b][tp + i], t)
            return t

        xread = [() for _ in range(B)]

        def add_to_x(b, bank, t, tp, gated, t_const):
            src = bank.ap[:, :].rearrange("p (t f) -> p t f", t=2)
            if not gated:
                t = ve.do(lambda e: e.tensor_tensor(x[b][:, tp:tp + 2, :], x[b][:, tp:tp + 2, :], src, ALU.add),
                          t, xtok[b][tp], xtok[b][tp + 1], xread[b], ns=600)
                bank.free = t
            else:
                y = y_ring.take()
                for i in range(2):
                    t1 = ve.do(lambda e, i=i: e.tensor_tensor(y.ap[:, i, :], src[:, i, :], tmc[b][:, 0, :], ALU.mult),
                               t, t_const, y.free)
                bank.free = t1
                t = po.do(lambda e: e.tensor_tensor(x[b][:, tp:tp + 2, :], x[b][:, tp:tp + 2, :], y.ap[:, :, :],
                                                    ALU.add), t1, xtok[b][tp], xtok[b][tp + 1], xread[b])
                y.free = t
            xtok[b][tp] = xtok[b][tp + 1] = (t,)
            return t

        def out_project(b, w, o_tok, gated, t_const, roll):
            o_view = hT[b][:, :, :].rearrange("p c (t f) -> p (c t) f", f=C)
            last = ()
            pend = []
            for bl in range(NB):
                banks_, lhs = [psum.take(), psum.take()], lhs_ring.take()
                for c in range(CC):
                    makes = []
                    if not roll:
                        for i in range(TPB):
                            makes.append(lambda e, i=i, c=c, bl=bl, bank=banks_[c]: e.transpose(
                                bank.ap[:, i * P:(i + 1) * P], o_view[:, bl * TPB + i, c * P:(c + 1) * P], ident[:, :]))
                    else:
                        for i in range(TPB):
                            r = bl * TPB + i
                            makes.append(lambda e, i=i, c=c, r=r, bank=banks_[c]: e.transpose(
                                bank.ap[:, i * P:(i + 1) * P], o_view[:, r, c * P:(c + 1) * P], ident[:, :]))
                    t = pe.group(makes, o_tok, banks_[c].free)
                    last = t
                    t = ac.do(lambda e, c=c, lhs=lhs, bank=banks_[c]: e.activation(lhs.ap[:, c, :], bank.ap[:, :], ACT.Copy),
                              t, lhs.free)
                    banks_[c].free = t
                    pend.append(t)
                if not roll:
                    for tp in range(0, TPB, 2):
                        t = project_pair(b, w, [[(lhs, (tp + i) * P, P, 0)] for i in range(2)], bl * TPB + tp, pend, gated, t_const)
                    lhs.free = t
                    yield
                else:
                    if bl == 0:
                        first = lhs
                        continue
                    def where(tok):
                        r = (tok - SHIFT) % S
                        return (first if r < BLK else lhs), r % BLK
                    for tp in range(0, NT, 2):
                        srcs = []
                        for i in range(2):
                            s0, s1 = where((tp + i) * P), where((tp + i) * P + SHIFT)
                            srcs.append([(s0[0], s0[1], SHIFT, 0), (s1[0], s1[1], SHIFT, SHIFT)])
                        t = project_pair(b, w, srcs, tp, pend, gated, t_const)
                    first.free = lhs.free = t
            return last

        def project_pair(b, w, srcs, tile, after, gated, t_const):
            bank = psum.take()
            makes = []
            for i, runs in enumerate(srcs):
                for buf, col, n, row in runs:
                    for k in range(CC):
                        makes.append(lambda e, i=i, k=k, buf=buf, col=col, n=n, row=row, bank=bank: e.matmul(
                            bank.ap[row:row + n, i * C:(i + 1) * C], buf.ap[:, k, col:col + n], w[:, k, :],
                            start=k == 0, stop=k == CC - 1))
            t = pe.group(makes, after, bank.free, ns=430)
            plan.aside("add", add_to_x, b, bank, t, tile, gated, t_const)
            return t

        hidden_holder = [None]

        def hold_hidden(b):
            while hidden_holder[0] not in (None, b):
                yield "wait"
            hidden_holder[0] = b

        def silu(bank, hid, half_bias, *after):
            act = act_ring.take()
            t1 = ac.do(lambda e: e.activation(act.ap[:, :], bank.ap[:, :], ACT.Tanh, scale=0.5, bias=half_bias), after,
                       act.free, ns=571)
            t2 = ac.do(lambda e: e.activation(hid.ap[:, :], bank.ap[:, :], ACT.Identity, scale=0.5, bias=half_bias),
                       hid.free, ns=571)
            bank.free = t2
            t = ve.do(lambda e: e.scalar_tensor_tensor(out=hid.ap[:, :], in0=act.ap[:, :], scalar=1.0, in1=hid.ap[:, :],
                                                       op0=ALU.add, op1=ALU.mult), t1, t2, ns=600)
            act.free = t
            return t

        def gelu(bank, hid, bias, half_bias, *after):
            act = act_ring.take()
            t1 = ac.do(lambda e: e.activation(act.ap[:, :], bank.ap[:, :], ACT.Square, bias=bias), after, act.free, ns=571)
            t2 = ac.do(lambda e: e.activation(hid.ap[:, :], bank.ap[:, :], ACT.Identity, scale=0.5, bias=half_bias),
                       hid.free, ns=571)
            bank.free = t2
            t = ve.do(lambda e: e.tensor_scalar(act.ap[:, :], act.ap[:, :], 2 * 0.044715, 2.0, ALU.mult, ALU.add), t1, ns=350)
            t = ve.do(lambda e: e.tensor_tensor(act.ap[:, :], act.ap[:, :], hid.ap[:, :], ALU.mult), t, t2, ns=600)
            t = ac.do(lambda e: e.activation(act.ap[:, :], act.ap[:, :], ACT.Tanh, scale=float(np.sqrt(2 / np.pi))), t)
            t = ve.do(lambda e: e.scalar_tensor_tensor(out=hid.ap[:, :], in0=act.ap[:, :], scalar=1.0, in1=hid.ap[:, :],
                                                       op0=ALU.add, op1=ALU.mult), t, ns=600)
            act.free = t
            return t

        def mlp(b, name, h_tok, gated_unit, t_const):
            yield from hold_hidden(b)
            w1, w2 = wt[name + "m1"], wt[name + "m2"]
            c1 = COLS[{"L0": "L0_b_m1", "L2": "L2_b1", "L3": "L3_b1"}[name]]
            last = ()
            for bl in range(NB):
                accs = [psum.take(), psum.take()]
                pend = None

                def down(j, hid, t):
                    makes = [lambda e, i=i, j=j, hid=hid, accs=accs: e.matmul(
                        accs[i // 2].ap[:, (i % 2) * C:(i % 2 + 1) * C], hid.ap[:, i * P:(i + 1) * P], w2[:, j, :],
                        start=(j == 0 and i % 2 == 0), stop=j == HID // P - 1, skip_group_check=True)
                        for i in range(TPB)]
                    t = pe.group(makes, t, accs[0].free if j == 0 else (), accs[1].free if j == 0 else (), ns=430)
                    hid.free = t
                    return t

                for j in range(HID // P):
                    ups = []
                    for part in ((0, HID) if gated_unit else (0,)):
                        bank = psum.take()
                        t = pe.group([lambda e, k=k, j=j, part=part, bank=bank, bl=bl: e.matmul(
                            bank.ap[:, :], w1[:, k, part + j * P:part + (j + 1) * P], hT[b][:, k, bl * BLK:(bl + 1) * BLK],
                            start=k == 0, stop=k == CC - 1) for k in range(CC)], h_tok, bank.free, ns=940)
                        ups.append((bank, t))
                    hid = hid_ring.take()
                    bank, t = ups[0]
                    if gated_unit:
                        t = silu(bank, hid, half_cols[:, c1 + j:c1 + j + 1], t, half_t)
                        bank2, t2 = ups[1]
                        t = ve.do(lambda e, j=j, bank2=bank2, hid=hid: e.scalar_tensor_tensor(
                            out=hid.ap[:, :], in0=bank2.ap[:, :], scalar=cols[:, c1 + 8 + j:c1 + 9 + j],
                            in1=hid.ap[:, :], op0=ALU.add, op1=ALU.mult), t, t2, ns=663)
                        bank2.free = t
                    else:
                        t = gelu(bank, hid, cols[:, c1 + j:c1 + j + 1], half_cols[:, c1 + j:c1 + j + 1], t, half_t)
                    if pend is not None:
                        plan.aside("down", down, *pend)
                    pend = (j, hid, t)
                    yield
                last = plan.aside("down", down, *pend)
                for i in range(2):
                    plan.aside("add", add_to_x, b, accs[i], last, bl * TPB + 2 * i, True, t_const)
                yield
            hidden_holder[0] = None
            return last

        def context_kv(wk, kcol, wv, vcol, k_bias, v_bias, key_mask, src, src_t, w_t):
            parts_stored = []
            for c in range(CC):
                bank = psum.take()
                n = B * LC
                t = pe.group([lambda e, k=k, c=c, bank=bank, n=n: e.matmul(
                    bank.ap[:, 0:n], wk[:, k, kcol + c * P:kcol + (c + 1) * P],
                    src[:, k, :, :].rearrange("p b l -> p (b l)"), start=k == 0, stop=k == CC - 1)
                    for k in range(CC)], src_t, w_t, bank.free, ns=340)
                parts_stored.append(split_parts(
                    bank, t, n, 1.0, cols[:, k_bias + c:k_bias + c + 1] if k_bias is not None else 0.0,
                    kx_dram, K_RUNS, c, 0, free_dram=tuple(flat(kx_read))))
            ks, vs = [], []
            for b in range(B):
                sp.dma(ld_kx[b], kx_stack[b][0:ROWS, :, :], kx_dram[b].rearrange("(h d) r t -> (d r) h t", d=D),
                       parts_stored, kx_free[b])
                ks.append(ld_kx[b].all())
                kx_read.append(ks[-1])
                if key_mask is not None:
                    ks[-1] = (ks[-1], key_mask(b))
                elif kx_masked[0]:
                    ks[-1] = (ks[-1], po.do(lambda e, b=b: e.memset(kx_stack[b][BIAS_ROW:BIAS_ROW + 1, :, :], 0.0), kx_free[b]))
                bank = psum.take()
                t = pe.group([lambda e, k=k, b=b, bank=bank: e.matmul(
                    bank.ap[0:LC, 0:C], src[:, k, b, :], wv[:, k, vcol:vcol + C], start=k == 0, stop=k == CC - 1)
                    for k in range(CC)], src_t, w_t, bank.free, ns=500)
                ctx_reads.append(t)
                dst = Vx[b][:, :, 0:D]
                vin = bank.ap[0:LC, 0:C].rearrange("p (h d) -> p h d", h=H)
                if v_bias is None:
                    t = ve.do(lambda e, dst=dst, vin=vin: e.tensor_copy(dst, vin), t, kx_free[b], stacks_init)
                else:
                    bs = r_ring.take()
                    tb = sp.dma(ld_row[r_ring.slots.index(bs)], bs.ap[0:LC, 0:C], v_bias.partition_broadcast(LC), bs.free)
                    t = ve.do(lambda e, dst=dst, vin=vin, bs=bs: e.tensor_tensor(
                        dst, vin, bs.ap[0:LC, 0:C].rearrange("p (h d) -> p h d", h=H), ALU.add),
                        t, tb, kx_free[b], stacks_init)
                    bs.free = t
                bank.free = t
                vs.append((t, stacks_init))
            return ks, vs

        kx_free = [(), ()]
        kx_read, ctx_reads, kx_masked = [], [], [False]
        ctx_ready = {}
        wl = {n: l for n, l in ld_w.items()}

        def ctx_stage(name):
            if name == "L0":
                ctx_ready[name] = context_kv(wt["L0kv"], 0, wt["L0kv"], C, COLS["L0_b_kv"], a["L0_b_kv"][C:2 * C],
                                             None, ctxT, const_t, wl["L0a"].all())
            elif name == "L2":
                def key_mask(b):
                    u8 = key_u8[:, b, :]
                    row = kx_row
                    t = ve.do(lambda e: e.tensor_scalar(row[:, :], u8, 1.0, -MASKED, ALU.subtract, ALU.mult),
                              const_t, km_free, ns=110)
                    for h in range(H):
                        t2 = sp.dma(ld_kx[b], kx_stack[b][BIAS_ROW:BIAS_ROW + 1, h, :], row[:, :], t, kx_free[b])
                    km_free[:] = [t2]
                    return t2
                ctx_ready[name] = context_kv(wt["L2k"], 0, wt["L2v"], 0, None, None, key_mask, ctxT, const_t,
                                             wl["L2a"].all())
                kx_masked[0] = True
            else:
                ts = []
                for b in range(B):
                    z = z_ring.take()
                    t = sp.dma(ld_ctx[b], z.ap[0:LC, :], a["ctx"][b], z.free)
                    t = ve.do(lambda e, z=z, b=b: e.bn_stats(cst[b][:, 0:6], z.ap[0:LC, :]), t)
                    t = ve.do(lambda e, b=b: e.bn_aggr(cst[b][:, 6:8], cst[b][:, 0:6]), t, ns=75)
                    t = inverse_root(cst[b][:, 9:10], newton_ctx, cst[b][:, 7:8], 1e-6, t)
                    t = ve.do(lambda e, z=z, b=b: e.tensor_scalar(z.ap[0:LC, :], z.ap[0:LC, :], cst[b][:, 6:7],
                                                                  cst[b][:, 9:10], ALU.subtract, ALU.mult), t)
                    bank = psum.take()
                    t = pe.group([lambda e, c=c, z=z, bank=bank: e.transpose(
                        bank.ap[:, c * LC:(c + 1) * LC], z.ap[0:LC, c * P:(c + 1) * P], ident[0:LC, 0:LC])
                        for c in range(CC)], t, bank.free)
                    z.free = t
                    t = ac.do(lambda e, b=b, bank=bank: e.activation(
                        ctxT[:, :, b, :], bank.ap[:, 0:CC * LC].rearrange("p (c l) -> p c l", c=CC), ACT.Copy),
                        t, ctx_reads, ns=180)
                    bank.free = t
                    ts.append(t)
                ctx_ready[name] = context_kv(wt["L3kv"], 0, wt["L3kv"], C, COLS["L3_b_kvc"], a["L3_b_kvc"][C:2 * C],
                                             None, ctxT, ts, wl["L3a"].all())

        key_u8 = sb("key_u8", [1, B, LC], U8)
        sp.dma(ld_const, key_u8[:, :, :], a["mask_ctx"].rearrange("(o b) l -> o b l", o=1))
        const_t = ld_const.all()
        kx_row = sb("key_mask_row", [1, LC], BF16)
        km_free = []
        cst = [sb(f"ctx_stats{b}", [LC, 10]) for b in range(B)]
        newton_ctx = sb("newton_ctx", [P, 2, 1])
        ctx_left = {}

        def left_context(name, b, toks):
            kx_free[b] = tuple(flat(toks))
            ctx_left.setdefault(name, set()).add(b)

        holder, cross_holder = [None], [None]

        def self_attention(b, name, bias_q, bias_k, v_bias, rope, mask, h_tok, kind):
            w = wt[name + "qkv"]
            hw = (h_tok, wl[name + "a"].all(), quarter_t)
            _, k_stored = yield from project_parts(b, 1, w, C, 1.0, bias_k, hw, rope)
            _, q_stored = yield from project_parts(b, 0, w, 0, 0.25, bias_q, hw, rope)
            if rope:
                finished("L2parts", ve.so_far(b), po.so_far(b))
            own = kind == "window" and b == 1
            while not own and holder[0] not in (None, b):
                yield "wait"
            holder[0] = holder[0] if own else b
            tb = None
            if v_bias is not None:
                tb = sp.dma(ld_tm[b], tmc[b][:, 1, :], v_bias.partition_broadcast(P), tm_free[b])
            v_t, last_v = yield from project_v(b, v_window1 if own else v_slot, w, 2 * C, (h_tok, wl[name + "a"].all()), tb)
            if tb is not None:
                tm_free[b] = (tm_free[b], v_t)
            stored = {"q": q_stored, "k": k_stored, "v": (v_t, stacks_init), "h_free": (last_v,)}
            o = yield from attention(b, name, kind, mask, stored)
            if own:
                load_L1m((pe.so_far(b), v_t))
                loaded.add("L1m")
            else:
                v_slot.free = pe.so_far(b)
                holder[0] = None
            return o

        tm_free = [(), ()]

        def cross_attention(b, name, bias_q, h_tok, kind):
            w = wt[name + "q"]
            hw = (h_tok, wl[name + "a"].all(), quarter_t)
            last_q, q_stored = yield from project_parts(b, 0, w, 0, 0.25, bias_q, hw)
            if name not in ctx_ready:
                prev = {"L2": "L0", "L3": "L2"}.get(name)
                while prev and len(ctx_left.get(prev, ())) < B:
                    yield "wait"
                if name not in ctx_ready:
                    ctx_stage(name)
            ks, vs = ctx_ready[name]
            while cross_holder[0] not in (None, b):
                yield "wait"
            cross_holder[0] = b
            while name not in x_rows:
                yield "wait"
            stored = {"q": q_stored, "k": (ks[b], stacks_init), "v": vs[b], "h_free": (last_q,)}
            o = yield from attention(b, name, kind, False, stored)
            cross_holder[0] = None
            if name == "L0":
                finished("L0x", pe.so_far(b), ve.so_far(b), ac.so_far(b))
            left_context(name, b, pe.so_far(b))
            return o

        def wait_loaded(n):
            while n not in loaded:
                yield "wait"

        def block(b, name, gates, shs, eps, self_bias, cross_bias, v_bias, out_biases, kind, roll, rope, mask, cross_kind,
                  gated_unit):
            def norm(i):
                sh, sc = shs[i]
                if sh is None:
                    return (lambda c: 1.0), (lambda c: 0.0)
                return mod_col(name, sc, b), mod_col(name, sh, b)

            def row_consts(i):
                g, bias = gates[i], out_biases[i]
                t = token_consts(b, (name, g) if g is not None else None, bias, tm_free[b])
                if bias is not None:
                    t = (t, pre_add(b, t, g is not None))
                return t
            yield from wait_loaded(name + "a") if name in ("L2", "L3") else ()
            sc, sh = norm(0)
            h_tok = yield from layer_norm(b, eps, sc, sh, (mod_done[name, 0], h_last[b]), hT[b], roll=roll)
            if mask:
                yield from wait_loaded("mask")
            if name == "L3":
                yield from wait_loaded("L3third")
            o = yield from self_attention(b, name, self_bias[0], self_bias[1], v_bias, rope, mask, h_tok, kind)
            if name == "L2":
                finished("L2self", pe.so_far(b))
            xread[b] = h_tok
            tc = row_consts(0)
            last = yield from out_project(b, wt[name + "so"], o, gates[0] is not None, tc, roll)
            tm_free[b] = tuple(flat((xtok[b], ve.so_far(b), po.so_far(b))))
            sc, sh = norm(1)
            h_tok = yield from layer_norm(b, eps, sc, sh, (mod_done[name, 1], last), hT[b])
            o = yield from cross_attention(b, name, cross_bias, h_tok, cross_kind)
            xread[b] = h_tok
            tc = row_consts(1)
            last = yield from out_project(b, wt[name + "co"], o, gates[1] is not None, tc, False)
            tm_free[b] = tuple(flat((xtok[b], ve.so_far(b), po.so_far(b))))
            finished(name + "a", pe.so_far(b)) if name == "L0" else None
            sc, sh = norm(2)
            h_tok = yield from layer_norm(b, eps, sc, sh, (mod_done[name, 2], last), hT[b])
            yield from wait_loaded(name + "m")
            xread[b] = h_tok
            tc = row_consts(2)
            last = yield from mlp(b, name, (h_tok, wl[name + "m"].all()), gated_unit, tc)
            tm_free[b] = tuple(flat((xtok[b], ve.so_far(b), po.so_far(b))))
            if name == "L0":
                finished("L0m", pe.so_far(b))
            h_last[b] = (last,)

        h_last = [(), ()]
        small_free = [()]

        l1_ready = []

        def l1_context():
            wk, wv = wt["L1k"], wt["L1v"]
            for c in range(CC):
                bank = psum.take()
                t = pe.group([lambda e, k=k, c=c, bank=bank: e.matmul(
                    bank.ap[:, 0:B * LC], wk[:, k, c * P:(c + 1) * P], ctxT[:, k, :, :].rearrange("p b l -> p (b l)"),
                    start=k == 0, stop=k == CC - 1) for k in range(CC)], const_t, wl["L1a"].all(), bank.free, ns=260)
                t = ac.do(lambda e, c=c, bank=bank: e.activation(
                    kT1[:, c, :, :].rearrange("p b l -> p (b l)"), bank.ap[:, 0:B * LC], ACT.Copy), t, ns=180)
                bank.free = t
                l1_ready.append(t)
            for b in range(B):
                bank = psum.take()
                t = pe.group([lambda e, k=k, b=b, bank=bank: e.matmul(
                    bank.ap[0:LC, 0:C], ctxT[:, k, b, :], wv[:, k, :], start=k == 0, stop=k == CC - 1)
                    for k in range(CC)], bank.free, ns=430)
                ctx_reads.append(t)
                t = ac.do(lambda e, b=b, bank=bank: e.activation(v1[b][:, :], bank.ap[0:LC, 0:C], ACT.Copy), t, ns=260)
                bank.free = t
                l1_ready.append(t)

        def softmax_rows(src, n, w, t, scale, dst, scr):
            mx, sm = scr
            t1 = ve.do(lambda e: e.tensor_reduce(mx, src, AX_X, ALU.max), t, small_free[0], ns=230)
            t2 = ve.do(lambda e: e.tensor_tensor(dst, src, mx.unsqueeze(2).to_broadcast([P, n, w]), ALU.subtract), t1,
                       small_free[0], ns=240)
            t3 = ac.do(lambda e: e.activation(dst, dst, ACT.Exp, scale=scale), t2, ns=230)
            t4 = ve.do(lambda e: e.tensor_reduce(sm, dst, AX_X, ALU.add), t3, ns=240)
            t5 = ve.do(lambda e: e.reciprocal(sm, sm), t4, ns=95)
            t6 = ve.do(lambda e: e.tensor_tensor(dst, dst, sm.unsqueeze(2).to_broadcast([P, n, w]), ALU.mult), t5, ns=240)
            return t2, t6

        prow = [sb("p_rows", [P, TPB, E])] * B
        comb = [hT[b][:, :, :].rearrange("p c (h s) -> p (c h) s", h=2) for b in range(B)]

        def layer1(b):
            yield from wait_loaded("L1a")
            yield from wait_loaded("L1m")
            if not l1_ready:
                l1_context()
            sp.dma(ld_tm[b], tmc[b][:, 0, :], a["L1_gate_b2"].partition_broadcast(P), tm_free[b])
            tc = sp.dma(ld_tm[b], tmc[b][:, 1, :], a["L1_out_b"].partition_broadcast(P), tm_free[b])
            cg, cb = COLS["L1_gamma"], COLS["L1_beta"]
            wa, wm = wl["L1a"].all(), wl["L1m"].all()
            cm = comb[b]
            for bl in range(NB):
                h_tok = yield from layer_norm1(b, bl, cm, cg, cb)
                xread[b] = h_tok
                yield from hold_hidden(b)
                qs = lhs_ring.take()
                qts = []
                for c in range(CC):
                    bank = psum.take()
                    t = pe.group([lambda e, k=k, c=c, bank=bank: e.matmul(
                        bank.ap[:, :], wt["L1q"][:, k, c * P:(c + 1) * P], cm[:, k, :], start=k == 0, stop=k == CC - 1)
                        for k in range(CC)], h_tok, wa, bank.free, ns=960)
                    t = ac.do(lambda e, c=c, bank=bank, qs=qs: e.activation(qs.ap[:, c, :], bank.ap[:, :], ACT.Copy), t, qs.free)
                    bank.free = t
                    qts.append(t)
                bank = psum.take()
                t = pe.group([lambda e, i=i, k=k, bank=bank, qs=qs: e.matmul(
                    bank.ap[:, i * LC:(i + 1) * LC], qs.ap[:, k, i * P:(i + 1) * P], kT1[:, k, b, :],
                    start=k == 0, stop=k == CC - 1) for i in range(TPB) for k in range(CC)], qts, l1_ready, bank.free, ns=210)
                qs.free = t
                src = bank.ap[:, 0:TPB * LC].rearrange("p (i n) -> p i n", n=LC)
                wr = act_ring.take()
                wrow = wr.ap[:, 0:TPB * LC].rearrange("p (i n) -> p i n", n=LC)
                rd, t = softmax_rows(src, TPB, LC, (t, wr.free), float(C) ** -0.5, wrow,
                                     (small[b][:, :, 0], small[b][:, :, 1]))
                bank.free = rd
                yield
                bank = psum.take()
                t = pe.group([lambda e, i=i, bank=bank, wrow=wrow: e.transpose(
                    bank.ap[0:LC, i * P:(i + 1) * P], wrow[:, i, :], ident[:, :]) for i in range(TPB)], t, bank.free, ns=210)
                wr.free = t
                wT = act_ring.take()
                t = ac.do(lambda e, bank=bank, wT=wT: e.activation(wT.ap[0:LC, :], bank.ap[0:LC, :], ACT.Copy), t, wT.free)
                bank.free = t
                ev = []
                for c in range(CC):
                    bank = psum.take()
                    t2 = pe.do(lambda e, c=c, bank=bank, wT=wT: e.matmul(
                        bank.ap[:, :], v1[b][:, c * P:(c + 1) * P], wT.ap[0:LC, :], start=True, stop=True), t, bank.free, ns=1710)
                    wT.free = t2
                    t2 = ac.do(lambda e, c=c, bank=bank: e.activation(cm[:, CC + c, :], bank.ap[:, :], ACT.Copy), t2, h_last[b])
                    bank.free = t2
                    ev.append(t2)
                cmt = (h_tok, ev)
                yield
                bank = psum.take()
                t = pe.group([lambda e, k=k, bank=bank: e.matmul(
                    bank.ap[0:E, :], wt["L1r"][:, k, :], cm[:, k, :], start=k == 0, stop=k == 3) for k in range(4)],
                    cmt, bank.free, ns=1360)
                lg = act_ring.take()
                t = ac.do(lambda e, bank=bank, lg=lg: e.activation(lg.ap[0:E, :], bank.ap[0:E, :], ACT.Identity,
                                                                   bias=anchor_r[:, b:b + 1]), t, anchor_done, lg.free)
                bank.free = t
                bank = psum.take()
                t = pe.group([lambda e, i=i, bank=bank, lg=lg: e.transpose(
                    bank.ap[:, i * E:(i + 1) * E], lg.ap[0:E, i * P:(i + 1) * P], ident[0:E, 0:E]) for i in range(TPB)],
                    t, bank.free, ns=40)
                lg.free = t
                src = bank.ap[:, 0:TPB * E].rearrange("p (i n) -> p i n", n=E)
                rd, p_t = softmax_rows(src, TPB, E, t, 1.0, prow[b][:, :, :], (small[b][:, :, 2], small[b][:, :, 3]))
                bank.free = rd
                bank = psum.take()
                t = pe.group([lambda e, i=i, bank=bank: e.transpose(
                    bank.ap[0:E, i * P:(i + 1) * P], prow[b][:, i, :], ident[:, :]) for i in range(TPB)], p_t, bank.free)
                pT = act_ring.take()
                t = ac.do(lambda e, bank=bank, pT=pT: e.activation(pT.ap[0:E, :], bank.ap[0:E, :], ACT.Copy), t, pT.free)
                bank.free = t
                rt = []
                for tp in range(0, TPB, 2):
                    bank = psum.take()
                    t2 = pe.group([lambda e, i=i, tp=tp, bank=bank, pT=pT: e.matmul(
                        bank.ap[:, i * C:(i + 1) * C], pT.ap[0:E, (tp + i) * P:(tp + i + 1) * P], eb2[:, :],
                        start=True, stop=True) for i in range(2)], t, const_t, bank.free, ns=640)
                    t2 = ac.do(lambda e, tp=tp, bank=bank: e.activation(
                        routed[b][:, tp:tp + 2, :], bank.ap[:, :].rearrange("p (t f) -> p t f", t=2), ACT.Copy),
                        t2, small_free[0])
                    pT.free = bank.free = t2
                    rt += [t2, t2]
                yield
                for ex in range(E):
                    accs = [psum.take(), psum.take()]
                    pend = None

                    def down(j, hid, t, ex=ex, accs=accs):
                        t = pe.group([lambda e, i=i, j=j, hid=hid: e.matmul(
                            accs[i // 2].ap[:, (i % 2) * C:(i % 2 + 1) * C], hid.ap[:, i * P:(i + 1) * P],
                            wt[f"L1w2_{ex}"][:, j, :], start=(j == 0 and i % 2 == 0), stop=j == RH // P - 1,
                            skip_group_check=True) for i in range(TPB)], t, wm,
                            accs[0].free if j == 0 else (), accs[1].free if j == 0 else (), ns=430)
                        hid.free = t
                        return t
                    for j in range(RH // P):
                        bank, hid = psum.take(), hid_ring.take()
                        t = pe.group([lambda e, k=k, j=j, ex=ex, bank=bank: e.matmul(
                            bank.ap[:, :], wt[f"L1w1_{ex}"][:, k, j * P:(j + 1) * P], cm[:, k, :],
                            start=k == 0, stop=k == 3) for k in range(4)], cmt, wm, bank.free, ns=840)
                        t = silu(bank, hid, half_anchor[:, ex * (RH // P) + j, b:b + 1], t, anchor_done)
                        if pend is not None:
                            plan.aside("down", down, *pend)
                        pend = (j, hid, t)
                        yield
                    t = plan.aside("down", down, *pend)
                    for i in range(TPB):
                        rt[i] = ve.do(lambda e, i=i, ex=ex, accs=accs: e.scalar_tensor_tensor(
                            out=routed[b][:, i, :], in0=accs[i // 2].ap[:, (i % 2) * C:(i % 2 + 1) * C],
                            scalar=prow[b][:, i, ex:ex + 1], in1=routed[b][:, i, :], op0=ALU.mult, op1=ALU.add),
                            t, rt[i], p_t, ns=400)
                        accs[i // 2].free = rt[i]
                    yield
                gh = lhs_ring.take()
                gts = []
                for c in range(CC):
                    bank = psum.take()
                    t = pe.group([lambda e, k=k, c=c, bank=bank: e.matmul(
                        bank.ap[:, :], wt["L1g1"][:, k, c * P:(c + 1) * P], cm[:, k, :], start=k == 0, stop=k == 3)
                        for k in range(4)], cmt, bank.free, ns=860)
                    h_last[b] = (t,)
                    part = Slot(gh.ap[:, c, :])
                    part.free = gh.free
                    t = silu(bank, part, half_anchor[:, E * RH // P + c, b:b + 1], t)
                    gts.append(t)
                rT = lhs_ring.take()
                rts = []
                for c in range(CC):
                    bank = psum.take()
                    t = pe.group([lambda e, i=i, c=c, bank=bank: e.transpose(
                        bank.ap[:, i * P:(i + 1) * P], routed[b][:, i, c * P:(c + 1) * P], ident[:, :])
                        for i in range(TPB)], rt, bank.free)
                    small_free[0] = (t,)
                    t = ac.do(lambda e, c=c, bank=bank, rT=rT: e.activation(rT.ap[:, c, :], bank.ap[:, :], ACT.Copy), t, rT.free)
                    bank.free = t
                    rts.append(t)
                for tp in range(0, TPB, 2):
                    g_bank = psum.take()
                    tg = pe.group([lambda e, i=i, k=k, tp=tp, bank=g_bank, gh=gh: e.matmul(
                        bank.ap[:, i * C:(i + 1) * C], gh.ap[:, k, (tp + i) * P:(tp + i + 1) * P], wt["L1g2"][:, k, :],
                        start=k == 0, stop=k == CC - 1) for i in range(2) for k in range(CC)], gts, g_bank.free, ns=430)
                    y = y_ring.take()
                    for i in range(2):
                        t1 = ve.do(lambda e, i=i, y=y, bank=g_bank: e.tensor_tensor(
                            y.ap[:, i, :], bank.ap[:, i * C:(i + 1) * C], tmc[b][:, 0, :], ALU.add), tg, tc, y.free)
                    g_bank.free = t1
                    t1 = ac.do(lambda e, y=y: e.activation(y.ap[:, :, :], y.ap[:, :, :], ACT.Tanh, scale=0.5), t1)
                    t1 = ve.do(lambda e, y=y: e.tensor_scalar(y.ap[:, :, :], y.ap[:, :, :], 0.5, 0.5, ALU.mult, ALU.add), t1)
                    o_bank = psum.take()
                    to = pe.group([lambda e, i=i, k=k, tp=tp, bank=o_bank, rT=rT: e.matmul(
                        bank.ap[:, i * C:(i + 1) * C], rT.ap[:, k, (tp + i) * P:(tp + i + 1) * P], wt["L1out"][:, k, :],
                        start=k == 0, stop=k == CC - 1) for i in range(2) for k in range(CC)], rts, o_bank.free, ns=430)
                    r_ = r_ring.take()
                    for i in range(2):
                        t2 = ve.do(lambda e, i=i, r_=r_, bank=o_bank: e.tensor_tensor(
                            r_.ap[:, i * C:(i + 1) * C], bank.ap[:, i * C:(i + 1) * C], tmc[b][:, 1, :], ALU.add),
                            to, tc, r_.free)
                    o_bank.free = t2
                    y2 = y.ap[:, :, :].rearrange("p t f -> p (t f)")
                    t3 = ve.do(lambda e, r_=r_, y2=y2: e.tensor_tensor(y2, r_.ap[:, :], y2, ALU.mult), t1, t2, ns=600)
                    r_.free = t3
                    tile = bl * TPB + tp
                    t4 = po.do(lambda e, tile=tile, y=y: e.tensor_tensor(
                        x[b][:, tile:tile + 2, :], x[b][:, tile:tile + 2, :], y.ap[:, :, :], ALU.add), t3, h_tok)
                    y.free = t4
                    xtok[b][tile] = xtok[b][tile + 1] = (t4,)
                gh.free = tg
                rT.free = to
                small_free[0] = (small_free[0], t, rt, p_t)
                hidden_holder[0] = None
                yield
            tm_free[b] = tuple(flat((t2, t1, ve.so_far(b))))
            finished("L1a", pe.so_far(b))
            finished("L1m", pe.so_far(b))

        def layer_norm1(b, bl, cm, cg, cb):
            return (yield from layer_norm(b, 1e-5, lambda c: cols[:, cg + c:cg + c + 1],
                                          lambda c: cols[:, cb + c:cb + c + 1], (h_last[b],),
                                          Shifted(cm, bl * BLK), blk=bl))

        class Shifted:
            def __init__(self, ap, base):
                self.ap, self.base = ap, base

            def __getitem__(self, key):
                p, c, s = key
                return self.ap[p, c, s.start - self.base:s.stop - self.base]

        def stream(b):
            def q4(i):
                return lambda c: bq[:, i + c:i + c + 1]

            def kcol(name):
                return lambda c: cols[:, COLS[name] + CC + c:COLS[name] + CC + c + 1]

            def zero(c):
                return 0.0
            yield from block(b, "L0", (2 * C, 5 * C, 8 * C), ((0, 2), (6, 8), (12, 14)), 1e-6,
                             (q4(0), kcol("L0_b_qkv")), q4(2), a["L0_b_qkv"][2 * C:3 * C],
                             (a["L0_b_so"], a["L0_b_co"], a["L0_b_m2"]), "window", True, False, False, "topk", True)
            yield from layer1(b)
            yield from block(b, "L2", (2 * C, 5 * C, 8 * C), ((0, 2), (6, 8), (12, 14)), 1e-5,
                             (zero, zero), zero, None, (None, None, a["L2_mlp_b2"]), "full", False, True, True, "context", False)
            yield from block(b, "L3", (2 * C, None, 5 * C), ((0, 2), (None, None), (6, 8)), 1e-6,
                             (q4(4), kcol("L3_b_qkv")), q4(6), a["L3_b_qkv"][2 * C:3 * C],
                             (a["L3_b_proj"], a["L3_b_cproj"], a["L3_b_mlp2"]), "full", False, False, False, "context", False)
            for tp in range(0, NT, 2):
                sp.dma(st_out, out[b].rearrange("(t p) c -> p t c", p=P)[:, tp:tp + 2, :], x[b][:, tp:tp + 2, :],
                       xtok[b][tp:tp + 2])

        streams = {b: stream(b) for b in range(B)}
        streams["anchor"] = anchor_stream()
        reached = {b: 0.0 for b in streams}
        waiting = set()
        while streams:
            able = [s for s in streams if s not in waiting]
            assert able, "all streams wait"
            b = min(able, key=lambda s: (reached[s] - (HOLDER_LEAD if holder[0] == s else 0), str(s)))
            plan.stream, plan.clock = b, reached[b]
            said = next(streams[b], "end")
            if said == "wait":
                waiting.add(b)
                continue
            if said == "end":
                del streams[b]
            reached[b] = plan.clock
            for s in waiting:
                reached[s] = max(reached[s], plan.clock)
            waiting.clear()
        plan.emit()
        sp.wait([l.all() for l in [st_out, st_mod] + st_parts if l.last is not None])


def kernel(**inputs):
    import concourse.bacc as bacc
    from concourse.bass_utils import run_bass_kernel_spmd

    raw = {k: np.asarray(v) for k, v in inputs.items()}

    def column(v):
        return v.reshape(-1, P).T

    names = {"L0": "L0_xcond_", "L1": "L1_xcond_", "L2": "L2_xcond_", "L3": "L3_xcond_"}
    arrays = {}
    for k, v in raw.items():
        for short, long in names.items():
            if k.startswith(long):
                arrays[short + "_" + k[len(long):]] = v
    cols = np.concatenate([column(arrays[n]) for n in (
        "L0_b_qkv", "L0_b_q", "L0_b_kv", "L0_b_m1", "L1_ln_gamma", "L1_ln_beta", "L2_norm1_w", "L2_normc_w",
        "L2_norm2_w", "L2_mlp_b1", "L3_b_qkv", "L3_b_qc", "L3_b_kvc", "L3_b_mlp1")], axis=1)
    cos, sin = rope_tables()
    arrays.update(
        x=raw["x"], ctx=raw["ctx_1024"], ctxT=raw["ctx_1024"].transpose(2, 0, 1), condT=raw["cond_1024"].T,
        mask_self=raw["mask_SxS_bk0"], mask_ctx=raw["mask_BxS2_bf1"],
        cols=cols, cos=cos, sin=sin, ident=np.eye(P, dtype=np.float32))
    for n in ("L0_b_q", "L0_b_m1", "L1_ln_gamma", "L1_ln_beta", "L2_norm1_w", "L2_normc_w", "L2_norm2_w", "L2_mlp_b1",
              "L3_b_qc", "L3_b_mlp1"):
        arrays.pop(n)
    arrays = {k: np.ascontiguousarray(v) for k, v in arrays.items()}

    nc = bacc.Bacc("TRN2", target_bir_lowering=False, num_devices=1, dynamic_dma_scratch_size=1024)
    aps = {k: nc.dram_tensor(f"in_{k}", v.shape, mybir.dt.from_np(v.dtype), kind="ExternalInput").ap()
           for k, v in arrays.items()}
    out = nc.dram_tensor("out_x", (B, S, C), F32, kind="ExternalOutput").ap()
    build_program(nc, aps, out)
    r = run_bass_kernel_spmd(nc, [{f"in_{k}": v for k, v in arrays.items()}], core_ids=[0])
    return r.results[0]["out_x"]
```
